# Optimizing a Trainium2 kernel written in Bass

```python
import numpy as np
import jax
import jax.numpy as jnp

def _softmax(x, axis=-1):
    return jax.nn.softmax(x, axis=axis)

def _gelu(x):
    return jax.nn.gelu(x, approximate=True)

def _silu(x):
    return jax.nn.silu(x)

def _sigmoid(x):
    return jax.nn.sigmoid(x)

def _layernorm(x, axis=-1, eps=1e-05):
    m = jnp.mean(x, axis=axis, keepdims=True)
    v = jnp.var(x, axis=axis, keepdims=True)
    return (x - m) / jnp.sqrt(v + eps)

def _scatter_add(tgt, idx, src, axis=0):
    return tgt.at[idx].add(src)

def _segment_sum(src, seg, n):
    return jax.ops.segment_sum(src, seg, n)
kernel_name = 'mk_gnn_ffn_d1_gnn_r8_26e6ef'

def setup_inputs(seed: int=0):
    np.random.seed(seed)
    _w = jnp.asarray

    def _rec_inputs():
        import jax
        import jax.numpy as jnp
        _gk = jax.random.key(seed)
        x = -0.0006008 + 1.001 * jax.random.normal(jax.random.fold_in(_gk, 1), (6250, 256), jnp.float32)
        src = jax.random.randint(jax.random.fold_in(_gk, 2), (100000,), 0, 6250, jnp.int32)
        dst = jnp.minimum((6250 * jax.random.uniform(jax.random.fold_in(_gk, 3), (100000,)) ** 2.0).astype(jnp.int32), 49999)
        _o = jnp.argsort(dst, stable=True)
        src = src[_o]
        dst = dst[_o]
        edge_attr_256 = 2.93046e-05 + 1.00006 * jax.random.normal(jax.random.fold_in(_gk, 11), (100000, 256), jnp.float32)
        return (x, src, dst, edge_attr_256)
    x, src, dst, edge_attr_256 = _rec_inputs()

    def _L0_gnn_setup():
        import jax, jax.numpy as jnp
        import numpy as np
        N, E, HID, HEADS = (1250, 40000, 256, 8)
        HEAD_DIM = HID // HEADS
        EPS = 1e-05
        key = jax.random.key(seed)
        ks = jax.random.split(key, 12)
        w = lambda k, shape: jax.random.normal(k, shape, dtype=jnp.float32) * 0.02
        return {'x': jax.random.normal(ks[0], (N, HID), dtype=jnp.float32), 'edge_index': jax.random.randint(ks[1], (2, E), 0, N, dtype=jnp.int32), 'edge_attr': jax.random.normal(ks[2], (E, HID), dtype=jnp.float32), 'WQ': w(ks[3], (HID, HID)), 'WK': w(ks[4], (HID, HID)), 'WV': w(ks[5], (HID, HID)), 'WE': w(ks[6], (HID, HID)), 'Wo': w(ks[7], (HID, HID)), 'bo': jnp.zeros((HID,), dtype=jnp.float32), 'gamma': jnp.ones((HID,), dtype=jnp.float32), 'beta': jnp.zeros((HID,), dtype=jnp.float32), 'mean_scale': jnp.ones((HID,), dtype=jnp.float32)}
    _L0_gnn_all = _L0_gnn_setup()
    _L0_gnn_in = {k: v for k, v in _L0_gnn_all.items() if k in ('WQ', 'WK', 'WV', 'WE', 'Wo', 'bo', 'gamma', 'beta', 'mean_scale')}
    del _L0_gnn_all

    def _L0_ffn_setup():
        import jax, jax.numpy as jnp
        import numpy as np
        B, S, H, F, E, K = (8, 512, 256, 512, 16, 2)
        EPS = 1e-05
        key = jax.random.key(seed)
        ks = jax.random.split(key, 9)
        sc = 0.02
        return {'x': jax.random.normal(ks[0], (B, S, H), dtype=jnp.float32), 'gate_w': jax.random.normal(ks[1], (H, E), dtype=jnp.float32) * sc, 'gate_b': jnp.zeros((E,), dtype=jnp.float32), 'w1': jax.random.normal(ks[2], (E, H, F), dtype=jnp.float32) * sc, 'b1': jnp.zeros((E, F), dtype=jnp.float32), 'w2': jax.random.normal(ks[3], (E, F, H), dtype=jnp.float32) * sc, 'b2': jnp.zeros((E, H), dtype=jnp.float32), 'gamma': jnp.ones((H,), dtype=jnp.float32), 'beta': jnp.zeros((H,), dtype=jnp.float32)}
    _L0_ffn_all = _L0_ffn_setup()
    _L0_ffn_in = {k: v for k, v in _L0_ffn_all.items() if k in ('gate_w', 'gate_b', 'w1', 'b1', 'w2', 'b2', 'gamma', 'beta')}
    del _L0_ffn_all
    return {'x': x, 'src': src, 'dst': dst, 'edge_attr_256': edge_attr_256, 'L0_gnn_WQ': _L0_gnn_in['WQ'], 'L0_gnn_WK': _L0_gnn_in['WK'], 'L0_gnn_WV': _L0_gnn_in['WV'], 'L0_gnn_WE': _L0_gnn_in['WE'], 'L0_gnn_Wo': _L0_gnn_in['Wo'], 'L0_gnn_bo': _L0_gnn_in['bo'], 'L0_gnn_gamma': _L0_gnn_in['gamma'], 'L0_gnn_beta': _L0_gnn_in['beta'], 'L0_gnn_mean_scale': _L0_gnn_in['mean_scale'], 'L0_ffn_gate_w': _L0_ffn_in['gate_w'], 'L0_ffn_gate_b': _L0_ffn_in['gate_b'], 'L0_ffn_w1': _L0_ffn_in['w1'], 'L0_ffn_b1': _L0_ffn_in['b1'], 'L0_ffn_w2': _L0_ffn_in['w2'], 'L0_ffn_b2': _L0_ffn_in['b2'], 'L0_ffn_gamma': _L0_ffn_in['gamma'], 'L0_ffn_beta': _L0_ffn_in['beta']}

def reference(x, src, dst, edge_attr_256, L0_gnn_WQ, L0_gnn_WK, L0_gnn_WV, L0_gnn_WE, L0_gnn_Wo, L0_gnn_bo, L0_gnn_gamma, L0_gnn_beta, L0_gnn_mean_scale, L0_ffn_gate_w, L0_ffn_gate_b, L0_ffn_w1, L0_ffn_b1, L0_ffn_w2, L0_ffn_b2, L0_ffn_gamma, L0_ffn_beta):
    import jax
    import jax.numpy as jnp

    def _L0_gnn_ref(x, edge_index, edge_attr, WQ, WK, WV, WE, Wo, bo, gamma, beta, mean_scale):
        import jax, jax.numpy as jnp
        import numpy as np
        N, E, HID, HEADS = (1250, 40000, 256, 8)
        HEAD_DIM = HID // HEADS
        EPS = 1e-05
        n = x.shape[0]
        src, dst = (edge_index[0], edge_index[1])
        q = (x @ WQ.T).reshape(n, HEADS, HEAD_DIM)
        k = (x @ WK.T).reshape(n, HEADS, HEAD_DIM)
        v = (x @ WV.T).reshape(n, HEADS, HEAD_DIM)
        e = (edge_attr @ WE.T).reshape(-1, HEADS, HEAD_DIM)
        q_i = q[dst]
        ke = k[src] + e
        ve = v[src] + e
        score = (q_i * ke).sum(-1) / jnp.sqrt(jnp.float32(HEAD_DIM))
        m = jax.ops.segment_max(score, dst, num_segments=n)
        p = jnp.exp(score - m[dst])
        s = jax.ops.segment_sum(p, dst, num_segments=n)
        alpha = p / s[dst]
        agg = jax.ops.segment_sum(alpha[..., None] * ve, dst, num_segments=n)
        out = agg.reshape(n, HID) @ Wo.T + bo + x
        mu = out.mean(axis=0)
        xc = out - mean_scale * mu
        var = (xc * xc).mean(axis=0)
        out = gamma * xc / jnp.sqrt(var + EPS) + beta
        return jax.nn.gelu(out, approximate=False)

    def _L0_ffn_ref(x, gate_w, gate_b, w1, b1, w2, b2, gamma, beta):
        import jax, jax.numpy as jnp
        import numpy as np
        B, S, H, F, E, K = (8, 512, 256, 512, 16, 2)
        EPS = 1e-05
        gate_logits = x @ gate_w + gate_b
        topk_vals, topk_idx = jax.lax.top_k(gate_logits, K)
        topk_w = jax.nn.softmax(topk_vals, axis=-1)
        h = jax.nn.relu(jnp.einsum('bsh,ehf->bsef', x, w1) + b1)
        expert_out = jnp.einsum('bsef,efh->bseh', h, w2) + b2
        sel = jnp.take_along_axis(expert_out, topk_idx[:, :, :, None], axis=2)
        moe = jnp.sum(topk_w[..., None] * sel, axis=2)
        y = x + moe
        mu = jnp.mean(y, axis=-1, keepdims=True)
        var = jnp.var(y, axis=-1, keepdims=True)
        return (y - mu) / jnp.sqrt(var + EPS) * gamma + beta
    edge_index = jnp.stack([src, dst])
    x = x + _L0_gnn_ref(_layernorm(x, axis=-1), edge_index, edge_attr_256, L0_gnn_WQ, L0_gnn_WK, L0_gnn_WV, L0_gnn_WE, L0_gnn_Wo, L0_gnn_bo, L0_gnn_gamma, L0_gnn_beta, L0_gnn_mean_scale)
    x = x + _L0_ffn_ref(_layernorm(x, axis=-1)[None], L0_ffn_gate_w, L0_ffn_gate_b, L0_ffn_w1, L0_ffn_b1, L0_ffn_w2, L0_ffn_b2, L0_ffn_gamma, L0_ffn_beta)[0]
    return x

_drawn_inputs = setup_inputs


def setup_inputs(seed=0):
    import zlib

    import numpy as np

    out = dict(_drawn_inputs(seed))
    spreads = {'L0_gnn_bo': (0.0, 0.8),
     'L0_gnn_gamma': (1.0, 0.2),
     'L0_gnn_beta': (0.0, 0.1),
     'L0_gnn_mean_scale': (1.0, 0.6),
     'L0_ffn_gate_b': (0.0, 0.297),
     'L0_ffn_b1': (0.0, 0.8),
     'L0_ffn_b2': (0.0, 0.278),
     'L0_ffn_gamma': (1.0, 0.2),
     'L0_ffn_beta': (0.0, 0.1)}
    factors = {'edge_attr_256': 3.826,
     'L0_gnn_WQ': 8.0,
     'L0_gnn_WK': 8.0,
     'L0_gnn_WV': 3.82,
     'L0_gnn_WE': 3.814,
     'L0_gnn_Wo': 2.777}
    for name, (base, spread) in spreads.items():
        noise = np.random.default_rng([zlib.crc32(name.encode()), seed]).standard_normal(out[name].shape)
        drawn = base * np.exp(spread * noise) if base else spread * noise
        out[name] = jnp.asarray(drawn.astype(out[name].dtype))
    for name, factor in factors.items():
        out[name] = (out[name] * factor).astype(out[name].dtype)
    return out
```

```python
import numpy as np
import concourse.bass as bass
from concourse import mybir
from contextlib import ExitStack

N = 6250
E = 100000
D = 256
H = 8
HD = D // H
EXP = 16
F = 512
P = 128
ND = D // P
NF = F // P
NT = -(-N // P)
NP = NT * P
G = 16
NG = -(-E // (P * G))
TE = NG * G
EPAD = TE * P
W = D + 2 * H
RW = W + 1
PART2 = NP
PART3 = PART2 + G * P
ROWS = PART3 + P
NOWHERE = 16384
SLOTS = TE + G + 1
assert 2 * TE <= G * P and 2 * G <= P and ROWS < NOWHERE and G * H == P
EPS = 1e-5
LOW = -1.0e30
CH = 7
NC = NT // CH
TX = (2 * NP + EXP * (P - 1)) // P // 2 * 2 + 2
assert NC * CH == NT and TX * P >= 2 * NP + EXP * (P - 1) and TX <= P

fp32 = mybir.dt.float32
bf16 = mybir.dt.bfloat16
i32 = mybir.dt.int32
ALU = mybir.AluOpType
ACT = mybir.ActivationFunctionType
AX = mybir.AxisListType


def wait(eng, sem, value):
    if isinstance(value, int) and value <= 0:
        return
    eng.wait_ge(sem, value)


def wait_apart(eng, waits, passed, count):
    waits = [(s, v if isinstance(v, int) else eng.to_reg(v)) for s, v in waits if not (isinstance(v, int) and v <= 0)]
    eng.wait_ge(passed, count)
    for s, v in waits:
        eng.wait_ge(s, v)


def rounds(eng, body, first, last):
    g = first
    while g <= last and (g < 3 or g % 2 == 0):
        body(g // 2 if g % 2 == 0 else (g - 1) // 2, 2 * 0 if g % 2 == 0 else 1)
        g += 1
    n = (last - g + 1) // 2
    if n > 0:
        k0 = (g - 1) // 2
        with eng.Fori(k0, k0 + n) as k:
            body(k, 1)
            body(k, 2)
        g += 2 * n
    while g <= last:
        body(g // 2 if g % 2 == 0 else (g - 1) // 2, 0 if g % 2 == 0 else 1)
        g += 1


def build(nc, a, out):
    ctx0 = ExitStack()
    with ctx0:
        def sem(name):
            return ctx0.enter_context(nc.semaphore(name))

        def keep(name, shape, dt):
            return ctx0.enter_context(nc.sbuf_tensor(name, shape, dt))

        kv_tab = nc.dram_tensor("kv_tab", [NP, 2 * D], fp32, kind="Internal").ap()
        q_tab = nc.dram_tensor("q_tab", [NP, D], fp32, kind="Internal").ap()
        xbo_d = nc.dram_tensor("xbo_d", [NP, D], fp32, kind="Internal").ap()
        tab = nc.dram_tensor("tab", [ROWS, W], fp32, kind="Internal").ap()
        xs = nc.dram_tensor("slot_in", [TX * P, D], fp32, kind="Internal").ap()
        ys = nc.dram_tensor("slot_out", [TX * P, D], fp32, kind="Internal").ap()

        ident = keep("ident", [P, P], fp32)
        ones = keep("ones", [P, P], fp32)
        iota_row = keep("iota_row", [P, P], fp32)
        rank = keep("rank", [P, SLOTS], fp32)
        lastf = keep("lastf", [P, SLOTS], fp32)
        target = keep("target", [P, SLOTS], fp32)

        nodes_stage(nc, sem, a, kv_tab, q_tab, xbo_d, tab, xs, ident, ones, iota_row, rank, lastf, target)
        edges_stage(nc, sem, a, kv_tab, q_tab, tab, ident, iota_row, rank, lastf, target)
        merge_stage(nc, sem, a, tab, ident, iota_row, rank, lastf, target)
        O = keep("O", [P, NT, D], fp32)
        XN = keep("XN", [P, NT, D], fp32)
        st = keep("row_stats", [P, NT, 6], fp32)
        mv = keep("row_meanvar", [P, NT, 2], fp32)
        rstd = keep("row_rstd", [P, NT], fp32)
        prob2 = keep("prob2", [P, 2, NT], fp32)
        slots = keep("slots", [P, 2 * NT], i32)
        experts = keep("experts", [P, TX], i32)
        update_stage(nc, sem, a, tab, xbo_d, ident, ones, O, XN, st, mv, rstd)
        route_stage(nc, sem, a, ident, XN, prob2, slots, experts)
        experts_stage(nc, sem, a, xs, ys, ident, XN, slots, experts)
        result_stage(nc, sem, a, ys, out, O, XN, prob2, slots, st, mv)


def nodes_stage(nc, sem, a, kv_tab, q_tab, xbo_d, tab, xs, ident, ones, iota_row, rank, lastf, target):
    with ExitStack() as ctx:
        def sb(name, shape, dt):
            return ctx.enter_context(nc.sbuf_tensor(name, shape, dt))

        def ps(name):
            return ctx.enter_context(nc.psum_tensor(name, [P, 512], fp32))

        wkv = sb("wkv", [P, ND, 2 * D], fp32)
        wq = sb("wq", [P, ND, D], fp32)
        bo = sb("bo", [P, D], fp32)
        neutral = sb("neutral", [P, W], fp32)
        neutral2 = sb("neutral2", [P, W], fp32)
        near = sb("near", [P, 3, SLOTS], i32)
        cur = sb("cur", [P, SLOTS], fp32)
        start = sb("start", [P, SLOTS], bf16)
        slot = sb("slot", [P, SLOTS], fp32)
        sloti = sb("sloti", [P, SLOTS], i32)
        tmp = sb("tmp", [P, SLOTS], fp32)
        iotai = sb("iotai", [P, P], i32)
        tri = sb("tri", [P, P], bf16)
        at127 = sb("at127", [P, 1], fp32)
        xin = sb("xin", [P, 2, D], fp32)
        st = sb("st", [P, 2, 6], fp32)
        mv = sb("mv", [P, 2, 2], fp32)
        rstd = sb("rstd", [P, 2, 1], fp32)
        var = sb("var", [P, 2, 1], fp32)
        std = sb("std", [P, 2, 1], fp32)
        xn = sb("xn", [P, 2, D], fp32)
        xbo = sb("xbo", [P, 2, D], fp32)
        xnT = sb("xnT", [P, 2, ND, P], fp32)
        kv = sb("kv_o", [P, 2, 2 * D], fp32)
        q = sb("q_o", [P, 2, D], fp32)
        psT = [ps("psT0"), ps("psT1")]
        psKV = [ps("psKV0"), ps("psKV1")]
        psQ = [ps("psQ0"), ps("psQ1")]
        psR = [ps("psR0"), ps("psR1")]

        s_w = sem("weights_loaded")
        s_near = sem("near_loaded")
        s_const = sem("constants_made")
        s_pool = sem("pool_chain")
        s_neutral = sem("neutral_made")
        s_fill = sem("table_filled")
        s_start = sem("starts_ready")
        s_rank = sem("ranks_summed")
        s_prep = sem("prep_chain")
        s_x = [sem("x_loaded0"), sem("x_loaded1")]
        s_st = sem("stats_done")
        s_mv = sem("meanvar_done")
        s_rstd = sem("rstd_done")
        s_var = sem("var_done")
        s_std = sem("std_done")
        s_xn = sem("xn_done")
        s_xbo = sem("xbo_done")
        s_xT = sem("xT_done")
        s_xTc = sem("xT_copied")
        s_kv = sem("kv_done")
        s_kvc = sem("kv_copied")
        s_q = sem("q_done")
        s_qc = sem("q_copied")
        s_out = [sem("node_rows_stored0"), sem("node_rows_stored1")]

        x_t = a["x"].rearrange("(t p) f -> t p f", p=P)
        kv_t = kv_tab.rearrange("(t p) f -> t p f", p=P)
        q_t = q_tab.rearrange("(t p) f -> t p f", p=P)
        xbo_t = xbo_d.rearrange("(t p) f -> t p f", p=P)

        with nc.Block() as block:

            @block.sync
            def _(sp):
                sp.dma_start(wkv[:, :, :], a["wkvT"].rearrange("(c p) n -> p c n", p=P)).then_inc(s_w, 16)
                sp.dma_start(wq[:, :, :], a["wqT"].rearrange("(c p) n -> p c n", p=P)).then_inc(s_w, 16)
                sp.dma_start(bo[:, :], a["bo"].partition_broadcast(P)).then_inc(s_w, 16)
                sp.dma_start(near[:, :, :], a["near"]).then_inc(s_near, 16)

                def load(k, c):
                    i, b = 2 * k + c, c % 2
                    wait(sp, s_xn, i - 1)
                    sp.dma_start(xin[:, b, :], x_t[i]).then_inc(s_x[b], 16)

                def store(k, c):
                    i, b = 2 * k + c, c % 2
                    wait(sp, s_kvc, i + 1)
                    sp.dma_start(kv_t[i], kv[:, b, :]).then_inc(s_out[b], 16)
                    wait(sp, s_qc, i + 1)
                    sp.dma_start(q_t[i], q[:, b, :]).then_inc(s_out[b], 16)
                    wait(sp, s_xbo, i + 1)
                    sp.dma_start(xbo_t[i], xbo[:, b, :]).then_inc(s_out[b], 16)

                def period(k, c):
                    load(k, c)
                    if c == 0:
                        store(k - 1, 1) if not isinstance(k, int) or k > 0 else None
                    else:
                        store(k, c - 1)

                load(0, 0)
                rounds(sp, period, 1, NT - 1)
                store((NT - 1) // 2, 0)
                sp.wait_ge(s_neutral, 2)
                nrow = tab[0:NP, :].rearrange("(t p) f -> t p f", p=P)
                prow = tab[NP:ROWS, :].rearrange("(t p) f -> t p f", p=P)
                for t in range(NT):
                    sp.dma_start(nrow[t], neutral[:, :]).then_inc(s_fill, 16)
                for t in range((ROWS - NP) // P):
                    sp.dma_start(prow[t], neutral2[:, :]).then_inc(s_fill, 16)
                srow = xs.rearrange("(t p) f -> t p f", p=P)
                for t in range(TX):
                    sp.dma_start(srow[t], neutral[:, 0:D]).then_inc(s_fill, 16)
                sp.wait_ge(s_fill, 16 * (ROWS // P + TX))
                sp.wait_ge(s_out[0], 48 * ((NT + 1) // 2))
                sp.wait_ge(s_out[1], 48 * (NT // 2))

            @block.gpsimd
            def _(pool):
                pool.memset(ident[:, :], 0.0).then_inc(s_pool, 1)
                pool.memset(ones[:, :], 1.0).then_inc(s_pool, 1)
                pool.iota(iotai[:, :], [[1, P]], base=0, channel_multiplier=0).then_inc(s_pool, 1)
                pool.memset(tri[:, :], 1.0).then_inc(s_pool, 1)
                pool.memset(at127[:, :], 0.0).then_inc(s_pool, 1)
                pool.iota(sloti[:, 0:TE], [[2, TE]], base=PART2, channel_multiplier=0).then_inc(s_pool, 1)
                pool.iota(sloti[:, TE:SLOTS], [[2, G + 1]], base=PART3, channel_multiplier=0).then_inc(s_pool, 1)
                pool.memset(neutral[:, :], 0.0).then_inc(s_neutral, 1)
                pool.memset(neutral2[:, 0:D + H], 0.0).then_inc(s_pool, 1)
                pool.memset(neutral2[:, D + H:W], LOW).then_inc(s_neutral, 1)
                pool.wait_ge(s_pool, 8)
                pool.affine_select(out=ident[:, :], in_=ident[:, :], compare_op=ALU.not_equal, fill=1.0,
                                   base=0, pattern=[[-1, P]], channel_multiplier=1).then_inc(s_const, 1)
                pool.affine_select(out=tri[:, :], in_=tri[:, :], compare_op=ALU.is_ge, fill=0.0,
                                   base=0, pattern=[[1, P]], channel_multiplier=-1).then_inc(s_pool, 1)
                pool.wait_ge(s_pool, 9)
                pool.affine_select(out=tri[:, :], in_=tri[:, :], compare_op=ALU.is_gt, fill=0.0,
                                   base=0, pattern=[[0, P]], channel_multiplier=1).then_inc(s_const, 1)
                pool.affine_select(out=at127[:, :], in_=at127[:, :], compare_op=ALU.not_equal, fill=1.0,
                                   base=-(P - 1), pattern=[[0, 1]], channel_multiplier=1).then_inc(s_const, 1)

            @block.vector
            def _(dve):
                chain = [0]

                def link(ins):
                    chain[0] += 1
                    ins.then_inc(s_prep, 1)
                    dve.wait_ge(s_prep, chain[0])

                dve.wait_ge(s_const, 3)
                dve.wait_ge(s_near, 16)
                link(nc.vector.tensor_copy(iota_row[:, :], iotai[:, :]))
                link(nc.vector.tensor_copy(cur[:, :], near[:, 0, :]))
                link(nc.vector.tensor_copy(slot[:, :], sloti[:, :]))
                nc.vector.tensor_tensor(start[:, :], near[:, 0, :], near[:, 1, :], ALU.not_equal).then_inc(s_start, 1)
                link(nc.vector.tensor_tensor(lastf[:, :], near[:, 0, :], near[:, 2, :], ALU.not_equal))
                link(nc.vector.tensor_scalar(lastf[:, :], lastf[:, :], at127[:, 0:1], None, ALU.max))
                dve.wait_ge(s_rank, 2)
                for h in range(2):
                    lo, hi = h * 512, min(SLOTS, (h + 1) * 512)
                    link(nc.vector.tensor_copy(rank[:, lo:hi], psR[h][:, 0:hi - lo]))
                PT = slice(0, TE + G)
                link(nc.vector.tensor_tensor(tmp[:, PT], slot[:, PT], cur[:, PT], ALU.subtract))
                link(nc.vector.tensor_scalar(tmp[:, PT], tmp[:, PT], 1.0, at127[:, 0:1], ALU.add, ALU.mult))
                link(nc.vector.tensor_tensor(target[:, PT], cur[:, PT], tmp[:, PT], ALU.add))
                link(nc.vector.tensor_tensor(slot[:, PT], slot[:, PT], target[:, PT], ALU.subtract))
                link(nc.vector.tensor_scalar(tmp[:, PT], rank[:, PT], 0.0, None, ALU.is_equal))
                link(nc.vector.tensor_tensor(tmp[:, PT], tmp[:, PT], slot[:, PT], ALU.mult))
                link(nc.vector.tensor_tensor(target[:, PT], target[:, PT], tmp[:, PT], ALU.add))
                link(nc.vector.tensor_copy(target[:, TE + G:SLOTS], cur[:, TE + G:SLOTS]))
                link(nc.vector.tensor_scalar(target[:, :], target[:, :], float(-NOWHERE), None, ALU.add))
                link(nc.vector.tensor_tensor(target[:, :], target[:, :], lastf[:, :], ALU.mult))
                dve.wait_ge(s_w, 48)

                def tile(k, c):
                    i, b = 2 * k + c, c % 2
                    wait(dve, s_x[b], 16 * (k + c // 2 + 1))
                    nc.vector.bn_stats(st[:, b, :], xin[:, b, :]).then_inc(s_st, 1)
                    wait_apart(dve, [(s_st, i + 1)], s_w, 48)
                    nc.vector.bn_aggr(mv[:, b, :], st[:, b, :]).then_inc(s_mv, 1)
                    wait(dve, s_mv, i + 1)
                    nc.vector.tensor_scalar(var[:, b, :], mv[:, b, 1:2], EPS, None, ALU.add).then_inc(s_var, 1)
                    wait(dve, s_std, i + 1)
                    nc.vector.reciprocal(rstd[:, b, :], std[:, b, :]).then_inc(s_rstd, 1)
                    wait(dve, s_rstd, i + 1)
                    wait(dve, s_xT, i - 1)
                    nc.vector.tensor_scalar(xn[:, b, :], xin[:, b, :], mv[:, b, 0:1], rstd[:, b, 0:1],
                                            ALU.subtract, ALU.mult).then_inc(s_xn, 1)
                    wait(dve, s_xn, i + 1)
                    wait(dve, s_out[b], 48 * (k + c // 2))
                    nc.vector.tensor_tensor(xbo[:, b, :], xn[:, b, :], bo[:, :], ALU.add).then_inc(s_xbo, 1)
                    wait(dve, s_q, i + 1)
                    nc.vector.tensor_scalar(q[:, b, :], psQ[b][:, 0:D], float(HD) ** -0.5, None,
                                            ALU.mult).then_inc(s_qc, 1)

                rounds(dve, tile, 0, NT - 1)

            @block.tensor
            def _(pe):
                pe.wait_ge(s_const, 3)
                pe.wait_ge(s_start, 1)
                for h in range(2):
                    lo, hi = h * 512, min(SLOTS, (h + 1) * 512)
                    nc.tensor.matmul(psR[h][:, 0:hi - lo], tri[:, :], start[:, lo:hi], start=True, stop=True).then_inc(s_rank, 1)
                pe.wait_ge(s_w, 48)

                def tile(k, c):
                    i, b = 2 * k + c, c % 2
                    wait(pe, s_xn, i + 1)
                    for f in range(ND):
                        mm = nc.tensor.transpose(psT[b][:, f * P:(f + 1) * P], xn[:, b, f * P:(f + 1) * P], ident[:, :])
                    mm.then_inc(s_xT, 1)
                    wait(pe, s_xTc, i + 1)
                    wait(pe, s_kvc, i - 1)
                    for f in range(ND):
                        mm = nc.tensor.matmul(psKV[b][:, :], xnT[:, b, f, :], wkv[:, f, :], start=f == 0, stop=f == ND - 1)
                    mm.then_inc(s_kv, 1)
                    wait(pe, s_qc, i - 1)
                    for f in range(ND):
                        mm = nc.tensor.matmul(psQ[b][:, 0:D], xnT[:, b, f, :], wq[:, f, :], start=f == 0, stop=f == ND - 1)
                    mm.then_inc(s_q, 1)

                rounds(pe, tile, 0, NT - 1)

            @block.scalar
            def _(act):
                def tile(k, c):
                    i, b = 2 * k + c, c % 2
                    wait(act, s_var, i + 1)
                    nc.scalar.activation(std[:, b, :], var[:, b, :], ACT.Sqrt).then_inc(s_std, 1)
                    wait(act, s_xT, i + 1)
                    wait(act, s_q, i - 1)
                    nc.scalar.copy(xnT[:, b, :, :].rearrange("p c n -> p (c n)"), psT[b][:, 0:D]).then_inc(s_xTc, 1)
                    wait(act, s_kv, i + 1)
                    wait(act, s_out[b], 48 * (k + c // 2))
                    nc.scalar.copy(kv[:, b, :], psKV[b][:, :]).then_inc(s_kvc, 1)

                rounds(act, tile, 0, NT - 1)


def edges_stage(nc, sem, a, kv_tab, q_tab, tab, ident, iota_row, rank, lastf, target):
    with ExitStack() as ctx:
        def sb(name, shape, dt):
            return ctx.enter_context(nc.sbuf_tensor(name, shape, dt))

        def ps(name):
            return ctx.enter_context(nc.psum_tensor(name, [P, 512], fp32))

        we = sb("we", [P, ND, D], fp32)
        AT = sb("attr_in", [P, 2, G, D], fp32)
        KV = sb("kv_in", [P, 2, G, 2 * D], fp32)
        Q = sb("q_in", [P, 2, G, D], fp32)
        idx = sb("idx_in", [P, 2, 2 * G], i32)
        win = sb("win_in", [P, 2, P + 2], i32)
        aT = sb("attrT", [P, 2, D], fp32)
        S = sb("scores", [P, 2, P], fp32)
        mask = sb("mask", [P, P + 1], fp32)
        fwd = sb("max_fwd", [P, P], fp32)
        bwd = sb("max_bwd", [P, P], fp32)
        mT = sb("maxT", [P, P], fp32)
        pT = sb("probT", [P, P], fp32)
        R = sb("rhs", [P, G, RW], fp32)
        OH = sb("onehot", [P, 4, P], fp32)
        ROW = sb("rows_out", [P, 4, W], fp32)
        TGT = sb("targets_out", [P, 4, 1], i32)
        psA = [ps("psA0"), ps("psA1")]
        psE = [ps("psE0"), ps("psE1")]
        psO = [ps("psO0"), ps("psO1")]
        psS, psB = ps("psS"), ps("psB")

        s_we = sem("we_loaded")
        s_attr = [sem("attr_loaded0"), sem("attr_loaded1")]
        s_idx = [sem("idx_loaded0"), sem("idx_loaded1")]
        s_win = [sem("win_loaded0"), sem("win_loaded1")]
        s_gat = [[sem(f"gathered{b}_{j}") for j in range(4)] for b in range(2)]
        s_aT = sem("attr_transposed")
        s_aTc = sem("attrT_copied")
        s_e = sem("e_done")
        s_kve = sem("kve_done")
        s_prod = sem("prod_done")
        s_score = sem("score_done")
        s_ne = sem("change_found")
        s_mask = sem("mask_done")
        s_sT = sem("scores_transposed")
        s_fwd = sem("fwd_max_done")
        s_bwd = sem("bwd_max_done")
        s_mT = sem("max_done")
        s_dT = sem("diff_done")
        s_pT = sem("probs_done")
        s_back = sem("probs_back")
        s_prob = sem("probs_copied")
        s_lm = sem("max_copied")
        s_tc = sem("targets_copied")
        s_oh = sem("onehot_done")
        s_pve = sem("pve_done")
        s_agg = sem("agg_done")
        s_row = sem("row_copied")
        s_tgt = sem("target_copied")
        s_scat = [sem(f"scattered{j}") for j in range(4)]

        attr_g = a["attr"].rearrange("(g t p) f -> g p t f", p=P, t=G)
        win_g = a["win"].rearrange("(g p) w -> g p w", p=P)
        BACKS = {6: (0, 1), 7: (2, 3), 8: (4, 5), 9: (6, 7), 10: (8, 9), 11: (10, 11), 12: (12,), 13: (13,), 14: (14,), 15: (15,)}

        with nc.Block() as block:

            @block.sync
            def _(sp):
                def load_attr(k, c):
                    g, b = 2 * k + c, c % 2
                    wait(sp, s_aT, G * (g - 1))
                    sp.dma_start(AT[:, b, :, :], attr_g[g]).then_inc(s_attr[b], 16)

                def load_idx(k, c):
                    b = c % 2
                    for j in range(4):
                        wait(sp, s_gat[b][j], 128 * (k + c // 2))
                    sp.dma_start(idx[:, b, :], a["idx"][2 * k + c]).then_inc(s_idx[b], 16)

                def load_win(k, c):
                    g, b = 2 * k + c, c % 2
                    wait(sp, s_ne, g - 1)
                    sp.dma_start(win[:, b, :], win_g[g]).then_inc(s_win[b], 16)

                def period(k, c):
                    load_idx(k + 1, c)
                    load_win(k, c)
                    load_attr(k, c + 1)

                sp.dma_start(we[:, :, :], a["weT"].rearrange("(c p) n -> p c n", p=P)).then_inc(s_we, 16)
                load_idx(0, 0)
                load_idx(0, 1)
                load_attr(0, 0)
                rounds(sp, period, 0, NG - 3)
                for g in (NG - 2, NG - 1):
                    load_win(g // 2, g % 2)
                    if g + 1 < NG:
                        load_attr((g + 1) // 2, (g + 1) % 2)

            @block.gpsimd
            def _(pool):
                def gather(k, c, t):
                    b = c % 2
                    ready = [(s_idx[b], 16 * (k + c // 2 + 1))] if t == 0 else []
                    wait_apart(pool, ready + [(s_pve, G * (2 * k + c - 2) + t + 1)], s_idx[b], 16)
                    pool.indirect_dma_start(
                        out=KV[:, b, t, :], out_offset=None, in_=kv_tab,
                        in_offset=bass.IndirectOffsetOnAxis(ap=idx[:, b, t:t + 1], axis=0)).then_inc(s_gat[b][t // 4], 16)
                    pool.indirect_dma_start(
                        out=Q[:, b, t, :], out_offset=None, in_=q_tab,
                        in_offset=bass.IndirectOffsetOnAxis(ap=idx[:, b, G + t:G + t + 1], axis=0)).then_inc(s_gat[b][t // 4], 16)

                def scatter(k, c, t):
                    n = G * (2 * k + c) + t
                    wait_apart(pool, [(s_row, n + 1), (s_tgt, n + 1)], s_idx[0], 16)
                    pool.indirect_dma_start(
                        out=tab, out_offset=bass.IndirectOffsetOnAxis(ap=TGT[:, t % 4, :], axis=0),
                        in_=ROW[:, t % 4, :], in_offset=None,
                        bounds_check=ROWS - 1, oob_is_err=False).then_inc(s_scat[t % 4], 16)

                def period(k, c):
                    for t in range(G):
                        gather(k + 1, c, t)
                        if t:
                            scatter(k, c, t - 1)
                    scatter(k, c, G - 1)

                for g in range(2):
                    for t in range(G):
                        gather(0, g, t)
                rounds(pool, period, 0, NG - 3)
                for g in (NG - 2, NG - 1):
                    for t in range(G):
                        scatter(g // 2, g % 2, t)
                for j in range(4):
                    pool.wait_ge(s_scat[j], 16 * (TE // 4))

            @block.vector
            def _(dve):
                def front(k, c, t):
                    n, b = G * (2 * k + c) + t, c % 2
                    if t % 4 == 0:
                        wait(dve, s_gat[b][t // 4], 128 * (k + c // 2 + 1))
                    wait(dve, s_e, n + 1)
                    e2 = psE[t % 2][:, 0:D].unsqueeze(1).to_broadcast([P, 2, D])
                    kv2 = KV[:, b, t, :].rearrange("p (a f) -> p a f", a=2)
                    nc.vector.tensor_tensor(kv2, kv2, e2, ALU.add).then_inc(s_kve, 1)
                    wait(dve, s_kve, n + 1)
                    nc.vector.tensor_tensor(Q[:, b, t, :], Q[:, b, t, :], KV[:, b, t, 0:D], ALU.mult).then_inc(s_prod, 1)
                    wait(dve, s_prod, n + 1)
                    nc.vector.tensor_reduce(S[:, b, t * H:(t + 1) * H], Q[:, b, t, :].rearrange("p (h d) -> p h d", h=H),
                                            AX.X, ALU.add).then_inc(s_score, 1)

                def masks(k, c):
                    g, b = 2 * k + c, c % 2
                    wait(dve, s_win[b], 16 * (k + c // 2 + 1))
                    nc.vector.tensor_tensor(mask[:, :], win[:, b, 0:P + 1], win[:, b, 1:P + 2], ALU.not_equal).then_inc(s_ne, 1)
                    wait(dve, s_ne, g + 1)
                    nc.vector.tensor_scalar(mask[:, :], mask[:, :], LOW, None, ALU.mult).then_inc(s_mask, 1)

                def maxima(k, c):
                    g = 2 * k + c
                    wait(dve, s_mask, g + 1)
                    wait(dve, s_sT, g + 1)
                    nc.vector.tensor_tensor_scan(fwd[:, :], mask[:, 0:P], psS[:, 0:P], LOW, ALU.add, ALU.max).then_inc(s_fwd, 1)
                    nc.vector.tensor_tensor_scan(bwd[:, ::-1], mask[:, P:0:-1], psS[:, P - 1::-1], LOW,
                                                 ALU.add, ALU.max).then_inc(s_bwd, 1)
                    wait(dve, s_bwd, g + 1)
                    wait(dve, s_fwd, g + 1)
                    nc.vector.tensor_tensor(mT[:, :], fwd[:, :], bwd[:, :], ALU.max).then_inc(s_mT, 1)
                    wait(dve, s_mT, g + 1)
                    nc.vector.tensor_tensor(fwd[:, :], psS[:, 0:P], mT[:, :], ALU.subtract).then_inc(s_dT, 1)

                def small(k, c):
                    g = 2 * k + c
                    cols = bass.ds(G * g, G)
                    wait(dve, s_back, g + 1)
                    wait(dve, s_agg, G * g)
                    nc.vector.tensor_copy(R[:, :, D:D + H], psB[:, 0:P].rearrange("p (t h) -> p t h", h=H)).then_inc(s_prob, 1)
                    nc.vector.tensor_tensor(R[:, :, D + H:W], psB[:, P:2 * P].rearrange("p (t h) -> p t h", h=H),
                                            lastf[:, cols].unsqueeze(2).to_broadcast([P, G, H]), ALU.mult).then_inc(s_lm, 1)
                    nc.vector.tensor_copy(R[:, :, W:RW], target[:, cols].unsqueeze(2)).then_inc(s_tc, 1)

                def back(k, c, t):
                    n, b = G * (2 * k + c) + t, c % 2
                    if t == 0:
                        wait(dve, s_prob, 2 * k + c + 1)
                    wait(dve, s_agg, n - 3)
                    nc.vector.tensor_scalar(OH[:, t % 4, :], iota_row[:, :], rank[:, bass.ds(n, 1)], None,
                                            ALU.is_equal).then_inc(s_oh, 1)
                    nc.vector.tensor_tensor(
                        R[:, t, 0:D].rearrange("p (h d) -> p h d", h=H),
                        KV[:, b, t, D:2 * D].rearrange("p (h d) -> p h d", h=H),
                        R[:, t, D:D + H].unsqueeze(2).to_broadcast([P, H, HD]), ALU.mult).then_inc(s_pve, 1)

                def period(k, c, do_front=True, do_back=True):
                    for t in range(G):
                        if do_back:
                            if t == 3:
                                masks(*prev(k, c))
                                maxima(*prev(k, c))
                            if t == 5:
                                small(*prev(k, c))
                            for j in BACKS.get(t, ()):
                                back(*prev(k, c), j)
                        if do_front:
                            front(k, c, t)

                period(0, 0, True, False)
                rounds(dve, period, 1, NG - 1)
                period(NG // 2, NG % 2, False, True)

            @block.tensor
            def _(pe):
                def front_in(k, c, t):
                    n, b = G * (2 * k + c) + t, c % 2
                    if t == 0:
                        wait(pe, s_attr[b], 16 * (k + c // 2 + 1))
                    wait(pe, s_aTc, n - 1)
                    for f in range(ND):
                        mm = nc.tensor.transpose(psA[t % 2][:, f * P:(f + 1) * P], AT[:, b, t, f * P:(f + 1) * P], ident[:, :])
                    mm.then_inc(s_aT, 1)

                def front_out(k, c, t):
                    n = G * (2 * k + c) + t
                    wait(pe, s_aTc, n + 1)
                    wait(pe, s_kve, n - 1)
                    for f in range(ND):
                        mm = nc.tensor.matmul(psE[t % 2][:, 0:D], aT[:, t % 2, f * P:(f + 1) * P], we[:, f, :],
                                              start=f == 0, stop=f == ND - 1)
                    mm.then_inc(s_e, 1)

                def agg(k, c, t):
                    n = G * (2 * k + c) + t
                    if t == 0:
                        wait(pe, s_lm, 2 * k + c + 1)
                        wait(pe, s_tc, 2 * k + c + 1)
                    wait(pe, s_oh, n + 1)
                    wait(pe, s_pve, n + 1)
                    wait(pe, s_row, n - 1)
                    wait(pe, s_tgt, n - 1)
                    nc.tensor.matmul(psO[t % 2][:, 0:RW], OH[:, t % 4, :], R[:, t, :], start=True, stop=True).then_inc(s_agg, 1)

                def period(k, c, do_front=True, do_back=True):
                    for t in range(G):
                        if do_front:
                            front_in(k, c, t)
                        if do_back:
                            kk, cc = prev(k, c)
                            g = 2 * kk + cc
                            if t == 2:
                                wait(pe, s_score, G * (g + 1))
                                wait(pe, s_dT, g)
                                nc.tensor.transpose(psS[:, 0:P], S[:, cc % 2, :], ident[:, :]).then_inc(s_sT, 1)
                            if t == 5:
                                wait(pe, s_pT, g + 1)
                                wait(pe, s_mT, g + 1)
                                wait(pe, s_lm, g)
                                nc.tensor.transpose(psB[:, 0:P], pT[:, :], ident[:, :])
                                nc.tensor.transpose(psB[:, P:2 * P], mT[:, :], ident[:, :]).then_inc(s_back, 1)
                            for j in BACKS.get(t, ()):
                                agg(kk, cc, j)
                        if do_front:
                            front_out(k, c, t)

                pe.wait_ge(s_we, 16)
                period(0, 0, True, False)
                rounds(pe, period, 1, NG - 1)
                period(NG // 2, NG % 2, False, True)

            @block.scalar
            def _(act):
                def front(k, c, t):
                    n = G * (2 * k + c) + t
                    wait(act, s_aT, n + 1)
                    wait(act, s_e, n - 1)
                    nc.scalar.copy(aT[:, t % 2, :], psA[t % 2][:, 0:D]).then_inc(s_aTc, 1)

                def back(k, c, t):
                    n = G * (2 * k + c) + t
                    wait(act, s_agg, n + 1)
                    wait(act, s_scat[t % 4], 16 * (4 * (2 * k + c) + t // 4))
                    nc.scalar.copy(ROW[:, t % 4, :], psO[t % 2][:, 0:W]).then_inc(s_row, 1)
                    nc.scalar.activation(TGT[:, t % 4, :], psO[t % 2][:, W:RW], ACT.Copy, bias=float(NOWHERE)).then_inc(s_tgt, 1)

                def period(k, c, do_front=True, do_back=True):
                    for t in range(G):
                        if do_front:
                            front(k, c, t)
                        if do_back:
                            kk, cc = prev(k, c)
                            g = 2 * kk + cc
                            if t == 4:
                                wait(act, s_dT, g + 1)
                                wait(act, s_back, g)
                                nc.scalar.activation(pT[:, :], fwd[:, :], ACT.Exp).then_inc(s_pT, 1)
                            for j in BACKS.get(t, ()):
                                back(kk, cc, j)

                period(0, 0, True, False)
                rounds(act, period, 1, NG - 1)
                period(NG // 2, NG % 2, False, True)


def one(i):
    return slice(i, i + 1) if isinstance(i, int) else bass.ds(i, 1)


def span(i):
    return slice(i * D, (i + 1) * D) if isinstance(i, int) else bass.ds(i * D, D)


def prev(k, c):
    return (k, c - 1) if c > 0 else (k - 1, 1)


def merge_stage(nc, sem, a, tab, ident, iota_row, rank, lastf, target):
    with ExitStack() as ctx:
        def sb(name, shape, dt):
            return ctx.enter_context(nc.sbuf_tensor(name, shape, dt))

        def ps(name):
            return ctx.enter_context(nc.psum_tensor(name, [P, 512], fp32))

        IN = sb("merge_in", [P, G, W], fp32)
        win = sb("merge_win", [P, P + 2], i32)
        S = sb("merge_scores", [P, P], fp32)
        mask = sb("merge_mask", [P, P + 1], fp32)
        fwd = sb("merge_fwd", [P, P], fp32)
        bwd = sb("merge_bwd", [P, P], fp32)
        mT = sb("merge_maxT", [P, P], fp32)
        pT = sb("merge_probT", [P, P], fp32)
        PR = sb("merge_prob", [P, G, H], fp32)
        R = sb("merge_rhs", [P, G, RW], fp32)
        OH = sb("merge_onehot", [P, P], fp32)
        ROW = sb("merge_row", [P, W], fp32)
        TGT = sb("merge_target", [P, 1], i32)
        psS, psB, psO = ps("mpsS"), ps("mpsB"), ps("mpsO")

        s_in = sem("merge_loaded")
        s_v = sem("merge_vector")
        s_t = sem("merge_tensor")
        s_a = sem("merge_scalar")
        s_o = sem("merge_scattered")
        LEVELS = [dict(tiles=G, first=PART2, col=TE, v=0, t=0, a=0, o=0)]
        per = 8
        LEVELS.append(dict(tiles=1, first=PART3, col=TE + G, v=per + 2 * G + 2, t=3 + G, a=1 + 2 * G, o=G))
        win_g = a["win"].rearrange("(g p) w -> g p w", p=P)

        with nc.Block() as block:

            @block.sync
            def _(sp):
                for n, lv in enumerate(LEVELS):
                    m = lv["tiles"]
                    sp.wait_ge(s_o, 16 * lv["o"]) if lv["o"] else None
                    sp.dma_start(IN[:, 0:m, :], tab[lv["first"]:lv["first"] + m * P, :].rearrange("(t p) f -> p t f", p=P)).then_inc(s_in, 16)
                    sp.dma_start(win[:, :], win_g[NG + n]).then_inc(s_in, 16)

            @block.vector
            def _(dve):
                done = [0]

                def link(ins):
                    done[0] += 1
                    ins.then_inc(s_v, 1)
                    dve.wait_ge(s_v, done[0])

                for n, lv in enumerate(LEVELS):
                    m = lv["tiles"]
                    q = m * H
                    cols = slice(lv["col"], lv["col"] + m)
                    assert done[0] == lv["v"]
                    dve.wait_ge(s_in, 32 * (n + 1))
                    link(nc.vector.tensor_copy(S[:, 0:q].rearrange("p (t h) -> p t h", h=H), IN[:, 0:m, D + H:W]))
                    link(nc.vector.tensor_tensor(mask[:, :], win[:, 0:P + 1], win[:, 1:P + 2], ALU.not_equal))
                    link(nc.vector.tensor_scalar(mask[:, :], mask[:, :], LOW, None, ALU.mult))
                    dve.wait_ge(s_t, lv["t"] + 1)
                    link(nc.vector.tensor_tensor_scan(fwd[0:q, :], mask[0:q, 0:P], psS[0:q, 0:P], LOW, ALU.add, ALU.max))
                    link(nc.vector.tensor_tensor_scan(bwd[0:q, ::-1], mask[0:q, P:0:-1], psS[0:q, P - 1::-1], LOW, ALU.add, ALU.max))
                    link(nc.vector.tensor_tensor(mT[0:q, :], fwd[0:q, :], bwd[0:q, :], ALU.max))
                    link(nc.vector.tensor_tensor(fwd[0:q, :], psS[0:q, 0:P], mT[0:q, :], ALU.subtract))
                    dve.wait_ge(s_t, lv["t"] + 3)
                    link(nc.vector.tensor_copy(PR[:, 0:m, :], psB[:, 0:q].rearrange("p (t h) -> p t h", h=H)))
                    link(nc.vector.tensor_tensor(R[:, 0:m, D:D + H], PR[:, 0:m, :], IN[:, 0:m, D:D + H], ALU.mult))
                    link(nc.vector.tensor_tensor(R[:, 0:m, D + H:W], psB[:, P:P + q].rearrange("p (t h) -> p t h", h=H),
                                                 lastf[:, cols].unsqueeze(2).to_broadcast([P, m, H]), ALU.mult))
                    link(nc.vector.tensor_copy(R[:, 0:m, W:RW], target[:, cols].unsqueeze(2)))
                    for t in range(m):
                        link(nc.vector.tensor_tensor(
                            R[:, t, 0:D].rearrange("p (h d) -> p h d", h=H), IN[:, t, 0:D].rearrange("p (h d) -> p h d", h=H),
                            PR[:, t, :].unsqueeze(2).to_broadcast([P, H, HD]), ALU.mult))
                        if t:
                            dve.wait_ge(s_t, lv["t"] + 3 + t)
                        link(nc.vector.tensor_scalar(OH[:, :], iota_row[:, :], rank[:, lv["col"] + t:lv["col"] + t + 1], None, ALU.is_equal))
                    if n + 1 < len(LEVELS):
                        LEVELS[n + 1]["v"] = done[0]

            @block.tensor
            def _(pe):
                for n, lv in enumerate(LEVELS):
                    m = lv["tiles"]
                    q = m * H
                    pe.wait_ge(s_v, lv["v"] + 3)
                    nc.tensor.transpose(psS[0:q, 0:P], S[:, 0:q], ident[:, :]).then_inc(s_t, 1)
                    pe.wait_ge(s_a, lv["a"] + 1)
                    nc.tensor.transpose(psB[:, 0:q], pT[0:q, :], ident[0:q, 0:q]).then_inc(s_t, 1)
                    nc.tensor.transpose(psB[:, P:P + q], mT[0:q, :], ident[0:q, 0:q]).then_inc(s_t, 1)
                    for t in range(m):
                        pe.wait_ge(s_v, lv["v"] + 11 + 2 * (t + 1))
                        if t:
                            pe.wait_ge(s_a, lv["a"] + 1 + 2 * t)
                        nc.tensor.matmul(psO[:, 0:RW], OH[:, :], R[:, t, :], start=True, stop=True).then_inc(s_t, 1)

            @block.scalar
            def _(act):
                for n, lv in enumerate(LEVELS):
                    m = lv["tiles"]
                    q = m * H
                    act.wait_ge(s_v, lv["v"] + 7)
                    nc.scalar.activation(pT[0:q, :], fwd[0:q, :], ACT.Exp).then_inc(s_a, 1)
                    for t in range(m):
                        act.wait_ge(s_t, lv["t"] + 3 + t + 1)
                        if lv["o"] + t:
                            act.wait_ge(s_o, 16 * (lv["o"] + t))
                        nc.scalar.copy(ROW[:, :], psO[:, 0:W]).then_inc(s_a, 1)
                        nc.scalar.activation(TGT[:, :], psO[:, W:RW], ACT.Copy, bias=float(NOWHERE)).then_inc(s_a, 1)

            @block.gpsimd
            def _(pool):
                for n, lv in enumerate(LEVELS):
                    for t in range(lv["tiles"]):
                        pool.wait_ge(s_a, lv["a"] + 1 + 2 * (t + 1))
                        pool.indirect_dma_start(
                            out=tab, out_offset=bass.IndirectOffsetOnAxis(ap=TGT[:, :], axis=0),
                            in_=ROW[:, :], in_offset=None, bounds_check=ROWS - 1, oob_is_err=False).then_inc(s_o, 16)
                pool.wait_ge(s_o, 16 * (G + 1))


def update_stage(nc, sem, a, tab, xbo_d, ident, ones, O, XN, st, mv, rstd):
    with ExitStack() as ctx:
        def sb(name, shape, dt):
            return ctx.enter_context(nc.sbuf_tensor(name, shape, dt))

        def ps(name):
            return ctx.enter_context(nc.psum_tensor(name, [P, 512], fp32))

        wo = sb("wo", [P, ND, D], fp32)
        vec = sb("norm_vectors", [P, 3, D], fp32)
        row = sb("row_in", [P, 2, W], fp32)
        xbo = sb("xbo_in", [P, 2, D], fp32)
        zr = sb("inv_sum", [P, 2, H], fp32)
        agg = sb("agg", [P, 2, D], fp32)
        aggT = sb("aggT", [P, 2, D], fp32)
        shift = sb("shift", [P, D], fp32)
        gain = sb("gain", [P, D], fp32)
        var = sb("col_var", [P, D], fp32)
        sq = sb("squares", [P, 2, CH, D], fp32)
        xc = sb("x_chunk", [P, 2, CH, D], fp32)
        eps = sb("var_eps", [P, NT], fp32)
        psT = [ps("upsT0"), ps("upsT1")]
        psY = [ps("upsY0"), ps("upsY1")]
        psM, psV = ps("psM"), ps("psV")

        s_w = sem("update_weights")
        s_in = [sem("rows_loaded0"), sem("rows_loaded1")]
        s_den = sem("sum_guarded")
        s_inv = sem("sum_inverted")
        s_agg = sem("agg_scaled")
        s_aT = sem("agg_transposed")
        s_aTc = sem("aggT_copied")
        s_y = sem("projected")
        s_o = sem("out_rows_done")
        s_mean = sem("mean_summed")
        s_chain = sem("norm_chain")
        s_cent = sem("centred")
        s_sq = sem("squared")
        s_sum = sem("squares_summed")
        s_var = sem("variance_summed")
        s_veps = sem("variance_done")
        s_std = sem("deviation_done")
        s_gain = sem("gain_done")
        s_x = [sem("x_chunk_loaded0"), sem("x_chunk_loaded1")]
        s_pre = sem("pre_gelu_done")
        s_gelu = sem("gelu_done")
        s_x2 = sem("residual_done")
        s_eps2 = sem("row_variance_done")
        s_std2 = sem("row_deviation_done")

        tab_t = tab[0:NP, :].rearrange("(t p) f -> t p f", p=P)
        xbo_t = xbo_d.rearrange("(t p) f -> t p f", p=P)
        x_c = a["x"].rearrange("(c t p) f -> c p t f", p=P, t=CH)
        O2 = O[:, :, :].rearrange("p t f -> p (t f)")
        O_c = O[:, :, :].rearrange("p (c t) f -> p c t f", t=CH)
        XN_c = XN[:, :, :].rearrange("p (c t) f -> p c t f", t=CH)
        REAL = N - (NT - 1) * P

        def across(v):
            return v.unsqueeze(1).to_broadcast([P, CH, D])

        with nc.Block() as block:

            @block.sync
            def _(sp):
                sp.dma_start(wo[:, :, :], a["woT"].rearrange("(c p) n -> p c n", p=P)).then_inc(s_w, 16)
                for j, n in enumerate(("gamma", "beta", "mean_scale")):
                    sp.dma_start(vec[:, j, :], a[n].partition_broadcast(P)).then_inc(s_w, 16)

                def load(k, c):
                    i, b = 2 * k + c, c % 2
                    wait(sp, s_agg, i - 1)
                    sp.dma_start(row[:, b, :], tab_t[i]).then_inc(s_in[b], 16)
                    wait(sp, s_o, i - 1)
                    sp.dma_start(xbo[:, b, :], xbo_t[i]).then_inc(s_in[b], 16)

                rounds(sp, load, 0, NT - 1)
                for c in range(NC):
                    if c >= 2:
                        sp.wait_ge(s_x2, c - 1)
                    sp.dma_start(xc[:, c % 2, :, :], x_c[c]).then_inc(s_x[c % 2], 16)

            @block.vector
            def _(dve):
                def tile(k, c):
                    i, b = 2 * k + c, c % 2
                    wait(dve, s_in[b], 32 * (k + c // 2 + 1))
                    nc.vector.tensor_scalar(zr[:, b, :], row[:, b, D:D + H], 1e-30, None, ALU.max).then_inc(s_den, 1)
                    wait(dve, s_den, i + 1)
                    nc.vector.reciprocal(zr[:, b, :], zr[:, b, :]).then_inc(s_inv, 1)
                    wait(dve, s_inv, i + 1)
                    wait(dve, s_aT, i - 1)
                    nc.vector.tensor_tensor(
                        agg[:, b, :].rearrange("p (h d) -> p h d", h=H), row[:, b, 0:D].rearrange("p (h d) -> p h d", h=H),
                        zr[:, b, :].unsqueeze(2).to_broadcast([P, H, HD]), ALU.mult).then_inc(s_agg, 1)

                def finish(k, c):
                    i, b = 2 * k + c, c % 2
                    wait(dve, s_y, i + 1)
                    nc.vector.tensor_tensor(O2[:, span(i)], psY[b][:, 0:D], xbo[:, b, :], ALU.add).then_inc(s_o, 1)

                def period(k, c):
                    tile(k, c)
                    finish(*prev(k, c))

                tile(0, 0)
                rounds(dve, period, 1, NT - 1)
                finish((NT - 1) // 2, 0)

                chain = [0]

                def link(ins):
                    chain[0] += 1
                    ins.then_inc(s_chain, 1)
                    dve.wait_ge(s_chain, chain[0])

                dve.wait_ge(s_w, 64)
                dve.wait_ge(s_mean, 1)
                link(nc.vector.tensor_scalar(shift[:, :], psM[:, 0:D], 1.0 / N, None, ALU.mult))
                link(nc.vector.tensor_tensor(shift[:, :], shift[:, :], vec[:, 2, :], ALU.mult))
                for c in range(NC):
                    nc.vector.tensor_tensor(O_c[:, c], O_c[:, c], across(shift[:, :]), ALU.subtract).then_inc(s_cent, 1)
                dve.wait_ge(s_var, 1)
                nc.vector.tensor_scalar(var[:, :], psV[:, 0:D], 1.0 / N, EPS, ALU.mult, ALU.add).then_inc(s_veps, 1)
                dve.wait_ge(s_std, 1)
                link(nc.vector.reciprocal(gain[:, :], var[:, :]))
                link(nc.vector.tensor_tensor(gain[:, :], gain[:, :], vec[:, 0, :], ALU.mult))

                def pre_gelu(c):
                    dve.wait_ge(s_cent, NC)
                    link(nc.vector.tensor_tensor(O_c[:, c], O_c[:, c], across(gain[:, :]), ALU.mult))
                    if c >= 2:
                        dve.wait_ge(s_gelu, c - 1)
                    nc.vector.tensor_tensor(sq[:, c % 2, :, :], O_c[:, c], across(vec[:, 1, :]), ALU.add).then_inc(s_pre, 1)

                def residual(c):
                    dve.wait_ge(s_gelu, c + 1)
                    dve.wait_ge(s_x[c % 2], 16 * (c // 2 + 1))
                    nc.vector.tensor_tensor(O_c[:, c], XN_c[:, c], xc[:, c % 2, :, :], ALU.add).then_inc(s_x2, 1)

                def stats(c):
                    dve.wait_ge(s_x2, c + 1)
                    for t in range(CH * c, CH * (c + 1)):
                        last = nc.vector.bn_stats(st[:, t, :], O[:, t, :])
                    link(last)
                    for t in range(CH * c, CH * (c + 1)):
                        last = nc.vector.bn_aggr(mv[:, t, :], st[:, t, :])
                    link(last)

                pre_gelu(0)
                for c in range(NC):
                    if c + 1 < NC:
                        pre_gelu(c + 1)
                    residual(c)
                    stats(c)
                nc.vector.tensor_scalar(eps[:, :], mv[:, :, 1], EPS, None, ALU.add).then_inc(s_eps2, 1)
                dve.wait_ge(s_std2, 1)
                link(nc.vector.reciprocal(rstd[:, :], eps[:, :]))
                for t in range(NT):
                    last = nc.vector.tensor_scalar(XN[:, t, :], O[:, t, :], mv[:, t, 0:1], rstd[:, t:t + 1], ALU.subtract, ALU.mult)
                link(last)

            @block.tensor
            def _(pe):
                pe.wait_ge(s_w, 64)

                def product(k, c):
                    i, b = 2 * k + c, c % 2
                    wait(pe, s_agg, i + 1)
                    wait(pe, s_aTc, i - 1)
                    for f in range(ND):
                        mm = nc.tensor.transpose(psT[b][:, f * P:(f + 1) * P], agg[:, b, f * P:(f + 1) * P], ident[:, :])
                    mm.then_inc(s_aT, 1)
                    wait(pe, s_aTc, i + 1)
                    wait(pe, s_o, i - 1)
                    for f in range(ND):
                        mm = nc.tensor.matmul(psY[b][:, 0:D], aggT[:, b, f * P:(f + 1) * P], wo[:, f, :], start=f == 0, stop=f == ND - 1)
                    mm.then_inc(s_y, 1)

                def mean(k, c, rows=P):
                    i = 2 * k + c
                    wait(pe, s_o, i + 1)
                    first, last = isinstance(i, int) and i == 0, isinstance(i, int) and i == NT - 1
                    mm = nc.tensor.matmul(psM[:, 0:D], ones[0:rows, :], O2[0:rows, span(i)], start=first, stop=last)
                    if last:
                        mm.then_inc(s_mean, 1)

                def period(k, c):
                    product(k, c)
                    mean(*prev(k, c))

                product(0, 0)
                rounds(pe, period, 1, NT - 1)
                mean((NT - 1) // 2, 0, REAL)
                for c in range(NC):
                    pe.wait_ge(s_sq, c + 1)
                    for t in range(CH):
                        rows = REAL if c * CH + t == NT - 1 else P
                        mm = nc.tensor.matmul(psV[:, 0:D], ones[0:rows, :], sq[0:rows, c % 2, t, :],
                                              start=c + t == 0, stop=rows == REAL)
                    mm.then_inc(s_sum, 1)
                pe.wait_ge(s_sum, NC)
                pe.nop().then_inc(s_var, 1)

            @block.scalar
            def _(act):
                def tile(k, c):
                    i, b = 2 * k + c, c % 2
                    wait(act, s_aT, i + 1)
                    wait(act, s_y, i - 1)
                    nc.scalar.copy(aggT[:, b, :], psT[b][:, 0:D]).then_inc(s_aTc, 1)

                rounds(act, tile, 0, NT - 1)
                for c in range(NC):
                    act.wait_ge(s_cent, c + 1)
                    if c >= 2:
                        act.wait_ge(s_sum, c - 1)
                    nc.scalar.activation(sq[:, c % 2, :, :], O_c[:, c], ACT.Square).then_inc(s_sq, 1)
                act.wait_ge(s_veps, 1)
                nc.scalar.activation(var[:, :], var[:, :], ACT.Sqrt).then_inc(s_std, 1)
                for c in range(NC):
                    act.wait_ge(s_pre, c + 1)
                    nc.scalar.activation(XN_c[:, c], sq[:, c % 2, :, :], ACT.Gelu).then_inc(s_gelu, 1)
                act.wait_ge(s_eps2, 1)
                nc.scalar.activation(eps[:, :], eps[:, :], ACT.Sqrt).then_inc(s_std2, 1)


def route_stage(nc, sem, a, ident, XN, prob2, slots, experts):
    J = 2 * NT
    with ExitStack() as ctx:
        def sb(name, shape, dt):
            return ctx.enter_context(nc.sbuf_tensor(name, shape, dt))

        def ps(name):
            return ctx.enter_context(nc.psum_tensor(name, [P, 512], fp32))

        wg = sb("gate_w", [P, ND, EXP], fp32)
        bg = sb("gate_b", [P, EXP], fp32)
        xT = sb("gate_xT", [P, 2, D], fp32)
        L = sb("logits", [P, NT, EXP], fp32)
        top = sb("top", [P, 2, NT], fp32)
        pick = sb("pick", [P, NT], fp32)
        eq = sb("equal", [P, NT, EXP], fp32)
        numi = sb("numbers_i", [P, P], i32)
        num = sb("numbers", [P, P], fp32)
        below = sb("expert_below", [P, EXP], fp32)
        pairs = sb("pairs", [P, EXP, J], fp32)
        pairs16 = sb("pairs16", [P, EXP, J], bf16)
        tri = sb("strict_tri", [P, P], bf16)
        all1 = sb("all_ones", [P, P], bf16)
        keepst = sb("keep_state", [P, EXP, J], fp32)
        total = sb("total", [P, EXP, J], fp32)
        upto = sb("upto", [P, EXP, J], fp32)
        place = sb("place", [P, EXP, J], fp32)
        ntile = sb("expert_tiles", [P, EXP], fp32)
        endt = sb("expert_end", [P, EXP], fp32)
        one16 = sb("one16", [P, EXP], fp32)
        mult = sb("multiples", [P, NT], fp32)
        over = sb("count_over", [P, EXP, NT], fp32)
        ended = sb("expert_ended", [P, TX, EXP], fp32)
        slotf = sb("slot_f", [P, J], fp32)
        eidf = sb("expert_f", [P, TX], fp32)
        psT = [ps("rpsT0"), ps("rpsT1")]
        psL = [ps("psL0"), ps("psL1")]
        psW = [ps(f"psW{j}") for j in range(4)]
        QB = EXP // 4

        s_w = sem("gate_loaded")
        s_c = sem("route_constants")
        s_cc = sem("route_const_chain")
        s_xT = sem("gate_transposed")
        s_xTc = sem("gate_xT_copied")
        s_l = sem("logits_done")
        s_lc = sem("logits_copied")
        s_v = sem("route_chain")
        s_d = sem("top_difference")
        s_e = sem("second_exp")
        s_p = sem("pairs_ready")
        s_in = sem("within_summed")
        s_inc = sem("within_copied")
        s_tot = sem("totals_summed")

        with nc.Block() as block:

            @block.sync
            def _(sp):
                sp.dma_start(wg[:, :, :], a["gate_w"].rearrange("(c p) n -> p c n", p=P)).then_inc(s_w, 16)
                sp.dma_start(bg[:, :], a["gate_b"].partition_broadcast(P)).then_inc(s_w, 16)

            @block.gpsimd
            def _(pool):
                pool.iota(numi[:, :], [[1, P]], base=0, channel_multiplier=0).then_inc(s_cc, 1)
                pool.memset(tri[:, :], 1.0).then_inc(s_cc, 1)
                pool.memset(all1[:, :], 1.0).then_inc(s_cc, 1)
                pool.memset(keepst[:, :, :], 1.0).then_inc(s_cc, 1)
                pool.memset(one16[:, :], 1.0).then_inc(s_cc, 1)
                pool.wait_ge(s_cc, 5)
                pool.affine_select(out=tri[:, :], in_=tri[:, :], compare_op=ALU.is_gt, fill=0.0,
                                   base=0, pattern=[[1, P]], channel_multiplier=-1).then_inc(s_c, 1)
                pool.memset(keepst[:, :, 0:1], 0.0).then_inc(s_c, 1)

            @block.tensor
            def _(pe):
                pe.wait_ge(s_w, 32)

                def tile(i):
                    b = i % 2
                    wait(pe, s_xTc, i - 1)
                    for f in range(ND):
                        mm = nc.tensor.transpose(psT[b][:, f * P:(f + 1) * P], XN[:, i, f * P:(f + 1) * P], ident[:, :])
                    mm.then_inc(s_xT, 1)
                    wait(pe, s_xTc, i + 1)
                    wait(pe, s_lc, i - 1)
                    for f in range(ND):
                        mm = nc.tensor.matmul(psL[b][:, 0:EXP], xT[:, b, f * P:(f + 1) * P], wg[:, f, :], start=f == 0, stop=f == ND - 1)
                    mm.then_inc(s_l, 1)

                for i in range(NT):
                    tile(i)
                pe.wait_ge(s_c, 2)
                pe.wait_ge(s_p, 1)
                for j in range(4):
                    mm = nc.tensor.matmul(psW[j][:, 0:QB * J], tri[:, :], pairs16[:, QB * j:QB * (j + 1), :].rearrange("p e j -> p (e j)"), start=True, stop=True)
                mm.then_inc(s_in, 1)
                pe.wait_ge(s_inc, 1)
                for j in range(4):
                    mm = nc.tensor.matmul(psW[j][:, 0:QB * J], all1[:, :], pairs16[:, QB * j:QB * (j + 1), :].rearrange("p e j -> p (e j)"), start=True, stop=True)
                mm.then_inc(s_tot, 1)

            @block.scalar
            def _(act):
                for i in range(NT):
                    b = i % 2
                    act.wait_ge(s_xT, i + 1)
                    wait(act, s_l, i - 1)
                    nc.scalar.copy(xT[:, b, :], psT[b][:, 0:D]).then_inc(s_xTc, 1)
                act.wait_ge(s_d, 1)
                nc.scalar.activation(prob2[:, 1, :], top[:, 1, :], ACT.Exp).then_inc(s_e, 1)

            @block.vector
            def _(dve):
                chain = [0]

                def link(ins):
                    chain[0] += 1
                    ins.then_inc(s_v, 1)
                    dve.wait_ge(s_v, chain[0])

                V = nc.vector
                dve.wait_ge(s_c, 2)
                link(V.tensor_copy(num[:, :], numi[:, :]))
                link(V.tensor_scalar(below[:, :], num[:, 0:EXP], float(-EXP), None, ALU.add))
                dve.wait_ge(s_w, 32)
                for i in range(NT):
                    dve.wait_ge(s_l, i + 1)
                    last = V.tensor_tensor(L[:, i, :], psL[i % 2][:, 0:EXP], bg[:, :], ALU.add)
                    last.then_inc(s_lc, 1)
                dve.wait_ge(s_lc, NT)
                by_expert = [P, NT, EXP]
                for k in range(2):
                    oh = pairs[:, :, k * NT:(k + 1) * NT].rearrange("p e t -> p t e")
                    link(V.tensor_reduce(top[:, k, :], L[:, :, :], AX.X, ALU.max))
                    link(V.tensor_tensor(eq[:, :, :], L[:, :, :], top[:, k, :].unsqueeze(2).to_broadcast(by_expert), ALU.is_equal))
                    link(V.tensor_tensor(eq[:, :, :], eq[:, :, :], below[:, :].unsqueeze(1).to_broadcast(by_expert), ALU.mult))
                    link(V.tensor_reduce(pick[:, :], eq[:, :, :], AX.X, ALU.min))
                    link(V.tensor_tensor(oh, below[:, :].unsqueeze(1).to_broadcast(by_expert), pick[:, :].unsqueeze(2).to_broadcast(by_expert), ALU.is_equal))
                    if k == 0:
                        link(V.tensor_scalar(eq[:, :, :], oh, LOW, None, ALU.mult))
                        link(V.tensor_tensor(L[:, :, :], L[:, :, :], eq[:, :, :], ALU.add))
                V.tensor_copy(pairs16[:, :, :], pairs[:, :, :]).then_inc(s_p, 1)
                V.tensor_tensor(top[:, 1, :], top[:, 1, :], top[:, 0, :], ALU.subtract).then_inc(s_d, 1)
                dve.wait_ge(s_e, 1)
                link(V.tensor_scalar(pick[:, :], prob2[:, 1, :], 1.0, None, ALU.add))
                link(V.reciprocal(prob2[:, 0, :], pick[:, :]))
                link(V.tensor_tensor(prob2[:, 1, :], prob2[:, 1, :], prob2[:, 0, :], ALU.mult))
                dve.wait_ge(s_in, 1)
                for j in range(4):
                    last = V.tensor_copy(place[:, QB * j:QB * (j + 1), :].rearrange("p e j -> p (e j)"), psW[j][:, 0:QB * J])
                last.then_inc(s_inc, 1)
                dve.wait_ge(s_tot, 1)
                for j in range(4):
                    last = V.tensor_copy(total[:, QB * j:QB * (j + 1), :].rearrange("p e j -> p (e j)"), psW[j][:, 0:QB * J])
                link(last)
                flat = lambda v: v[:, :, :].rearrange("p e j -> p (e j)")
                link(V.tensor_tensor_scan(flat(upto), flat(keepst), flat(total), 0.0, ALU.mult, ALU.add))
                link(V.tensor_tensor(place[:, :, :], place[:, :, :], upto[:, :, :], ALU.add))
                link(V.tensor_tensor(place[:, :, :], place[:, :, :], total[:, :, :], ALU.subtract))
                link(V.tensor_scalar(mult[:, :], num[:, 0:NT], float(P), None, ALU.mult))
                link(V.tensor_tensor(over[:, :, :], upto[:, :, J - 1:J].to_broadcast([P, EXP, NT]),
                                     mult[:, :].unsqueeze(1).to_broadcast([P, EXP, NT]), ALU.is_gt))
                link(V.tensor_reduce(ntile[:, :], over[:, :, :], AX.X, ALU.add))
                link(V.tensor_tensor_scan(endt[:, :], one16[:, :], ntile[:, :], 0.0, ALU.mult, ALU.add))
                link(V.tensor_tensor(ntile[:, :], endt[:, :], ntile[:, :], ALU.subtract))
                link(V.tensor_scalar(ntile[:, :], ntile[:, :], float(P), None, ALU.mult))
                link(V.tensor_tensor(place[:, :, :], place[:, :, :], ntile[:, :].unsqueeze(2).to_broadcast([P, EXP, J]), ALU.add))
                link(V.tensor_tensor(place[:, :, :], place[:, :, :], pairs[:, :, :], ALU.mult))
                link(V.tensor_reduce(slotf[:, :], place[:, :, :].rearrange("p e j -> p j e"), AX.X, ALU.add))
                link(V.tensor_copy(slots[:, :], slotf[:, :]))
                link(V.tensor_tensor(ended[:, :, :], num[:, 0:TX].unsqueeze(2).to_broadcast([P, TX, EXP]),
                                     endt[:, :].unsqueeze(1).to_broadcast([P, TX, EXP]), ALU.is_ge))
                link(V.tensor_reduce(eidf[:, :], ended[:, :, :], AX.X, ALU.add))
                link(V.tensor_scalar(experts[:, :], eidf[:, :], float(EXP - 1), None, ALU.min))


def experts_stage(nc, sem, a, xs, ys, ident, XN, slots, experts):
    with ExitStack() as ctx:
        def sb(name, shape, dt):
            return ctx.enter_context(nc.sbuf_tensor(name, shape, dt))

        def ps(name):
            return ctx.enter_context(nc.psum_tensor(name, [P, 512], fp32))

        w1 = sb("w1", [P, 2, ND, F], fp32)
        w2 = sb("w2", [P, 2, NF, D], fp32)
        b1 = sb("b1", [P, 2, NF], fp32)
        b2 = sb("b2", [P, 2, D], fp32)
        xin = sb("slot_x", [P, 2, D], fp32)
        xT = sb("slot_xT", [P, 2, D], fp32)
        hT = sb("hidden", [P, 2, F], fp32)
        y = sb("slot_y", [P, 2, D], fp32)
        psT = [ps("epsT0"), ps("epsT1")]
        psH = [ps("epsH0"), ps("epsH1")]
        psY = [ps("epsY0"), ps("epsY1")]

        s_sc = sem("slots_written")
        s_ld = [sem("expert_loaded0"), sem("expert_loaded1")]
        s_xT = sem("slot_transposed")
        s_xTc = sem("slot_xT_copied")
        s_h = sem("hidden_summed")
        s_hc = sem("hidden_done")
        s_hv = sem("hidden_done_v")
        s_y = sem("slot_y_summed")
        s_yc = sem("slot_y_done")
        s_st = [sem("slot_y_stored0"), sem("slot_y_stored1")]

        xs_t = xs.rearrange("(t p) f -> t p f", p=P)
        ys_t = ys.rearrange("(t p) f -> t p f", p=P)
        w1_e = a["w1"].rearrange("e (c p) n -> e p c n", p=P)
        w2_e = a["w2"].rearrange("e (c p) n -> e p c n", p=P)

        with nc.Block() as block:

            @block.gpsimd
            def _(pool):
                for j in range(2 * NT):
                    pool.indirect_dma_start(
                        out=xs, out_offset=bass.IndirectOffsetOnAxis(ap=slots[:, j:j + 1], axis=0),
                        in_=XN[:, j % NT, :], in_offset=None, bounds_check=TX * P - 1, oob_is_err=False).then_inc(s_sc, 16)

            @block.sync
            def _(sp):
                sp.wait_ge(s_sc, 16 * 2 * NT)

                def load(k, c):
                    i, b = 2 * k + c, c % 2
                    e = sp.value_load(experts[0:1, one(i)], min_val=0, max_val=EXP - 1)
                    wait(sp, s_xT, i - 1)
                    sp.dma_start(xin[:, b, :], xs_t[i]).then_inc(s_ld[b], 16)
                    wait(sp, s_h, i - 1)
                    sp.dma_start(w1[:, b, :, :], w1_e[e]).then_inc(s_ld[b], 16)
                    wait(sp, s_y, i - 1)
                    sp.dma_start(w2[:, b, :, :], w2_e[e]).then_inc(s_ld[b], 16)
                    wait(sp, s_hc, i - 1)
                    wait(sp, s_hv, i - 1)
                    sp.dma_start(b1[:, b, :], a["b1"][e]).then_inc(s_ld[b], 16)
                    wait(sp, s_yc, i - 1)
                    sp.dma_start(b2[:, b, :], a["b2"][e].partition_broadcast(P)).then_inc(s_ld[b], 16)

                rounds(sp, load, 0, TX - 1)

            @block.tensor
            def _(pe):
                def tile(k, c):
                    i, b = 2 * k + c, c % 2
                    wait(pe, s_ld[b], 80 * (k + c // 2 + 1))
                    wait(pe, s_xTc, i - 1)
                    for f in range(ND):
                        mm = nc.tensor.transpose(psT[b][:, f * P:(f + 1) * P], xin[:, b, f * P:(f + 1) * P], ident[:, :])
                    mm.then_inc(s_xT, 1)
                    wait(pe, s_xTc, i + 1)
                    wait(pe, s_hc, i - 1)
                    wait(pe, s_hv, i - 1)
                    for f in range(NF):
                        for d in range(ND):
                            mm = nc.tensor.matmul(psH[b][:, f * P:(f + 1) * P], w1[:, b, d, f * P:(f + 1) * P],
                                                  xT[:, b, d * P:(d + 1) * P], start=d == 0, stop=d == ND - 1)
                    mm.then_inc(s_h, 1)

                def second(k, c):
                    i, b = 2 * k + c, c % 2
                    wait(pe, s_hc, i + 1)
                    wait(pe, s_hv, i + 1)
                    wait(pe, s_yc, i - 1)
                    for f in range(NF):
                        mm = nc.tensor.matmul(psY[b][:, 0:D], hT[:, b, f * P:(f + 1) * P], w2[:, b, f, :], start=f == 0, stop=f == NF - 1)
                    mm.then_inc(s_y, 1)

                def period(k, c):
                    tile(k, c)
                    second(*prev(k, c))

                tile(0, 0)
                rounds(pe, period, 1, TX - 1)
                second((TX - 1) // 2, (TX - 1) % 2)

            @block.scalar
            def _(act):
                def tile(k, c):
                    i, b = 2 * k + c, c % 2
                    wait(act, s_xT, i + 1)
                    wait(act, s_h, i - 1)
                    nc.scalar.copy(xT[:, b, :], psT[b][:, 0:D]).then_inc(s_xTc, 1)
                    wait(act, s_h, i + 1)
                    wait(act, s_y, i - 1)
                    for f in range(NF // 2):
                        last = nc.scalar.activation(hT[:, b, f * P:(f + 1) * P], psH[b][:, f * P:(f + 1) * P], ACT.Relu, bias=b1[:, b, f:f + 1])
                    last.then_inc(s_hc, 1)

                def store(k, c):
                    i, b = 2 * k + c, c % 2
                    wait(act, s_yc, i + 1)
                    act.dma_start(ys_t[i], y[:, b, :]).then_inc(s_st[b], 16)

                def period(k, c):
                    tile(k, c)
                    store(*prev(k, c))

                tile(0, 0)
                rounds(act, period, 1, TX - 1)
                store((TX - 1) // 2, (TX - 1) % 2)
                for b in range(2):
                    act.wait_ge(s_st[b], 16 * (TX // 2))

            @block.vector
            def _(dve):
                def tile(k, c):
                    i, b = 2 * k + c, c % 2
                    wait(dve, s_hc, i + 1)
                    wait(dve, s_y, i - 1)
                    for f in range(NF // 2, NF):
                        last = nc.vector.tensor_scalar(hT[:, b, f * P:(f + 1) * P], psH[b][:, f * P:(f + 1) * P], b1[:, b, f:f + 1], 0.0, ALU.add, ALU.max)
                    last.then_inc(s_hv, 1)

                def out_rows(k, c):
                    i, b = 2 * k + c, c % 2
                    wait(dve, s_y, i + 1)
                    wait(dve, s_st[b], 16 * (k + c // 2))
                    nc.vector.tensor_tensor(y[:, b, :], psY[b][:, 0:D], b2[:, b, :], ALU.add).then_inc(s_yc, 1)

                def period(k, c):
                    tile(k, c)
                    out_rows(*prev(k, c))

                tile(0, 0)
                rounds(dve, period, 1, TX - 1)
                out_rows((TX - 1) // 2, (TX - 1) % 2)


def result_stage(nc, sem, a, ys, out, O, XN, prob2, slots, st, mv):
    with ExitStack() as ctx:
        def sb(name, shape, dt):
            return ctx.enter_context(nc.sbuf_tensor(name, shape, dt))

        vec = sb("ffn_vectors", [P, 2, D], fp32)
        Y = sb("expert_rows", [P, 8, D], fp32)
        eps = sb("out_eps", [P, NT], fp32)
        rstd = sb("out_rstd", [P, NT], fp32)

        s_w = sem("ffn_vectors_loaded")
        s_g = [sem(f"rows_gathered{j}") for j in range(4)]
        s_first = sem("first_added")
        s_moe = sem("second_added")
        s_v = sem("result_chain")
        s_eps = sem("result_variance")
        s_std = sem("result_deviation")
        s_res = sem("result_ready")
        s_out = sem("result_stored")
        REAL = N - (NT - 1) * P

        def across(v):
            return v.unsqueeze(1).to_broadcast([P, CH, D])

        O_c = O[:, :, :].rearrange("p (c t) f -> p c t f", t=CH)
        XN_c = XN[:, :, :].rearrange("p (c t) f -> p c t f", t=CH)

        with nc.Block() as block:

            @block.gpsimd
            def _(pool):
                for t in range(NT):
                    if t >= 4:
                        pool.wait_ge(s_moe, t - 3)
                    for k in range(2):
                        pool.indirect_dma_start(
                            out=Y[:, 2 * (t % 4) + k, :], out_offset=None, in_=ys,
                            in_offset=bass.IndirectOffsetOnAxis(ap=slots[:, k * NT + t:k * NT + t + 1], axis=0)).then_inc(s_g[t % 4], 16)

            @block.sync
            def _(sp):
                for j, n in enumerate(("ffn_gamma", "ffn_beta")):
                    sp.dma_start(vec[:, j, :], a[n].partition_broadcast(P)).then_inc(s_w, 16)
                for c in range(NC):
                    sp.wait_ge(s_res, c + 1)
                    rows = min(N, (c + 1) * CH * P) // P - c * CH
                    sp.dma_start(out[c * CH * P:(c * CH + rows) * P, :].rearrange("(t p) f -> p t f", p=P),
                                 XN_c[:, c, 0:rows, :]).then_inc(s_out, 16)
                sp.dma_start(out[(NT - 1) * P:N, :], XN[0:REAL, NT - 1, :]).then_inc(s_out, 16)
                sp.wait_ge(s_out, 16 * (NC + 1))

            @block.scalar
            def _(act):
                for c in range(NC):
                    act.wait_ge(s_eps, c + 1)
                    cols = slice(CH * c, CH * (c + 1))
                    nc.scalar.activation(eps[:, cols], eps[:, cols], ACT.Sqrt).then_inc(s_std, 1)

            @block.vector
            def _(dve):
                chain = [0]

                def link(ins):
                    chain[0] += 1
                    ins.then_inc(s_v, 1)
                    dve.wait_ge(s_v, chain[0])

                V = nc.vector

                def moe(c):
                    for t in range(CH * c, CH * (c + 1)):
                        dve.wait_ge(s_g[t % 4], 32 * (t // 4 + 1))
                        V.scalar_tensor_tensor(out=XN[:, t, :], in0=Y[:, 2 * (t % 4), :], scalar=prob2[:, 0, t:t + 1],
                                               in1=XN[:, t, :], op0=ALU.mult, op1=ALU.add).then_inc(s_first, 1)
                        dve.wait_ge(s_first, t + 1)
                        V.scalar_tensor_tensor(out=XN[:, t, :], in0=Y[:, 2 * (t % 4) + 1, :], scalar=prob2[:, 1, t:t + 1],
                                               in1=XN[:, t, :], op0=ALU.mult, op1=ALU.add).then_inc(s_moe, 1)
                    dve.wait_ge(s_moe, CH * (c + 1))
                    for t in range(CH * c, CH * (c + 1)):
                        last = V.bn_stats(st[:, t, :], XN[:, t, :])
                    link(last)
                    for t in range(CH * c, CH * (c + 1)):
                        last = V.bn_aggr(mv[:, t, :], st[:, t, :])
                    link(last)
                    cols = slice(CH * c, CH * (c + 1))
                    V.tensor_scalar(eps[:, cols], mv[:, cols, 1], EPS, None, ALU.add).then_inc(s_eps, 1)

                def norm(c):
                    cols = slice(CH * c, CH * (c + 1))
                    dve.wait_ge(s_std, c + 1)
                    link(V.reciprocal(rstd[:, cols], eps[:, cols]))
                    for t in range(CH * c, CH * (c + 1)):
                        last = V.tensor_scalar(XN[:, t, :], XN[:, t, :], mv[:, t, 0:1], rstd[:, t:t + 1], ALU.subtract, ALU.mult)
                    link(last)
                    link(V.tensor_tensor(XN_c[:, c], XN_c[:, c], across(vec[:, 0, :]), ALU.mult))
                    link(V.tensor_tensor(XN_c[:, c], XN_c[:, c], across(vec[:, 1, :]), ALU.add))
                    V.tensor_tensor(XN_c[:, c], XN_c[:, c], O_c[:, c], ALU.add).then_inc(s_res, 1)

                dve.wait_ge(s_w, 32)
                moe(0)
                for c in range(NC):
                    if c + 1 < NC:
                        moe(c + 1)
                    norm(c)


def layouts(inputs):
    x = np.asarray(inputs["x"])
    src = np.asarray(inputs["src"]).astype(np.int32)
    dst = np.asarray(inputs["dst"]).astype(np.int32)
    attr = np.asarray(inputs["edge_attr_256"])
    got = {}
    got["x"] = np.concatenate([x, np.zeros((NP - N, D), x.dtype)])
    got["attr"] = np.concatenate([attr, np.zeros((EPAD - E, D), attr.dtype)])
    g = lambda n: np.asarray(inputs["L0_gnn_" + n])
    got["wkvT"] = np.ascontiguousarray(np.concatenate([g("WK"), g("WV")]).T)
    got["wqT"] = np.ascontiguousarray(g("WQ").T)
    got["weT"] = np.ascontiguousarray(g("WE").T)
    got["bo"] = g("bo")
    got["woT"] = np.ascontiguousarray(g("Wo").T)
    for n in ("gamma", "beta", "mean_scale"):
        got[n] = g(n)
    f = lambda n: np.asarray(inputs["L0_ffn_" + n])
    for n in ("gate_w", "gate_b", "w1", "w2", "b2"):
        got[n] = f(n)
    got["b1"] = np.ascontiguousarray(f("b1").reshape(EXP, NF, P).transpose(0, 2, 1))
    got["ffn_gamma"], got["ffn_beta"] = f("gamma"), f("beta")
    srcp = np.concatenate([src, np.zeros(EPAD - E, np.int32)])
    ids = [np.concatenate([dst, np.full(EPAD - E, N, np.int32)])]
    for size in (G * P, P):
        ends = ids[-1].reshape(-1, P)[:, [0, P - 1]].reshape(-1)
        ids.append(np.concatenate([ends, np.full(size - len(ends), N, np.int32)]))
    near, win = [], []
    for v in ids:
        ext = np.concatenate([[-1], v, [-1]]).astype(np.int32)
        near.append(np.stack([ext[1:-1].reshape(-1, P).T, ext[:-2].reshape(-1, P).T, ext[2:].reshape(-1, P).T], 1))
        rows = np.stack([ext[t * P:t * P + P + 2] for t in range(len(v) // P)])
        rows = np.repeat(rows, H, 0)
        win.append(np.concatenate([rows, np.zeros((-len(rows) % P, P + 2), np.int32)]))
    got["near"] = np.ascontiguousarray(np.concatenate(near, 2))
    got["win"] = np.ascontiguousarray(np.concatenate(win))
    cols = np.stack([srcp.reshape(NG, G, P), ids[0].reshape(NG, G, P)], 1)
    got["idx"] = np.ascontiguousarray(cols.reshape(NG, 2 * G, P).transpose(0, 2, 1))
    return got


def kernel(**inputs):
    import concourse.bacc as bacc
    from concourse.bass_utils import run_bass_kernel_spmd
    nc = bacc.Bacc("TRN2", target_bir_lowering=False, num_devices=1)
    arrays = {"in_" + n: v for n, v in layouts(inputs).items()}
    args = {n[3:]: nc.dram_tensor(n, list(v.shape), mybir.dt.from_np(v.dtype), kind="ExternalInput").ap() for n, v in arrays.items()}
    out = nc.dram_tensor("out", [N, D], fp32, kind="ExternalOutput").ap()
    build(nc, args, out)
    r = run_bass_kernel_spmd(nc, [arrays], core_ids=[0])
    return r.results[0]["out"]
```

```python
import numpy as np
import concourse.bass as bass
from concourse import mybir
from contextlib import ExitStack

N = 6250
E = 100000
D = 256
H = 8
HD = D // H
EXP = 16
F = 512
P = 128
ND = D // P
NF = F // P
NT = -(-N // P)
NP = NT * P
G = 16
NG = -(-E // (P * G))
TE = NG * G
EPAD = TE * P
W = D + 2 * H
RW = W + 1
PART2 = NP
PART3 = PART2 + G * P
ROWS = PART3 + P
NOWHERE = 16384
SLOTS = TE + G + 1
assert 2 * TE <= G * P and 2 * G <= P and ROWS < NOWHERE and G * H == P
EPS = 1e-5
LOW = -1.0e30
QD = 4
RD = 8
CH = 7
NC = NT // CH
TS = 256
WD = 4
TX = -(-((2 * NP + EXP * (TS - 1)) // TS) // WD) * WD
assert NC * CH == NT and TX <= P and NF == 2 * ND == WD

fp32 = mybir.dt.float32
bf16 = mybir.dt.bfloat16
i32 = mybir.dt.int32
ALU = mybir.AluOpType
ACT = mybir.ActivationFunctionType
AX = mybir.AxisListType


def wait(eng, sem, value):
    if isinstance(value, int) and value <= 0:
        return
    eng.wait_ge(sem, value)


def wait_apart(eng, waits, passed, count):
    waits = [(s, v if isinstance(v, int) else eng.to_reg(v)) for s, v in waits if not (isinstance(v, int) and v <= 0)]
    eng.wait_ge(passed, count)
    for s, v in waits:
        eng.wait_ge(s, v)


def rounds(eng, body, first, last):
    g = first
    while g <= last and (g < 3 or g % 2 == 0):
        body(g // 2 if g % 2 == 0 else (g - 1) // 2, 2 * 0 if g % 2 == 0 else 1)
        g += 1
    n = (last - g + 1) // 2
    if n > 0:
        k0 = (g - 1) // 2
        with eng.Fori(k0, k0 + n) as k:
            body(k, 1)
            body(k, 2)
        g += 2 * n
    while g <= last:
        body(g // 2 if g % 2 == 0 else (g - 1) // 2, 0 if g % 2 == 0 else 1)
        g += 1


def build(nc, a, out):
    ctx0 = ExitStack()
    with ctx0:
        taken = []

        def sem(name):
            taken.append(nc.alloc_semaphore(name))
            return taken[-1]

        def free():
            nc.all_engine_barrier()
            nc.clear_and_free_semaphores(taken)
            nc.all_engine_barrier()
            taken.clear()

        def keep(name, shape, dt):
            return ctx0.enter_context(nc.sbuf_tensor(name, shape, dt))

        kv_tab = nc.dram_tensor("kv_tab", [NP, 2 * D], fp32, kind="Internal").ap()
        q_seg = nc.dram_tensor("q_seg", [NP + P, D], fp32, kind="Internal").ap()
        xbo_d = nc.dram_tensor("xbo_d", [NP, D], fp32, kind="Internal").ap()
        tab = nc.dram_tensor("tab", [ROWS, W], fp32, kind="Internal").ap()
        xs = nc.dram_tensor("slot_in", [TX * TS, D], fp32, kind="Internal").ap()
        ys = nc.dram_tensor("slot_out", [TX * TS, D], fp32, kind="Internal").ap()

        ident = keep("ident", [P, P], fp32)
        ones = keep("ones", [P, P], fp32)
        iota_row = keep("iota_row", [P, P], fp32)
        rank = keep("rank", [P, SLOTS], fp32)
        lastf = keep("lastf", [P, SLOTS], fp32)
        target = keep("target", [P, SLOTS], fp32)

        base = keep("base", [1, TE], i32)
        nodes_stage(nc, sem, a, kv_tab, q_seg, xbo_d, tab, xs, ident, ones, iota_row, rank, lastf, target, base)
        free()
        edges_stage(nc, sem, a, kv_tab, q_seg, tab, ident, iota_row, rank, lastf, target, base)
        free()
        merge_stage(nc, sem, a, tab, ident, iota_row, rank, lastf, target)
        O = keep("O", [P, NT, D], fp32)
        XN = keep("XN", [P, NT, D], fp32)
        st = keep("row_stats", [P, NT, 6], fp32)
        mv = keep("row_meanvar", [P, NT, 2], fp32)
        rstd = keep("row_rstd", [P, NT], fp32)
        prob2 = keep("prob2", [P, 2, NT], fp32)
        slots = keep("slots", [P, 2 * NT], i32)
        experts = keep("experts", [P, TX], i32)
        update_stage(nc, sem, a, tab, xbo_d, ident, ones, O, XN, st, mv, rstd)
        route_stage(nc, sem, a, ident, XN, prob2, slots, experts)
        free()
        experts_stage(nc, sem, a, xs, ys, ident, XN, slots, experts)
        result_stage(nc, sem, a, ys, out, O, XN, prob2, slots, st, mv)


def nodes_stage(nc, sem, a, kv_tab, q_seg, xbo_d, tab, xs, ident, ones, iota_row, rank, lastf, target, base):
    with ExitStack() as ctx:
        def sb(name, shape, dt):
            return ctx.enter_context(nc.sbuf_tensor(name, shape, dt))

        def ps(name):
            return ctx.enter_context(nc.psum_tensor(name, [P, 512], fp32))

        wkv = sb("wkv", [P, ND, 2 * D], fp32)
        wq = sb("wq", [P, ND, D], fp32)
        bo = sb("bo", [P, D], fp32)
        neutral = sb("neutral", [P, W], fp32)
        neutral2 = sb("neutral2", [P, W], fp32)
        near = sb("near", [P, 3, SLOTS], i32)
        cur = sb("cur", [P, SLOTS], fp32)
        start = sb("start", [P, SLOTS], bf16)
        slot = sb("slot", [P, SLOTS], fp32)
        sloti = sb("sloti", [P, SLOTS], i32)
        tmp = sb("tmp", [P, SLOTS], fp32)
        iotai = sb("iotai", [P, P], i32)
        iota16 = sb("iota16", [P, P], bf16)
        tri = sb("tri", [P, P], bf16)
        below = sb("below", [P, P], bf16)
        all1 = sb("all1", [P, P], bf16)
        onerow = sb("onerow", [P, TE], fp32)
        at127 = sb("at127", [P, 1], fp32)
        digi = sb("digit_i", [P, 2, TE], i32)
        digit = sb("digit", [P, 2, TE], bf16)
        ohlo = sb("onehot_lo", [P, 2, G, P], bf16)
        ohhi = sb("onehot_hi", [P, 2, G, NT], bf16)
        has = sb("has_edges", [P, NT], fp32)
        has16 = sb("has_edges16", [P, NT], bf16)
        ordf = sb("ordinal_f", [P, NT], fp32)
        ordx = sb("ordinal_x", [P, NT], fp32)
        ordt = sb("ordinal_total", [P, NT], fp32)
        ordi = sb("ordinal", [P, NT], i32)
        X = sb("x_all", [P, NT, D], fp32)
        st = sb("st", [P, NT, 6], fp32)
        mv = sb("mv", [P, NT, 2], fp32)
        eps = sb("eps", [P, NT], fp32)
        rstd = sb("rstd", [P, NT], fp32)
        xn = sb("xn", [P, 2, D], fp32)
        xbo = sb("xbo", [P, 2, D], fp32)
        xnT = sb("xnT", [P, 2, ND, P], fp32)
        kv = sb("kv_o", [P, 2, 2 * D], fp32)
        Q = sb("q_all", [P, NT, D], fp32)
        psT = [ps("psT0"), ps("psT1")]
        psKV = [ps("psKV0"), ps("psKV1")]
        psQ = [ps("psQ0"), ps("psQ1")]
        psC = ps("psC")
        psR = ps("psR")

        s_w = sem("weights_loaded")
        s_near = sem("near_loaded")
        s_const = sem("constants_made")
        s_pool = sem("pool_chain")
        s_neutral = sem("neutral_made")
        s_fill = sem("table_filled")
        s_start = sem("starts_ready")
        s_rank = sem("ranks_summed")
        s_rankc = sem("ranks_copied")
        s_prep = sem("prep_chain")
        s_dig = sem("digits_ready")
        s_x = [sem(f"x_loaded{c}") for c in range(NC)]
        s_eps = sem("variance_ready")
        s_std = sem("deviation_ready")
        s_xn = sem("xn_done")
        s_xbo = sem("xbo_done")
        s_xT = sem("xT_done")
        s_xTc = sem("xT_copied")
        s_kv = sem("kv_done")
        s_kvc = sem("kv_copied")
        s_q = sem("q_done")
        s_qc = sem("q_copied")
        s_lo = sem("onehot_lo_done")
        s_hi = sem("onehot_hi_done")
        s_cnt = sem("edges_counted")
        s_has = sem("has_edges_ready")
        s_ord = sem("ordinals_ready")
        s_oin = sem("ordinal_within_summed")
        s_oinc = sem("ordinal_within_copied")
        s_otot = sem("ordinal_totals_summed")
        s_qs = sem("q_scattered")
        s_out = [sem("node_rows_stored0"), sem("node_rows_stored1")]

        x_c = a["x"].rearrange("(c t p) f -> c p t f", p=P, t=CH)
        kv_t = kv_tab.rearrange("(t p) f -> t p f", p=P)
        xbo_t = xbo_d.rearrange("(t p) f -> t p f", p=P)
        Q2 = Q[:, :, :].rearrange("p t f -> p (t f)")
        X2 = X[:, :, :].rearrange("p t f -> p (t f)")

        with nc.Block() as block:

            @block.sync
            def _(sp):
                sp.dma_start(near[:, :, :], a["near"]).then_inc(s_near, 16)
                for c in range(NC):
                    sp.dma_start(X[:, c * CH:(c + 1) * CH, :], x_c[c]).then_inc(s_x[c], 16)
                sp.dma_start(wkv[:, :, :], a["wkvT"].rearrange("(c p) n -> p c n", p=P)).then_inc(s_w, 16)
                sp.dma_start(wq[:, :, :], a["wqT"].rearrange("(c p) n -> p c n", p=P)).then_inc(s_w, 16)
                sp.dma_start(bo[:, :], a["bo"].partition_broadcast(P)).then_inc(s_w, 16)
                sp.wait_ge(s_neutral, 2)
                for dest, src, width in ((q_seg, neutral, D), (tab[0:NP, :], neutral, W), (tab[NP:ROWS, :], neutral2, W), (xs, neutral, D)):
                    dest = dest.rearrange("(t p) f -> p t f", p=P)
                    sp.dma_start(dest, src[:, 0:width].unsqueeze(1).to_broadcast([P, dest.shape[1], width])).then_inc(s_fill, 16)

                def store(k, c):
                    i, b = 2 * k + c, c % 2
                    wait(sp, s_kvc, i + 1)
                    sp.dma_start(kv_t[i], kv[:, b, :]).then_inc(s_out[b], 16)
                    wait(sp, s_xbo, i + 1)
                    sp.dma_start(xbo_t[i], xbo[:, b, :]).then_inc(s_out[b], 16)

                rounds(sp, store, 0, NT - 1)
                sp.wait_ge(s_fill, 64)
                sp.wait_ge(s_out[0], 32 * ((NT + 1) // 2))
                sp.wait_ge(s_out[1], 32 * (NT // 2))

            @block.gpsimd
            def _(pool):
                pool.memset(neutral[:, :], 0.0).then_inc(s_neutral, 1)
                pool.memset(neutral2[:, 0:D + H], 0.0).then_inc(s_pool, 1)
                pool.memset(neutral2[:, D + H:W], LOW).then_inc(s_neutral, 1)
                pool.memset(ident[:, :], 0.0).then_inc(s_pool, 1)
                pool.memset(ones[:, :], 1.0).then_inc(s_pool, 1)
                pool.iota(iotai[:, :], [[1, P]], base=0, channel_multiplier=0).then_inc(s_pool, 1)
                pool.memset(tri[:, :], 1.0).then_inc(s_pool, 1)
                pool.memset(below[:, :], 1.0).then_inc(s_pool, 1)
                pool.memset(all1[:, :], 1.0).then_inc(s_pool, 1)
                pool.memset(onerow[:, :], 1.0).then_inc(s_pool, 1)
                pool.memset(at127[:, :], 0.0).then_inc(s_pool, 1)
                pool.iota(sloti[:, 0:TE], [[2, TE]], base=PART2, channel_multiplier=0).then_inc(s_pool, 1)
                pool.iota(sloti[:, TE:SLOTS], [[2, G + 1]], base=PART3, channel_multiplier=0).then_inc(s_pool, 1)
                pool.wait_ge(s_pool, 11)
                pool.affine_select(out=ident[:, :], in_=ident[:, :], compare_op=ALU.not_equal, fill=1.0,
                                   base=0, pattern=[[-1, P]], channel_multiplier=1).then_inc(s_const, 1)
                pool.affine_select(out=below[:, :], in_=below[:, :], compare_op=ALU.is_gt, fill=0.0,
                                   base=0, pattern=[[1, P]], channel_multiplier=-1).then_inc(s_const, 1)
                pool.affine_select(out=tri[:, :], in_=tri[:, :], compare_op=ALU.is_ge, fill=0.0,
                                   base=0, pattern=[[1, P]], channel_multiplier=-1).then_inc(s_pool, 1)
                pool.wait_ge(s_pool, 12)
                pool.affine_select(out=tri[:, :], in_=tri[:, :], compare_op=ALU.is_gt, fill=0.0,
                                   base=0, pattern=[[0, P]], channel_multiplier=1).then_inc(s_const, 1)
                pool.affine_select(out=at127[:, :], in_=at127[:, :], compare_op=ALU.not_equal, fill=1.0,
                                   base=-(P - 1), pattern=[[0, 1]], channel_multiplier=1).then_inc(s_const, 1)
                pool.wait_ge(s_w, 48)

                def tile(k, c):
                    i, b = 2 * k + c, c % 2
                    wait(pool, s_xn, i + 1)
                    wait(pool, s_out[b], 32 * (k + c // 2))
                    nc.gpsimd.tensor_tensor(xbo[:, b, :], xn[:, b, :], bo[:, :], ALU.add).then_inc(s_xbo, 1)

                rounds(pool, tile, 0, NT - 1)
                pool.wait_ge(s_fill, 64)
                pool.wait_ge(s_ord, 1)
                pool.wait_ge(s_qc, NT)
                for t in range(NT):
                    pool.indirect_dma_start(
                        out=q_seg, out_offset=bass.IndirectOffsetOnAxis(ap=ordi[:, t:t + 1], axis=0),
                        in_=Q[:, t, :], in_offset=None, bounds_check=NP + P - 1, oob_is_err=False).then_inc(s_qs, 16)
                pool.wait_ge(s_qs, 16 * NT)

            @block.vector
            def _(dve):
                chain = [0]

                def link(ins):
                    chain[0] += 1
                    ins.then_inc(s_prep, 1)
                    dve.wait_ge(s_prep, chain[0])

                V = nc.vector
                dve.wait_ge(s_const, 4)
                dve.wait_ge(s_near, 16)
                V.tensor_copy(iota_row[:, :], iotai[:, :])
                V.tensor_copy(iota16[:, :], iotai[:, :])
                V.tensor_copy(cur[:, :], near[:, 0, :])
                V.tensor_copy(slot[:, :], sloti[:, :])
                V.tensor_tensor(start[:, :], near[:, 0, :], near[:, 1, :], ALU.not_equal).then_inc(s_start, 1)
                V.tensor_scalar(digi[:, 0, :], near[:, 0, 0:TE], P - 1, None, ALU.bitwise_and)
                V.tensor_scalar(digi[:, 1, :], near[:, 0, 0:TE], P.bit_length() - 1, None, ALU.arith_shift_right)
                link(V.tensor_tensor(lastf[:, :], near[:, 0, :], near[:, 2, :], ALU.not_equal))
                V.tensor_copy(digit[:, :, :], digi[:, :, :]).then_inc(s_dig, 1)
                link(V.tensor_scalar(lastf[:, :], lastf[:, :], at127[:, 0:1], None, ALU.max))
                for h in range(2):
                    lo, hi = h * 512, min(SLOTS, (h + 1) * 512)
                    dve.wait_ge(s_rank, h + 1)
                    last = V.tensor_copy(rank[:, lo:hi], psR[:, 0:hi - lo])
                    last.then_inc(s_rankc, 1)
                for h in range(2):
                    lo, hi = h * 512, min(TE, (h + 1) * 512)
                    dve.wait_ge(s_rank, h + 3)
                    last = V.tensor_copy(tmp[:, lo:hi], psR[:, 0:hi - lo])
                    last.then_inc(s_rankc, 1)
                dve.wait_ge(s_rankc, 4)
                link(V.tensor_tensor_scan(onerow[:, :], onerow[:, :], tmp[:, 0:TE], 0.0, ALU.mult, ALU.add))
                link(V.tensor_tensor(tmp[:, 0:TE], onerow[:, :], tmp[:, 0:TE], ALU.subtract))
                link(V.tensor_tensor(tmp[:, 0:TE], tmp[:, 0:TE], start[:, 0:TE], ALU.add))
                link(V.tensor_scalar(base[0:1, :], tmp[0:1, 0:TE], -1.0, None, ALU.add))
                PT = slice(0, TE + G)
                link(V.tensor_tensor(tmp[:, PT], slot[:, PT], cur[:, PT], ALU.subtract))
                link(V.tensor_scalar(tmp[:, PT], tmp[:, PT], 1.0, at127[:, 0:1], ALU.add, ALU.mult))
                link(V.tensor_tensor(target[:, PT], cur[:, PT], tmp[:, PT], ALU.add))
                link(V.tensor_tensor(slot[:, PT], slot[:, PT], target[:, PT], ALU.subtract))
                link(V.tensor_scalar(tmp[:, PT], rank[:, PT], 0.0, None, ALU.is_equal))
                link(V.tensor_tensor(tmp[:, PT], tmp[:, PT], slot[:, PT], ALU.mult))
                link(V.tensor_tensor(target[:, PT], target[:, PT], tmp[:, PT], ALU.add))
                link(V.tensor_copy(target[:, TE + G:SLOTS], cur[:, TE + G:SLOTS]))
                link(V.tensor_scalar(target[:, :], target[:, :], float(-NOWHERE), None, ALU.add))
                link(V.tensor_tensor(target[:, :], target[:, :], lastf[:, :], ALU.mult))
                for c in range(NC):
                    dve.wait_ge(s_x[c], 16)
                    for t in range(CH * c, CH * (c + 1)):
                        last = V.bn_stats(st[:, t, :], X[:, t, :])
                    link(last)
                    for t in range(CH * c, CH * (c + 1)):
                        last = V.bn_aggr(mv[:, t, :], st[:, t, :])
                    link(last)
                V.tensor_scalar(eps[:, :], mv[:, :, 1], EPS, None, ALU.add).then_inc(s_eps, 1)
                dve.wait_ge(s_std, 1)
                link(V.reciprocal(rstd[:, :], eps[:, :]))

                def tile(k, c):
                    i, b = 2 * k + c, c % 2
                    wait(dve, s_xT, i - 1)
                    wait(dve, s_xbo, i - 1)
                    V.tensor_scalar(xn[:, b, :], X2[:, span(i)], mean2[:, span(i, 1)], rstd[:, span(i, 1)],
                                    ALU.subtract, ALU.mult).then_inc(s_xn, 1)
                    wait(dve, s_cnt, i - 1)
                    V.tensor_tensor(ohlo[:, b, :, :], digit[:, 0, span(i, G)].unsqueeze(2).to_broadcast([P, G, P]),
                                    iota16[:, :].unsqueeze(1).to_broadcast([P, G, P]), ALU.is_equal).then_inc(s_lo, 1)
                    V.tensor_tensor(ohhi[:, b, :, :], digit[:, 1, span(i, G)].unsqueeze(2).to_broadcast([P, G, NT]),
                                    iota16[:, 0:NT].unsqueeze(1).to_broadcast([P, G, NT]), ALU.is_equal).then_inc(s_hi, 1)

                mean2 = ordx
                link(V.tensor_copy(mean2[:, :], mv[:, :, 0]))
                rounds(dve, tile, 0, NT - 1)
                dve.wait_ge(s_cnt, NT)
                link(V.tensor_scalar(has[:, :], psC[:, 0:NT], 0.0, None, ALU.is_gt))
                V.tensor_copy(has16[:, :], has[:, :]).then_inc(s_has, 1)
                dve.wait_ge(s_oin, 1)
                V.tensor_copy(ordf[:, :], psR[:, 0:NT]).then_inc(s_oinc, 1)
                dve.wait_ge(s_otot, 1)
                link(V.tensor_copy(ordt[:, :], psR[:, 0:NT]))
                link(V.tensor_tensor_scan(ordx[:, :], ones[:, 0:NT], ordt[:, :], 0.0, ALU.mult, ALU.add))
                link(V.tensor_tensor(ordx[:, :], ordx[:, :], ordt[:, :], ALU.subtract))
                link(V.tensor_tensor(ordf[:, :], ordf[:, :], ordx[:, :], ALU.add))
                link(V.tensor_scalar(has[:, :], has[:, :], float(-NOWHERE), float(NOWHERE), ALU.mult, ALU.add))
                link(V.tensor_tensor(ordf[:, :], ordf[:, :], has[:, :], ALU.add))
                V.tensor_copy(ordi[:, :], ordf[:, :]).then_inc(s_ord, 1)

            @block.tensor
            def _(pe):
                pe.wait_ge(s_const, 4)
                pe.wait_ge(s_start, 1)
                for h in range(4):
                    m, hi = (tri, SLOTS) if h < 2 else (all1, TE)
                    lo = h % 2 * 512
                    hi = min(hi, lo + 512)
                    wait(pe, s_rankc, h)
                    nc.tensor.matmul(psR[:, 0:hi - lo], m[:, :], start[:, lo:hi], start=True, stop=True).then_inc(s_rank, 1)
                pe.wait_ge(s_w, 48)

                def tile(k, c):
                    i, b = 2 * k + c, c % 2
                    wait(pe, s_xn, i + 1)
                    wait(pe, s_xTc, i - 1)
                    for f in range(ND):
                        mm = nc.tensor.transpose(psT[b][:, f * P:(f + 1) * P], xn[:, b, f * P:(f + 1) * P], ident[:, :])
                    mm.then_inc(s_xT, 1)

                def count(k, c):
                    i, b = 2 * k + c, c % 2
                    wait(pe, s_lo, i + 1)
                    wait(pe, s_hi, i + 1)
                    first, last = isinstance(i, int) and i == 0, isinstance(i, int) and i == NT - 1
                    for t in range(G):
                        mm = nc.tensor.matmul(psC[:, 0:NT], ohlo[:, b, t, :], ohhi[:, b, t, :],
                                              start=first and t == 0, stop=last and t == G - 1)
                    mm.then_inc(s_cnt, 1)

                def products(k, c):
                    i, b = 2 * k + c, c % 2
                    wait(pe, s_xTc, i + 1)
                    wait(pe, s_kvc, i - 1)
                    for f in range(ND):
                        mm = nc.tensor.matmul(psKV[b][:, :], xnT[:, b, f, :], wkv[:, f, :], start=f == 0, stop=f == ND - 1)
                    mm.then_inc(s_kv, 1)
                    wait(pe, s_qc, i - 1)
                    for f in range(ND):
                        mm = nc.tensor.matmul(psQ[b][:, 0:D], xnT[:, b, f, :], wq[:, f, :], start=f == 0, stop=f == ND - 1)
                    mm.then_inc(s_q, 1)

                def period(k, c):
                    tile(k, c)
                    products(k, c)
                    count(k, c)

                rounds(pe, period, 0, NT - 2)
                period(NT // 2, 0)
                pe.wait_ge(s_has, 1)
                nc.tensor.matmul(psR[:, 0:NT], below[:, :], has16[:, :], start=True, stop=True).then_inc(s_oin, 1)
                pe.wait_ge(s_oinc, 1)
                nc.tensor.matmul(psR[:, 0:NT], all1[:, :], has16[:, :], start=True, stop=True).then_inc(s_otot, 1)

            @block.scalar
            def _(act):
                act.wait_ge(s_eps, 1)
                nc.scalar.activation(eps[:, :], eps[:, :], ACT.Sqrt).then_inc(s_std, 1)

                def tile(k, c):
                    i, b = 2 * k + c, c % 2
                    wait(act, s_xT, i + 1)
                    wait(act, s_q, i - 1)
                    nc.scalar.copy(xnT[:, b, :, :].rearrange("p c n -> p (c n)"), psT[b][:, 0:D]).then_inc(s_xTc, 1)
                    wait(act, s_kv, i + 1)
                    wait(act, s_out[b], 32 * (k + c // 2))
                    nc.scalar.copy(kv[:, b, :], psKV[b][:, :]).then_inc(s_kvc, 1)
                    wait(act, s_q, i + 1)
                    nc.scalar.activation(Q2[:, span(i)], psQ[b][:, 0:D], ACT.Copy, scale=float(HD) ** -0.5).then_inc(s_qc, 1)

                rounds(act, tile, 0, NT - 1)


def edges_stage(nc, sem, a, kv_tab, q_seg, tab, ident, iota_row, rank, lastf, target, base):
    with ExitStack() as ctx:
        def sb(name, shape, dt):
            return ctx.enter_context(nc.sbuf_tensor(name, shape, dt))

        def ps(name):
            return ctx.enter_context(nc.psum_tensor(name, [P, 512], fp32))

        we = sb("we", [P, ND, D], fp32)
        AT = sb("attr_in", [P, 2, G, D], fp32)
        KV = sb("kv_in", [P, 2, G, 2 * D], fp32)
        Q = sb("q_in", [P, QD, D], fp32)
        prod = sb("prod", [P, 2, D], fp32)
        idx = sb("idx_in", [P, 2, G], i32)
        win = sb("win_in", [P, 2, P + 2], i32)
        aT = sb("attrT", [P, 2, D + P], fp32)
        S = sb("scores", [P, 2, P], fp32)
        mask = sb("mask", [P, P + 1], fp32)
        fwd = sb("max_fwd", [P, P], fp32)
        bwd = sb("max_bwd", [P, P], fp32)
        mT = sb("maxT", [P, P], fp32)
        pT = sb("probT", [P, P], fp32)
        R = sb("rhs", [P, G, RW], fp32)
        OH = sb("onehot", [P, 2, G, P], fp32)
        ROW = sb("rows_out", [P, RD, W], fp32)
        TGT = sb("targets_out", [P, RD, 1], i32)
        psA = [ps("psA0"), ps("psA1")]
        psE = [ps("psE0"), ps("psE1")]
        psO = [ps("psO0"), ps("psO1")]
        psS, psB = ps("psS"), ps("psB")

        s_we = sem("we_loaded")
        s_attr = [sem("attr_loaded0"), sem("attr_loaded1")]
        s_idx = [sem("idx_loaded0"), sem("idx_loaded1")]
        s_win = [sem("win_loaded0"), sem("win_loaded1")]
        s_gat = [[sem(f"gathered{b}_{j}") for j in range(4)] for b in range(2)]
        s_ql = [sem(f"q_loaded{j}") for j in range(QD)]
        s_aT = sem("attr_transposed")
        s_aTc = sem("attrT_copied")
        s_e = sem("e_done")
        s_kve = sem("kve_done")
        s_prod = sem("prod_done")
        s_score = sem("score_done")
        s_ne = sem("change_found")
        s_mask = sem("mask_done")
        s_sT = sem("scores_transposed")
        s_fwd = sem("fwd_max_done")
        s_bwd = sem("bwd_max_done")
        s_mT = sem("max_done")
        s_dT = sem("diff_done")
        s_pT = sem("probs_done")
        s_back = sem("probs_back")
        s_prob = sem("probs_copied")
        s_lm = sem("max_copied")
        s_tc = sem("targets_copied")
        s_oh = sem("onehot_done")
        s_pve = sem("pve_done")
        s_agg = sem("agg_done")
        s_row = sem("row_copied")
        s_tgt = sem("target_copied")
        s_scat = [sem(f"scattered{j}") for j in range(RD)]

        attr_g = a["attr"].rearrange("(g t p) f -> g p t f", p=P, t=G)
        win_g = a["win"].rearrange("(g p) w -> g p w", p=P)
        BACKS = {6 + j: (2 * j, 2 * j + 1) for j in range(8)}
        SUMS = {8 + j: (2 * j, 2 * j + 1) for j in range(8)}

        with nc.Block() as block:

            @block.sync
            def _(sp):
                def load_attr(k, c, j):
                    g, b = 2 * k + c, c % 2
                    if j == 0:
                        wait(sp, s_aT, G * (g - 1))
                    sp.dma_start(AT[:, b, 2 * j:2 * j + 2, :], attr_g[g][:, 2 * j:2 * j + 2, :]).then_inc(s_attr[b], 16)

                def load_idx(k, c):
                    b = c % 2
                    for j in range(4):
                        wait(sp, s_gat[b][j], 64 * (k + c // 2))
                    sp.dma_start(idx[:, b, :], a["idx"][2 * k + c]).then_inc(s_idx[b], 16)

                def load_win(k, c):
                    g, b = 2 * k + c, c % 2
                    wait(sp, s_ne, g - 1)
                    sp.dma_start(win[:, b, :], win_g[g]).then_inc(s_win[b], 16)

                def load_q(k, c, t):
                    n = G * (2 * k + c) + t
                    first = sp.value_load(base[0:1, span(n, 1)], min_val=0, max_val=NP)
                    wait(sp, s_e, n - QD + 1)
                    sp.dma_start(Q[:, t % QD, :], q_seg[bass.ds(first, P), :]).then_inc(s_ql[t % QD], 16)

                def period(k, c, more=2):
                    for t in range(QD):
                        load_q(k, c, t)
                    load_win(k, c)
                    for t in range(QD, G):
                        load_q(k, c, t)
                        if more > 0 and t < QD + G // 2:
                            load_attr(k, c + 1, t - QD)
                        if more > 1 and t == G - 3:
                            load_idx(k + 1, c)

                sp.dma_start(we[:, :, :], a["weT"].rearrange("(c p) n -> p c n", p=P)).then_inc(s_we, 16)
                load_idx(0, 0)
                load_idx(0, 1)
                for j in range(G // 2):
                    load_attr(0, 0, j)
                rounds(sp, period, 0, NG - 3)
                period((NG - 2) // 2, (NG - 2) % 2, 1)
                period((NG - 1) // 2, (NG - 1) % 2, 0)

            @block.gpsimd
            def _(pool):
                def gather(k, c, t):
                    b = c % 2
                    ready = [(s_idx[b], 16 * (k + c // 2 + 1))] if t == 0 else []
                    wait_apart(pool, ready + [(s_pve, G * (2 * k + c - 2) + t + 1)], s_idx[b], 16)
                    pool.indirect_dma_start(
                        out=KV[:, b, t, :], out_offset=None, in_=kv_tab,
                        in_offset=bass.IndirectOffsetOnAxis(ap=idx[:, b, t:t + 1], axis=0)).then_inc(s_gat[b][t // 4], 16)

                def scatter(k, c, t):
                    n = G * (2 * k + c) + t
                    wait_apart(pool, [(s_row, n + 1), (s_tgt, n + 1)], s_idx[0], 16)
                    pool.indirect_dma_start(
                        out=tab, out_offset=bass.IndirectOffsetOnAxis(ap=TGT[:, t % RD, :], axis=0),
                        in_=ROW[:, t % RD, :], in_offset=None,
                        bounds_check=ROWS - 1, oob_is_err=False).then_inc(s_scat[t % RD], 16)

                def period(k, c):
                    for t in range(G):
                        gather(k + 1, c, t)
                        if t:
                            scatter(k, c, t - 1)
                    scatter(k, c, G - 1)

                for g in range(2):
                    for t in range(G):
                        gather(0, g, t)
                rounds(pool, period, 0, NG - 3)
                for g in (NG - 2, NG - 1):
                    for t in range(G):
                        scatter(g // 2, g % 2, t)
                for j in range(RD):
                    pool.wait_ge(s_scat[j], 16 * (TE // RD))

            @block.vector
            def _(dve):
                def onehot(k, c, t):
                    n, b = G * (2 * k + c) + t, c % 2
                    wait(dve, s_agg, n - 2 * G + 1)
                    nc.vector.tensor_scalar(OH[:, b, t, :], iota_row[:, :], rank[:, span(n, 1)], None,
                                            ALU.is_equal).then_inc(s_oh, 1)

                def front_sum(k, c, t):
                    n, b = G * (2 * k + c) + t, c % 2
                    if t % 4 == 0:
                        wait(dve, s_gat[b][t // 4], 64 * (k + c // 2 + 1))
                    wait(dve, s_e, n + 1)
                    e2 = psE[t % 2][:, 0:D].unsqueeze(1).to_broadcast([P, 2, D])
                    kv2 = KV[:, b, t, :].rearrange("p (a f) -> p a f", a=2)
                    nc.vector.tensor_tensor(kv2, kv2, e2, ALU.add).then_inc(s_kve, 1)

                def front_product(k, c, t):
                    n, b = G * (2 * k + c) + t, c % 2
                    wait(dve, s_kve, n + 1)
                    nc.vector.tensor_tensor(prod[:, t % 2, :], KV[:, b, t, 0:D], psE[t % 2][:, D:2 * D], ALU.mult).then_inc(s_prod, 1)

                def front_score(k, c, t):
                    n, b = G * (2 * k + c) + t, c % 2
                    wait(dve, s_prod, n + 1)
                    nc.vector.tensor_reduce(S[:, b, t * H:(t + 1) * H], prod[:, t % 2, :].rearrange("p (h d) -> p h d", h=H),
                                            AX.X, ALU.add).then_inc(s_score, 1)

                def masks(k, c):
                    g, b = 2 * k + c, c % 2
                    wait(dve, s_win[b], 16 * (k + c // 2 + 1))
                    nc.vector.tensor_tensor(mask[:, :], win[:, b, 0:P + 1], win[:, b, 1:P + 2], ALU.not_equal).then_inc(s_ne, 1)
                    wait(dve, s_ne, g + 1)
                    nc.vector.tensor_scalar(mask[:, :], mask[:, :], LOW, None, ALU.mult).then_inc(s_mask, 1)

                def maxima(k, c):
                    g = 2 * k + c
                    wait(dve, s_mask, g + 1)
                    wait(dve, s_sT, g + 1)
                    nc.vector.tensor_tensor_scan(fwd[:, :], mask[:, 0:P], psS[:, 0:P], LOW, ALU.add, ALU.max).then_inc(s_fwd, 1)
                    nc.vector.tensor_tensor_scan(bwd[:, ::-1], mask[:, P:0:-1], psS[:, P - 1::-1], LOW,
                                                 ALU.add, ALU.max).then_inc(s_bwd, 1)
                    wait(dve, s_bwd, g + 1)
                    wait(dve, s_fwd, g + 1)
                    nc.vector.tensor_tensor(mT[:, :], fwd[:, :], bwd[:, :], ALU.max).then_inc(s_mT, 1)
                    wait(dve, s_mT, g + 1)
                    nc.vector.tensor_tensor(fwd[:, :], psS[:, 0:P], mT[:, :], ALU.subtract).then_inc(s_dT, 1)

                def small(k, c):
                    g = 2 * k + c
                    cols = bass.ds(G * g, G)
                    wait(dve, s_back, g + 1)
                    wait(dve, s_agg, G * g)
                    nc.vector.tensor_copy(R[:, :, D:D + H], psB[:, 0:P].rearrange("p (t h) -> p t h", h=H)).then_inc(s_prob, 1)
                    nc.vector.tensor_tensor(R[:, :, D + H:W], psB[:, P:2 * P].rearrange("p (t h) -> p t h", h=H),
                                            lastf[:, cols].unsqueeze(2).to_broadcast([P, G, H]), ALU.mult).then_inc(s_lm, 1)
                    nc.vector.tensor_copy(R[:, :, W:RW], target[:, cols].unsqueeze(2)).then_inc(s_tc, 1)

                def back(k, c, t):
                    n, b = G * (2 * k + c) + t, c % 2
                    if t == 0:
                        wait(dve, s_prob, 2 * k + c + 1)
                    nc.vector.tensor_tensor(
                        R[:, t, 0:D].rearrange("p (h d) -> p h d", h=H),
                        KV[:, b, t, D:2 * D].rearrange("p (h d) -> p h d", h=H),
                        R[:, t, D:D + H].unsqueeze(2).to_broadcast([P, H, HD]), ALU.mult).then_inc(s_pve, 1)

                def period(k, c, do_front=True, do_back=True, last=False):
                    for t in range(G):
                        backs = BACKS.get(t, ()) if do_back else ()
                        if do_back and t == 3:
                            masks(*prev(k, c))
                            maxima(*prev(k, c))
                        if do_back and t == 6:
                            small(*prev(k, c))
                        if do_front:
                            front_sum(k, c, t)
                        if do_front and t + 3 < G:
                            onehot(k, c, t + 3)
                        elif do_front and not last:
                            onehot(k, c + 1, t + 3 - G)
                        for j in backs[1:]:
                            back(*prev(k, c), j - 1)
                        if do_front:
                            front_product(k, c, t)
                        for j in backs[1:]:
                            back(*prev(k, c), j)
                        if do_front:
                            front_score(k, c, t)

                onehot(0, 0, 0)
                onehot(0, 0, 1)
                onehot(0, 0, 2)
                period(0, 0, True, False)
                rounds(dve, period, 1, NG - 2)
                period((NG - 1) // 2, (NG - 1) % 2, last=True)
                period(NG // 2, NG % 2, False, True)

            @block.tensor
            def _(pe):
                def front_in(k, c, t):
                    n, b = G * (2 * k + c) + t, c % 2
                    if t == 0:
                        wait(pe, s_attr[b], 16 * (G // 2) * (k + c // 2 + 1))
                    wait(pe, s_aTc, n - 1)
                    for f in range(ND):
                        mm = nc.tensor.transpose(psA[t % 2][:, f * P:(f + 1) * P], AT[:, b, t, f * P:(f + 1) * P], ident[:, :])
                    wait(pe, s_oh, n + 1)
                    nc.tensor.transpose(psA[t % 2][:, D:D + P], OH[:, b, t, :], ident[:, :]).then_inc(s_aT, 1)

                def front_out(k, c, t):
                    n = G * (2 * k + c) + t
                    wait(pe, s_aTc, n + 1)
                    wait(pe, s_prod, n - 1)
                    for f in range(ND):
                        mm = nc.tensor.matmul(psE[t % 2][:, 0:D], aT[:, t % 2, f * P:(f + 1) * P], we[:, f, :],
                                              start=f == 0, stop=f == ND - 1)
                    wait(pe, s_ql[t % QD], 16 * (G // QD * (2 * k + c) + t // QD + 1))
                    nc.tensor.matmul(psE[t % 2][:, D:2 * D], aT[:, t % 2, D:D + P], Q[:, t % QD, :], start=True, stop=True).then_inc(s_e, 1)

                def agg(k, c, t):
                    n = G * (2 * k + c) + t
                    b = c % 2
                    if t == 0:
                        wait(pe, s_lm, 2 * k + c + 1)
                        wait(pe, s_tc, 2 * k + c + 1)
                    wait(pe, s_pve, n + 1)
                    wait(pe, s_row, n - 1)
                    wait(pe, s_tgt, n - 1)
                    nc.tensor.matmul(psO[t % 2][:, 0:RW], OH[:, b, t, :], R[:, t, :], start=True, stop=True).then_inc(s_agg, 1)

                def period(k, c, do_front=True, do_back=True, last=False):
                    for t in range(G):
                        if do_front and t + 1 < G:
                            front_in(k, c, t + 1)
                        elif do_front and not last:
                            front_in(k, c + 1, 0)
                        if do_back:
                            kk, cc = prev(k, c)
                            g = 2 * kk + cc
                            if t == 2:
                                wait(pe, s_score, G * (g + 1))
                                wait(pe, s_dT, g)
                                nc.tensor.transpose(psS[:, 0:P], S[:, cc % 2, :], ident[:, :]).then_inc(s_sT, 1)
                            if t == 5:
                                wait(pe, s_pT, g + 1)
                                wait(pe, s_mT, g + 1)
                                wait(pe, s_lm, g)
                                nc.tensor.transpose(psB[:, 0:P], pT[:, :], ident[:, :])
                                nc.tensor.transpose(psB[:, P:2 * P], mT[:, :], ident[:, :]).then_inc(s_back, 1)
                            for j in SUMS.get(t, ()):
                                agg(kk, cc, j)
                        if do_front:
                            front_out(k, c, t)

                pe.wait_ge(s_we, 16)
                front_in(0, 0, 0)
                period(0, 0, True, False)
                rounds(pe, period, 1, NG - 2)
                period((NG - 1) // 2, (NG - 1) % 2, last=True)
                period(NG // 2, NG % 2, False, True)

            @block.scalar
            def _(act):
                def front(k, c, t):
                    n = G * (2 * k + c) + t
                    wait(act, s_aT, n + 1)
                    wait(act, s_e, n - 1)
                    nc.scalar.copy(aT[:, t % 2, :], psA[t % 2][:, 0:D + P]).then_inc(s_aTc, 1)

                def back(k, c, t):
                    n = G * (2 * k + c) + t
                    wait(act, s_agg, n + 1)
                    wait(act, s_scat[t % RD], 16 * (G // RD * (2 * k + c) + t // RD))
                    nc.scalar.copy(ROW[:, t % RD, :], psO[t % 2][:, 0:W]).then_inc(s_row, 1)
                    nc.scalar.activation(TGT[:, t % RD, :], psO[t % 2][:, W:RW], ACT.Copy, bias=float(NOWHERE)).then_inc(s_tgt, 1)

                def period(k, c, do_front=True, do_back=True, last=False):
                    for t in range(G):
                        if do_front and t + 1 < G:
                            front(k, c, t + 1)
                        elif do_front and not last:
                            front(k, c + 1, 0)
                        if do_back:
                            kk, cc = prev(k, c)
                            g = 2 * kk + cc
                            if t == 4:
                                wait(act, s_dT, g + 1)
                                wait(act, s_back, g)
                                nc.scalar.activation(pT[:, :], fwd[:, :], ACT.Exp).then_inc(s_pT, 1)
                            for j in SUMS.get(t, ()):
                                back(kk, cc, j)

                front(0, 0, 0)
                period(0, 0, True, False)
                rounds(act, period, 1, NG - 2)
                period((NG - 1) // 2, (NG - 1) % 2, last=True)
                period(NG // 2, NG % 2, False, True)


def one(i):
    return slice(i, i + 1) if isinstance(i, int) else bass.ds(i, 1)


def span(i, width=D):
    return slice(i * width, (i + 1) * width) if isinstance(i, int) else bass.ds(i * width, width)


def prev(k, c):
    return (k, c - 1) if c > 0 else (k - 1, 1)


def merge_stage(nc, sem, a, tab, ident, iota_row, rank, lastf, target):
    with ExitStack() as ctx:
        def sb(name, shape, dt):
            return ctx.enter_context(nc.sbuf_tensor(name, shape, dt))

        def ps(name):
            return ctx.enter_context(nc.psum_tensor(name, [P, 512], fp32))

        IN = sb("merge_in", [P, G, W], fp32)
        win = sb("merge_win", [P, P + 2], i32)
        S = sb("merge_scores", [P, P], fp32)
        mask = sb("merge_mask", [P, P + 1], fp32)
        fwd = sb("merge_fwd", [P, P], fp32)
        bwd = sb("merge_bwd", [P, P], fp32)
        mT = sb("merge_maxT", [P, P], fp32)
        pT = sb("merge_probT", [P, P], fp32)
        PR = sb("merge_prob", [P, G, H], fp32)
        R = sb("merge_rhs", [P, G, RW], fp32)
        OH = sb("merge_onehot", [P, P], fp32)
        ROW = sb("merge_row", [P, W], fp32)
        TGT = sb("merge_target", [P, 1], i32)
        psS, psB, psO = ps("mpsS"), ps("mpsB"), ps("mpsO")

        s_in = sem("merge_loaded")
        s_v = sem("merge_vector")
        s_t = sem("merge_tensor")
        s_a = sem("merge_scalar")
        s_o = sem("merge_scattered")
        LEVELS = [dict(tiles=G, first=PART2, col=TE, v=0, t=0, a=0, o=0)]
        per = 8
        LEVELS.append(dict(tiles=1, first=PART3, col=TE + G, v=per + 2 * G + 2, t=3 + G, a=1 + 2 * G, o=G))
        win_g = a["win"].rearrange("(g p) w -> g p w", p=P)

        with nc.Block() as block:

            @block.sync
            def _(sp):
                for n, lv in enumerate(LEVELS):
                    m = lv["tiles"]
                    sp.wait_ge(s_o, 16 * lv["o"]) if lv["o"] else None
                    sp.dma_start(IN[:, 0:m, :], tab[lv["first"]:lv["first"] + m * P, :].rearrange("(t p) f -> p t f", p=P)).then_inc(s_in, 16)
                    sp.dma_start(win[:, :], win_g[NG + n]).then_inc(s_in, 16)

            @block.vector
            def _(dve):
                done = [0]

                def link(ins):
                    done[0] += 1
                    ins.then_inc(s_v, 1)
                    dve.wait_ge(s_v, done[0])

                for n, lv in enumerate(LEVELS):
                    m = lv["tiles"]
                    q = m * H
                    cols = slice(lv["col"], lv["col"] + m)
                    assert done[0] == lv["v"]
                    dve.wait_ge(s_in, 32 * (n + 1))
                    link(nc.vector.tensor_copy(S[:, 0:q].rearrange("p (t h) -> p t h", h=H), IN[:, 0:m, D + H:W]))
                    link(nc.vector.tensor_tensor(mask[:, :], win[:, 0:P + 1], win[:, 1:P + 2], ALU.not_equal))
                    link(nc.vector.tensor_scalar(mask[:, :], mask[:, :], LOW, None, ALU.mult))
                    dve.wait_ge(s_t, lv["t"] + 1)
                    link(nc.vector.tensor_tensor_scan(fwd[0:q, :], mask[0:q, 0:P], psS[0:q, 0:P], LOW, ALU.add, ALU.max))
                    link(nc.vector.tensor_tensor_scan(bwd[0:q, ::-1], mask[0:q, P:0:-1], psS[0:q, P - 1::-1], LOW, ALU.add, ALU.max))
                    link(nc.vector.tensor_tensor(mT[0:q, :], fwd[0:q, :], bwd[0:q, :], ALU.max))
                    link(nc.vector.tensor_tensor(fwd[0:q, :], psS[0:q, 0:P], mT[0:q, :], ALU.subtract))
                    dve.wait_ge(s_t, lv["t"] + 3)
                    link(nc.vector.tensor_copy(PR[:, 0:m, :], psB[:, 0:q].rearrange("p (t h) -> p t h", h=H)))
                    link(nc.vector.tensor_tensor(R[:, 0:m, D:D + H], PR[:, 0:m, :], IN[:, 0:m, D:D + H], ALU.mult))
                    link(nc.vector.tensor_tensor(R[:, 0:m, D + H:W], psB[:, P:P + q].rearrange("p (t h) -> p t h", h=H),
                                                 lastf[:, cols].unsqueeze(2).to_broadcast([P, m, H]), ALU.mult))
                    link(nc.vector.tensor_copy(R[:, 0:m, W:RW], target[:, cols].unsqueeze(2)))
                    for t in range(m):
                        link(nc.vector.tensor_tensor(
                            R[:, t, 0:D].rearrange("p (h d) -> p h d", h=H), IN[:, t, 0:D].rearrange("p (h d) -> p h d", h=H),
                            PR[:, t, :].unsqueeze(2).to_broadcast([P, H, HD]), ALU.mult))
                        if t:
                            dve.wait_ge(s_t, lv["t"] + 3 + t)
                        link(nc.vector.tensor_scalar(OH[:, :], iota_row[:, :], rank[:, lv["col"] + t:lv["col"] + t + 1], None, ALU.is_equal))
                    if n + 1 < len(LEVELS):
                        LEVELS[n + 1]["v"] = done[0]

            @block.tensor
            def _(pe):
                for n, lv in enumerate(LEVELS):
                    m = lv["tiles"]
                    q = m * H
                    pe.wait_ge(s_v, lv["v"] + 3)
                    nc.tensor.transpose(psS[0:q, 0:P], S[:, 0:q], ident[:, :]).then_inc(s_t, 1)
                    pe.wait_ge(s_a, lv["a"] + 1)
                    nc.tensor.transpose(psB[:, 0:q], pT[0:q, :], ident[0:q, 0:q]).then_inc(s_t, 1)
                    nc.tensor.transpose(psB[:, P:P + q], mT[0:q, :], ident[0:q, 0:q]).then_inc(s_t, 1)
                    for t in range(m):
                        pe.wait_ge(s_v, lv["v"] + 11 + 2 * (t + 1))
                        if t:
                            pe.wait_ge(s_a, lv["a"] + 1 + 2 * t)
                        nc.tensor.matmul(psO[:, 0:RW], OH[:, :], R[:, t, :], start=True, stop=True).then_inc(s_t, 1)

            @block.scalar
            def _(act):
                for n, lv in enumerate(LEVELS):
                    m = lv["tiles"]
                    q = m * H
                    act.wait_ge(s_v, lv["v"] + 7)
                    nc.scalar.activation(pT[0:q, :], fwd[0:q, :], ACT.Exp).then_inc(s_a, 1)
                    for t in range(m):
                        act.wait_ge(s_t, lv["t"] + 3 + t + 1)
                        if lv["o"] + t:
                            act.wait_ge(s_o, 16 * (lv["o"] + t))
                        nc.scalar.copy(ROW[:, :], psO[:, 0:W]).then_inc(s_a, 1)
                        nc.scalar.activation(TGT[:, :], psO[:, W:RW], ACT.Copy, bias=float(NOWHERE)).then_inc(s_a, 1)

            @block.gpsimd
            def _(pool):
                for n, lv in enumerate(LEVELS):
                    for t in range(lv["tiles"]):
                        pool.wait_ge(s_a, lv["a"] + 1 + 2 * (t + 1))
                        pool.indirect_dma_start(
                            out=tab, out_offset=bass.IndirectOffsetOnAxis(ap=TGT[:, :], axis=0),
                            in_=ROW[:, :], in_offset=None, bounds_check=ROWS - 1, oob_is_err=False).then_inc(s_o, 16)
                pool.wait_ge(s_o, 16 * (G + 1))


def update_stage(nc, sem, a, tab, xbo_d, ident, ones, O, XN, st, mv, rstd):
    with ExitStack() as ctx:
        def sb(name, shape, dt):
            return ctx.enter_context(nc.sbuf_tensor(name, shape, dt))

        def ps(name):
            return ctx.enter_context(nc.psum_tensor(name, [P, 512], fp32))

        wo = sb("wo", [P, ND, D], fp32)
        vec = sb("norm_vectors", [P, 3, D], fp32)
        row = sb("row_in", [P, 2, W], fp32)
        xbo = sb("xbo_in", [P, 2, D], fp32)
        zr = sb("inv_sum", [P, 2, H], fp32)
        agg = sb("agg", [P, 2, D], fp32)
        aggT = sb("aggT", [P, 2, D], fp32)
        shift = sb("shift", [P, D], fp32)
        gain = sb("gain", [P, D], fp32)
        var = sb("col_var", [P, D], fp32)
        sq = sb("squares", [P, 2, CH, D], fp32)
        xc = sb("x_chunk", [P, 2, CH, D], fp32)
        eps = sb("var_eps", [P, NT], fp32)
        psT = [ps("upsT0"), ps("upsT1")]
        psY = [ps("upsY0"), ps("upsY1")]
        psM, psV = ps("psM"), ps("psV")

        s_w = sem("update_weights")
        s_in = [sem("rows_loaded0"), sem("rows_loaded1")]
        s_den = sem("sum_guarded")
        s_inv = sem("sum_inverted")
        s_agg = sem("agg_scaled")
        s_aT = sem("agg_transposed")
        s_aTc = sem("aggT_copied")
        s_y = sem("projected")
        s_o = sem("out_rows_done")
        s_mean = sem("mean_summed")
        s_chain = sem("norm_chain")
        s_cent = sem("centred")
        s_sq = sem("squared")
        s_sum = sem("squares_summed")
        s_var = sem("variance_summed")
        s_veps = sem("variance_done")
        s_std = sem("deviation_done")
        s_gain = sem("gain_done")
        s_x = [sem("x_chunk_loaded0"), sem("x_chunk_loaded1")]
        s_pre = sem("pre_gelu_done")
        s_gelu = sem("gelu_done")
        s_x2 = sem("residual_done")
        s_eps2 = sem("row_variance_done")
        s_std2 = sem("row_deviation_done")

        tab_t = tab[0:NP, :].rearrange("(t p) f -> t p f", p=P)
        xbo_t = xbo_d.rearrange("(t p) f -> t p f", p=P)
        x_c = a["x"].rearrange("(c t p) f -> c p t f", p=P, t=CH)
        O2 = O[:, :, :].rearrange("p t f -> p (t f)")
        O_c = O[:, :, :].rearrange("p (c t) f -> p c t f", t=CH)
        XN_c = XN[:, :, :].rearrange("p (c t) f -> p c t f", t=CH)
        REAL = N - (NT - 1) * P

        def across(v):
            return v.unsqueeze(1).to_broadcast([P, CH, D])

        with nc.Block() as block:

            @block.sync
            def _(sp):
                sp.dma_start(wo[:, :, :], a["woT"].rearrange("(c p) n -> p c n", p=P)).then_inc(s_w, 16)
                for j, n in enumerate(("gamma", "beta", "mean_scale")):
                    sp.dma_start(vec[:, j, :], a[n].partition_broadcast(P)).then_inc(s_w, 16)

                def load(k, c):
                    i, b = 2 * k + c, c % 2
                    wait(sp, s_agg, i - 1)
                    sp.dma_start(row[:, b, :], tab_t[i]).then_inc(s_in[b], 16)
                    wait(sp, s_o, i - 1)
                    sp.dma_start(xbo[:, b, :], xbo_t[i]).then_inc(s_in[b], 16)

                rounds(sp, load, 0, NT - 1)
                for c in range(NC):
                    if c >= 2:
                        sp.wait_ge(s_x2, c - 1)
                    sp.dma_start(xc[:, c % 2, :, :], x_c[c]).then_inc(s_x[c % 2], 16)

            @block.vector
            def _(dve):
                def tile(k, c):
                    i, b = 2 * k + c, c % 2
                    wait(dve, s_in[b], 32 * (k + c // 2 + 1))
                    nc.vector.tensor_scalar(zr[:, b, :], row[:, b, D:D + H], 1e-30, None, ALU.max).then_inc(s_den, 1)
                    wait(dve, s_den, i + 1)
                    nc.vector.reciprocal(zr[:, b, :], zr[:, b, :]).then_inc(s_inv, 1)
                    wait(dve, s_inv, i + 1)
                    wait(dve, s_aT, i - 1)
                    nc.vector.tensor_tensor(
                        agg[:, b, :].rearrange("p (h d) -> p h d", h=H), row[:, b, 0:D].rearrange("p (h d) -> p h d", h=H),
                        zr[:, b, :].unsqueeze(2).to_broadcast([P, H, HD]), ALU.mult).then_inc(s_agg, 1)

                def finish(k, c):
                    i, b = 2 * k + c, c % 2
                    wait(dve, s_y, i + 1)
                    nc.vector.tensor_tensor(O2[:, span(i)], psY[b][:, 0:D], xbo[:, b, :], ALU.add).then_inc(s_o, 1)

                def period(k, c):
                    tile(k, c)
                    finish(*prev(k, c))

                tile(0, 0)
                rounds(dve, period, 1, NT - 1)
                finish((NT - 1) // 2, 0)

                chain = [0]

                def link(ins):
                    chain[0] += 1
                    ins.then_inc(s_chain, 1)
                    dve.wait_ge(s_chain, chain[0])

                dve.wait_ge(s_w, 64)
                dve.wait_ge(s_mean, 1)
                link(nc.vector.tensor_scalar(shift[:, :], psM[:, 0:D], 1.0 / N, None, ALU.mult))
                link(nc.vector.tensor_tensor(shift[:, :], shift[:, :], vec[:, 2, :], ALU.mult))
                for c in range(NC):
                    nc.vector.tensor_tensor(O_c[:, c], O_c[:, c], across(shift[:, :]), ALU.subtract).then_inc(s_cent, 1)
                dve.wait_ge(s_var, 1)
                nc.vector.tensor_scalar(var[:, :], psV[:, 0:D], 1.0 / N, EPS, ALU.mult, ALU.add).then_inc(s_veps, 1)
                dve.wait_ge(s_std, 1)
                link(nc.vector.reciprocal(gain[:, :], var[:, :]))
                link(nc.vector.tensor_tensor(gain[:, :], gain[:, :], vec[:, 0, :], ALU.mult))

                def pre_gelu(c):
                    dve.wait_ge(s_cent, NC)
                    link(nc.vector.tensor_tensor(O_c[:, c], O_c[:, c], across(gain[:, :]), ALU.mult))
                    if c >= 2:
                        dve.wait_ge(s_gelu, c - 1)
                    nc.vector.tensor_tensor(sq[:, c % 2, :, :], O_c[:, c], across(vec[:, 1, :]), ALU.add).then_inc(s_pre, 1)

                def residual(c):
                    dve.wait_ge(s_gelu, c + 1)
                    dve.wait_ge(s_x[c % 2], 16 * (c // 2 + 1))
                    nc.vector.tensor_tensor(O_c[:, c], XN_c[:, c], xc[:, c % 2, :, :], ALU.add).then_inc(s_x2, 1)

                def stats(c):
                    dve.wait_ge(s_x2, c + 1)
                    for t in range(CH * c, CH * (c + 1)):
                        last = nc.vector.bn_stats(st[:, t, :], O[:, t, :])
                    link(last)
                    for t in range(CH * c, CH * (c + 1)):
                        last = nc.vector.bn_aggr(mv[:, t, :], st[:, t, :])
                    link(last)

                pre_gelu(0)
                for c in range(NC):
                    if c + 1 < NC:
                        pre_gelu(c + 1)
                    residual(c)
                    stats(c)
                nc.vector.tensor_scalar(eps[:, :], mv[:, :, 1], EPS, None, ALU.add).then_inc(s_eps2, 1)
                dve.wait_ge(s_std2, 1)
                link(nc.vector.reciprocal(rstd[:, :], eps[:, :]))
                for t in range(NT):
                    last = nc.vector.tensor_scalar(XN[:, t, :], O[:, t, :], mv[:, t, 0:1], rstd[:, t:t + 1], ALU.subtract, ALU.mult)
                link(last)

            @block.tensor
            def _(pe):
                pe.wait_ge(s_w, 64)

                def product(k, c):
                    i, b = 2 * k + c, c % 2
                    wait(pe, s_agg, i + 1)
                    wait(pe, s_aTc, i - 1)
                    for f in range(ND):
                        mm = nc.tensor.transpose(psT[b][:, f * P:(f + 1) * P], agg[:, b, f * P:(f + 1) * P], ident[:, :])
                    mm.then_inc(s_aT, 1)
                    wait(pe, s_aTc, i + 1)
                    wait(pe, s_o, i - 1)
                    for f in range(ND):
                        mm = nc.tensor.matmul(psY[b][:, 0:D], aggT[:, b, f * P:(f + 1) * P], wo[:, f, :], start=f == 0, stop=f == ND - 1)
                    mm.then_inc(s_y, 1)

                def mean(k, c, rows=P):
                    i = 2 * k + c
                    wait(pe, s_o, i + 1)
                    first, last = isinstance(i, int) and i == 0, isinstance(i, int) and i == NT - 1
                    mm = nc.tensor.matmul(psM[:, 0:D], ones[0:rows, :], O2[0:rows, span(i)], start=first, stop=last)
                    if last:
                        mm.then_inc(s_mean, 1)

                def period(k, c):
                    product(k, c)
                    mean(*prev(k, c))

                product(0, 0)
                rounds(pe, period, 1, NT - 1)
                mean((NT - 1) // 2, 0, REAL)
                for c in range(NC):
                    pe.wait_ge(s_sq, c + 1)
                    for t in range(CH):
                        rows = REAL if c * CH + t == NT - 1 else P
                        mm = nc.tensor.matmul(psV[:, 0:D], ones[0:rows, :], sq[0:rows, c % 2, t, :],
                                              start=c + t == 0, stop=rows == REAL)
                    mm.then_inc(s_sum, 1)
                pe.wait_ge(s_sum, NC)
                pe.nop().then_inc(s_var, 1)

            @block.scalar
            def _(act):
                def tile(k, c):
                    i, b = 2 * k + c, c % 2
                    wait(act, s_aT, i + 1)
                    wait(act, s_y, i - 1)
                    nc.scalar.copy(aggT[:, b, :], psT[b][:, 0:D]).then_inc(s_aTc, 1)

                rounds(act, tile, 0, NT - 1)
                for c in range(NC):
                    act.wait_ge(s_cent, c + 1)
                    if c >= 2:
                        act.wait_ge(s_sum, c - 1)
                    nc.scalar.activation(sq[:, c % 2, :, :], O_c[:, c], ACT.Square).then_inc(s_sq, 1)
                act.wait_ge(s_veps, 1)
                nc.scalar.activation(var[:, :], var[:, :], ACT.Sqrt).then_inc(s_std, 1)
                for c in range(NC):
                    act.wait_ge(s_pre, c + 1)
                    nc.scalar.activation(XN_c[:, c], sq[:, c % 2, :, :], ACT.Gelu).then_inc(s_gelu, 1)
                act.wait_ge(s_eps2, 1)
                nc.scalar.activation(eps[:, :], eps[:, :], ACT.Sqrt).then_inc(s_std2, 1)


def route_stage(nc, sem, a, ident, XN, prob2, slots, experts):
    J = 2 * NT
    MT = -(-NP // TS)
    with ExitStack() as ctx:
        def sb(name, shape, dt):
            return ctx.enter_context(nc.sbuf_tensor(name, shape, dt))

        def ps(name):
            return ctx.enter_context(nc.psum_tensor(name, [P, 512], fp32))

        wg = sb("gate_w", [P, ND, EXP], fp32)
        bg = sb("gate_b", [P, EXP], fp32)
        xT = sb("gate_xT", [P, 2, D], fp32)
        L = sb("logits", [P, NT, EXP], fp32)
        top = sb("top", [P, 2, NT], fp32)
        pick = sb("pick", [P, NT], fp32)
        eq = sb("equal", [P, NT, EXP], fp32)
        numi = sb("numbers_i", [P, P], i32)
        num = sb("numbers", [P, P], fp32)
        below = sb("expert_below", [P, EXP], fp32)
        pairs = sb("pairs", [P, EXP, J], fp32)
        pairs16 = sb("pairs16", [P, EXP, J], bf16)
        tri = sb("strict_tri", [P, P], bf16)
        all1 = sb("all_ones", [P, P], bf16)
        keepst = sb("keep_state", [P, EXP, J], fp32)
        total = sb("total", [P, EXP, J], fp32)
        upto = sb("upto", [P, EXP, J], fp32)
        place = sb("place", [P, EXP, J], fp32)
        ntile = sb("expert_tiles", [P, EXP], fp32)
        endt = sb("expert_end", [P, EXP], fp32)
        one16 = sb("one16", [P, EXP], fp32)
        mult = sb("multiples", [P, MT], fp32)
        over = sb("count_over", [P, EXP, MT], fp32)
        ended = sb("expert_ended", [P, TX, EXP], fp32)
        slotf = sb("slot_f", [P, J], fp32)
        eidf = sb("expert_f", [P, TX], fp32)
        psT = [ps("rpsT0"), ps("rpsT1")]
        psL = [ps("psL0"), ps("psL1")]
        psW = [ps(f"psW{j}") for j in range(4)]
        QB = EXP // 4

        s_w = sem("gate_loaded")
        s_c = sem("route_constants")
        s_cc = sem("route_const_chain")
        s_xT = sem("gate_transposed")
        s_xTc = sem("gate_xT_copied")
        s_l = sem("logits_done")
        s_lc = sem("logits_copied")
        s_v = sem("route_chain")
        s_d = sem("top_difference")
        s_e = sem("second_exp")
        s_p = sem("pairs_ready")
        s_in = sem("within_summed")
        s_inc = sem("within_copied")
        s_tot = sem("totals_summed")

        with nc.Block() as block:

            @block.sync
            def _(sp):
                sp.dma_start(wg[:, :, :], a["gate_w"].rearrange("(c p) n -> p c n", p=P)).then_inc(s_w, 16)
                sp.dma_start(bg[:, :], a["gate_b"].partition_broadcast(P)).then_inc(s_w, 16)

            @block.gpsimd
            def _(pool):
                pool.iota(numi[:, :], [[1, P]], base=0, channel_multiplier=0).then_inc(s_cc, 1)
                pool.memset(tri[:, :], 1.0).then_inc(s_cc, 1)
                pool.memset(all1[:, :], 1.0).then_inc(s_cc, 1)
                pool.memset(keepst[:, :, :], 1.0).then_inc(s_cc, 1)
                pool.memset(one16[:, :], 1.0).then_inc(s_cc, 1)
                pool.wait_ge(s_cc, 5)
                pool.affine_select(out=tri[:, :], in_=tri[:, :], compare_op=ALU.is_gt, fill=0.0,
                                   base=0, pattern=[[1, P]], channel_multiplier=-1).then_inc(s_c, 1)
                pool.memset(keepst[:, :, 0:1], 0.0).then_inc(s_c, 1)

            @block.tensor
            def _(pe):
                pe.wait_ge(s_w, 32)

                def tile(i):
                    b = i % 2
                    wait(pe, s_xTc, i - 1)
                    for f in range(ND):
                        mm = nc.tensor.transpose(psT[b][:, f * P:(f + 1) * P], XN[:, i, f * P:(f + 1) * P], ident[:, :])
                    mm.then_inc(s_xT, 1)
                    wait(pe, s_xTc, i + 1)
                    wait(pe, s_lc, i - 1)
                    for f in range(ND):
                        mm = nc.tensor.matmul(psL[b][:, 0:EXP], xT[:, b, f * P:(f + 1) * P], wg[:, f, :], start=f == 0, stop=f == ND - 1)
                    mm.then_inc(s_l, 1)

                for i in range(NT):
                    tile(i)
                pe.wait_ge(s_c, 2)
                pe.wait_ge(s_p, 1)
                for j in range(4):
                    mm = nc.tensor.matmul(psW[j][:, 0:QB * J], tri[:, :], pairs16[:, QB * j:QB * (j + 1), :].rearrange("p e j -> p (e j)"), start=True, stop=True)
                mm.then_inc(s_in, 1)
                pe.wait_ge(s_inc, 1)
                for j in range(4):
                    mm = nc.tensor.matmul(psW[j][:, 0:QB * J], all1[:, :], pairs16[:, QB * j:QB * (j + 1), :].rearrange("p e j -> p (e j)"), start=True, stop=True)
                mm.then_inc(s_tot, 1)

            @block.scalar
            def _(act):
                for i in range(NT):
                    b = i % 2
                    act.wait_ge(s_xT, i + 1)
                    wait(act, s_l, i - 1)
                    nc.scalar.copy(xT[:, b, :], psT[b][:, 0:D]).then_inc(s_xTc, 1)
                act.wait_ge(s_d, 1)
                nc.scalar.activation(prob2[:, 1, :], top[:, 1, :], ACT.Exp).then_inc(s_e, 1)

            @block.vector
            def _(dve):
                chain = [0]

                def link(ins):
                    chain[0] += 1
                    ins.then_inc(s_v, 1)
                    dve.wait_ge(s_v, chain[0])

                V = nc.vector
                dve.wait_ge(s_c, 2)
                link(V.tensor_copy(num[:, :], numi[:, :]))
                link(V.tensor_scalar(below[:, :], num[:, 0:EXP], float(-EXP), None, ALU.add))
                dve.wait_ge(s_w, 32)
                for i in range(NT):
                    dve.wait_ge(s_l, i + 1)
                    last = V.tensor_tensor(L[:, i, :], psL[i % 2][:, 0:EXP], bg[:, :], ALU.add)
                    last.then_inc(s_lc, 1)
                dve.wait_ge(s_lc, NT)
                by_expert = [P, NT, EXP]
                for k in range(2):
                    oh = pairs[:, :, k * NT:(k + 1) * NT].rearrange("p e t -> p t e")
                    link(V.tensor_reduce(top[:, k, :], L[:, :, :], AX.X, ALU.max))
                    link(V.tensor_tensor(eq[:, :, :], L[:, :, :], top[:, k, :].unsqueeze(2).to_broadcast(by_expert), ALU.is_equal))
                    link(V.tensor_tensor(eq[:, :, :], eq[:, :, :], below[:, :].unsqueeze(1).to_broadcast(by_expert), ALU.mult))
                    link(V.tensor_reduce(pick[:, :], eq[:, :, :], AX.X, ALU.min))
                    link(V.tensor_tensor(oh, below[:, :].unsqueeze(1).to_broadcast(by_expert), pick[:, :].unsqueeze(2).to_broadcast(by_expert), ALU.is_equal))
                    if k == 0:
                        link(V.tensor_scalar(eq[:, :, :], oh, LOW, None, ALU.mult))
                        link(V.tensor_tensor(L[:, :, :], L[:, :, :], eq[:, :, :], ALU.add))
                V.tensor_copy(pairs16[:, :, :], pairs[:, :, :]).then_inc(s_p, 1)
                V.tensor_tensor(top[:, 1, :], top[:, 1, :], top[:, 0, :], ALU.subtract).then_inc(s_d, 1)
                dve.wait_ge(s_e, 1)
                link(V.tensor_scalar(pick[:, :], prob2[:, 1, :], 1.0, None, ALU.add))
                link(V.reciprocal(prob2[:, 0, :], pick[:, :]))
                link(V.tensor_tensor(prob2[:, 1, :], prob2[:, 1, :], prob2[:, 0, :], ALU.mult))
                dve.wait_ge(s_in, 1)
                for j in range(4):
                    last = V.tensor_copy(place[:, QB * j:QB * (j + 1), :].rearrange("p e j -> p (e j)"), psW[j][:, 0:QB * J])
                last.then_inc(s_inc, 1)
                dve.wait_ge(s_tot, 1)
                for j in range(4):
                    last = V.tensor_copy(total[:, QB * j:QB * (j + 1), :].rearrange("p e j -> p (e j)"), psW[j][:, 0:QB * J])
                link(last)
                flat = lambda v: v[:, :, :].rearrange("p e j -> p (e j)")
                link(V.tensor_tensor_scan(flat(upto), flat(keepst), flat(total), 0.0, ALU.mult, ALU.add))
                link(V.tensor_tensor(place[:, :, :], place[:, :, :], upto[:, :, :], ALU.add))
                link(V.tensor_tensor(place[:, :, :], place[:, :, :], total[:, :, :], ALU.subtract))
                link(V.tensor_scalar(mult[:, :], num[:, 0:MT], float(TS), None, ALU.mult))
                link(V.tensor_tensor(over[:, :, :], upto[:, :, J - 1:J].to_broadcast([P, EXP, MT]),
                                     mult[:, :].unsqueeze(1).to_broadcast([P, EXP, MT]), ALU.is_gt))
                link(V.tensor_reduce(ntile[:, :], over[:, :, :], AX.X, ALU.add))
                link(V.tensor_tensor_scan(endt[:, :], one16[:, :], ntile[:, :], 0.0, ALU.mult, ALU.add))
                link(V.tensor_tensor(ntile[:, :], endt[:, :], ntile[:, :], ALU.subtract))
                link(V.tensor_scalar(ntile[:, :], ntile[:, :], float(TS), None, ALU.mult))
                link(V.tensor_tensor(place[:, :, :], place[:, :, :], ntile[:, :].unsqueeze(2).to_broadcast([P, EXP, J]), ALU.add))
                link(V.tensor_tensor(place[:, :, :], place[:, :, :], pairs[:, :, :], ALU.mult))
                link(V.tensor_reduce(slotf[:, :], place[:, :, :].rearrange("p e j -> p j e"), AX.X, ALU.add))
                link(V.tensor_copy(slots[:, :], slotf[:, :]))
                link(V.tensor_tensor(ended[:, :, :], num[:, 0:TX].unsqueeze(2).to_broadcast([P, TX, EXP]),
                                     endt[:, :].unsqueeze(1).to_broadcast([P, TX, EXP]), ALU.is_ge))
                link(V.tensor_reduce(eidf[:, :], ended[:, :, :], AX.X, ALU.add))
                link(V.tensor_scalar(experts[:, :], eidf[:, :], float(EXP - 1), None, ALU.min))


def experts_stage(nc, sem, a, xs, ys, ident, XN, slots, experts):
    SH = TS // P
    with ExitStack() as ctx:
        def sb(name, shape, dt):
            return ctx.enter_context(nc.sbuf_tensor(name, shape, dt))

        def ps(name):
            return ctx.enter_context(nc.psum_tensor(name, [P, 512], fp32))

        w1 = sb("w1", [P, WD, ND, F], fp32)
        w2 = sb("w2", [P, WD, NF, D], fp32)
        b1 = sb("b1", [P, WD, NF], fp32)
        b2 = sb("b2", [P, WD, D], fp32)
        xin = sb("slot_x", [P, WD, SH, D], fp32)
        xT = sb("slot_xT", [P, 2, ND * TS], fp32)
        hT = sb("hidden", [P, 2, NF, TS], fp32)
        y = sb("slot_y", [P, 2, SH, D], fp32)
        psT = [ps("epsT0"), ps("epsT1")]
        psH = [[ps(f"epsH{b}{g}") for g in range(2)] for b in range(2)]
        psY = [ps("epsY0"), ps("epsY1")]

        s_sc = sem("slots_written")
        s_lx = [sem(f"slot_x_loaded{j}") for j in range(WD)]
        s_l1 = [sem(f"w1_loaded{j}") for j in range(WD)]
        s_l2 = [sem(f"w2_loaded{j}") for j in range(WD)]
        s_lb = [sem(f"biases_loaded{j}") for j in range(WD)]
        s_xT = sem("slot_transposed")
        s_xTc = sem("slot_xT_copied")
        s_h = [sem("hidden_summed0"), sem("hidden_summed1")]
        s_ha = sem("hidden_done_act")
        s_hv = sem("hidden_done_vector")
        s_y = sem("slot_y_summed")
        s_yc = sem("slot_y_done")
        s_st = [sem("slot_y_stored0"), sem("slot_y_stored1")]

        xs_t = xs.rearrange("(t h p) f -> t p h f", p=P, h=SH)
        ys_t = ys.rearrange("(t h p) f -> t p h f", p=P, h=SH)
        w1_e = a["w1"].rearrange("e (c p) n -> e p c n", p=P)
        w2_e = a["w2"].rearrange("e (c p) n -> e p c n", p=P)

        def before(k, c):
            return (k, c - 1) if c > 0 else (k - 1, WD - 1)

        def after(k, c):
            return (k, c + 1) if c < WD - 1 else (k + 1, 0)

        def tiles(eng, period):
            for c in range(WD):
                period(0, c)
            with eng.Fori(1, TX // WD - 1) as k:
                for c in range(WD):
                    period(k, c)
            for c in range(WD):
                period(TX // WD - 1, c)

        with nc.Block() as block:

            @block.gpsimd
            def _(pool):
                for j in range(2 * NT):
                    pool.indirect_dma_start(
                        out=xs, out_offset=bass.IndirectOffsetOnAxis(ap=slots[:, j:j + 1], axis=0),
                        in_=XN[:, j % NT, :], in_offset=None, bounds_check=TX * TS - 1, oob_is_err=False).then_inc(s_sc, 16)

            @block.sync
            def _(sp):
                def load_weights(k, c):
                    i = WD * k + c
                    e = sp.value_load(experts[0:1, one(i)], min_val=0, max_val=EXP - 1)
                    wait(sp, s_h[1], i - WD + 1)
                    sp.dma_start(w1[:, c, :, :], w1_e[e]).then_inc(s_l1[c], 16)
                    wait(sp, s_ha, i - WD + 1)
                    wait(sp, s_hv, i - WD + 1)
                    sp.dma_start(b1[:, c, :], a["b1"][e]).then_inc(s_lb[c], 16)
                    wait(sp, s_y, i - WD + 1)
                    sp.dma_start(w2[:, c, :, :], w2_e[e]).then_inc(s_l2[c], 16)
                    wait(sp, s_yc, i - WD + 1)
                    sp.dma_start(b2[:, c, :], a["b2"][e].partition_broadcast(P)).then_inc(s_lb[c], 16)

                def load_x(k, c):
                    i = WD * k + c
                    wait(sp, s_xT, i - WD + 1)
                    sp.dma_start(xin[:, c, :, :], xs_t[i]).then_inc(s_lx[c], 16)

                for c in range(WD):
                    load_weights(0, c)
                sp.wait_ge(s_sc, 16 * 2 * NT)
                for c in range(WD):
                    load_x(0, c)
                with sp.Fori(1, TX // WD) as k:
                    for c in range(WD):
                        load_x(k, c)
                        load_weights(k, c)

            @block.tensor
            def _(pe):
                def transposes(k, c):
                    i, b = WD * k + c, c % 2
                    wait(pe, s_lx[c], 16 * (k + 1))
                    wait(pe, s_xTc, i - 1)
                    for d in range(ND):
                        for h in range(SH):
                            at = d * TS + h * P
                            mm = nc.tensor.transpose(psT[b][:, at:at + P], xin[:, c, h, d * P:(d + 1) * P], ident[:, :])
                    mm.then_inc(s_xT, 1)

                def hidden(k, c):
                    i, b = WD * k + c, c % 2
                    wait(pe, s_xTc, i + 1)
                    wait(pe, s_l1[c], 16 * (k + 1))
                    for g in range(2):
                        wait(pe, (s_ha, s_hv)[g], i - 1)
                        for f in (2 * g, 2 * g + 1):
                            for d in range(ND):
                                mm = nc.tensor.matmul(psH[b][g][:, (f % 2) * TS:(f % 2 + 1) * TS], w1[:, c, d, f * P:(f + 1) * P],
                                                      xT[:, b, d * TS:(d + 1) * TS], start=d == 0, stop=d == ND - 1)
                        mm.then_inc(s_h[g], 1)

                def second(k, c):
                    i, b = WD * k + c, c % 2
                    wait(pe, s_ha, i + 1)
                    wait(pe, s_hv, i + 1)
                    wait(pe, s_l2[c], 16 * (k + 1))
                    wait(pe, s_yc, i - 1)
                    for h in range(SH):
                        for f in range(NF):
                            mm = nc.tensor.matmul(psY[b][:, h * D:(h + 1) * D], hT[:, b, f, h * P:(h + 1) * P], w2[:, c, f, :],
                                                  start=f == 0, stop=f == NF - 1)
                    mm.then_inc(s_y, 1)

                def period(k, c):
                    first, last = isinstance(k, int) and k + c == 0, isinstance(k, int) and WD * k + c == TX - 1
                    if not last:
                        transposes(*after(k, c))
                    hidden(k, c)
                    if not first:
                        second(*before(k, c))
                    if last:
                        second(k, c)

                transposes(0, 0)
                tiles(pe, period)

            @block.scalar
            def _(act):
                def copy(k, c):
                    i, b = WD * k + c, c % 2
                    wait(act, s_xT, i + 1)
                    wait(act, s_h[1], i - 1)
                    nc.scalar.copy(xT[:, b, :], psT[b][:, :]).then_inc(s_xTc, 1)

                def relu(k, c):
                    i, b = WD * k + c, c % 2
                    wait(act, s_lb[c], 32 * (k + 1))
                    wait(act, s_h[0], i + 1)
                    wait(act, s_y, i - 1)
                    for f in range(2):
                        last = nc.scalar.activation(hT[:, b, f, :], psH[b][0][:, f * TS:(f + 1) * TS], ACT.Relu, bias=b1[:, c, f:f + 1])
                    last.then_inc(s_ha, 1)

                def store(k, c):
                    i, b = WD * k + c, c % 2
                    wait(act, s_yc, i + 1)
                    act.dma_start(ys_t[i], y[:, b, :, :]).then_inc(s_st[b], 16)

                def period(k, c):
                    first, last = isinstance(k, int) and k + c == 0, isinstance(k, int) and WD * k + c == TX - 1
                    if not last:
                        copy(*after(k, c))
                    relu(k, c)
                    if not first:
                        store(*before(k, c))
                    if last:
                        store(k, c)

                copy(0, 0)
                tiles(act, period)
                for b in range(2):
                    act.wait_ge(s_st[b], 16 * (TX // 2))

            @block.vector
            def _(dve):
                def relu(k, c):
                    i, b = WD * k + c, c % 2
                    wait(dve, s_lb[c], 32 * (k + 1))
                    wait(dve, s_h[1], i + 1)
                    wait(dve, s_y, i - 1)
                    for f in range(2, NF):
                        last = nc.vector.tensor_scalar(hT[:, b, f, :], psH[b][1][:, (f - 2) * TS:(f - 1) * TS], b1[:, c, f:f + 1], 0.0, ALU.add, ALU.max)
                    last.then_inc(s_hv, 1)

                def out_rows(k, c):
                    i, b = WD * k + c, c % 2
                    wait(dve, s_y, i + 1)
                    wait(dve, s_st[b], 16 * (WD // 2 * k + c // 2))
                    nc.vector.tensor_tensor(y[:, b, :, :], psY[b][:, :].rearrange("p (h f) -> p h f", h=SH),
                                            b2[:, c, :].unsqueeze(1).to_broadcast([P, SH, D]), ALU.add).then_inc(s_yc, 1)

                def period(k, c):
                    first, last = isinstance(k, int) and k + c == 0, isinstance(k, int) and WD * k + c == TX - 1
                    relu(k, c)
                    if not first:
                        out_rows(*before(k, c))
                    if last:
                        out_rows(k, c)

                tiles(dve, period)


def result_stage(nc, sem, a, ys, out, O, XN, prob2, slots, st, mv):
    with ExitStack() as ctx:
        def sb(name, shape, dt):
            return ctx.enter_context(nc.sbuf_tensor(name, shape, dt))

        vec = sb("ffn_vectors", [P, 2, D], fp32)
        Y = sb("expert_rows", [P, 8, D], fp32)
        eps = sb("out_eps", [P, NT], fp32)
        rstd = sb("out_rstd", [P, NT], fp32)

        s_w = sem("ffn_vectors_loaded")
        s_g = [sem(f"rows_gathered{j}") for j in range(4)]
        s_first = sem("first_added")
        s_moe = sem("second_added")
        s_v = sem("result_chain")
        s_eps = sem("result_variance")
        s_std = sem("result_deviation")
        s_res = sem("result_ready")
        s_out = sem("result_stored")
        REAL = N - (NT - 1) * P

        def across(v):
            return v.unsqueeze(1).to_broadcast([P, CH, D])

        O_c = O[:, :, :].rearrange("p (c t) f -> p c t f", t=CH)
        XN_c = XN[:, :, :].rearrange("p (c t) f -> p c t f", t=CH)

        with nc.Block() as block:

            @block.gpsimd
            def _(pool):
                for t in range(NT):
                    if t >= 4:
                        pool.wait_ge(s_moe, t - 3)
                    for k in range(2):
                        pool.indirect_dma_start(
                            out=Y[:, 2 * (t % 4) + k, :], out_offset=None, in_=ys,
                            in_offset=bass.IndirectOffsetOnAxis(ap=slots[:, k * NT + t:k * NT + t + 1], axis=0)).then_inc(s_g[t % 4], 16)

            @block.sync
            def _(sp):
                for j, n in enumerate(("ffn_gamma", "ffn_beta")):
                    sp.dma_start(vec[:, j, :], a[n].partition_broadcast(P)).then_inc(s_w, 16)
                for c in range(NC):
                    sp.wait_ge(s_res, c + 1)
                    rows = min(N, (c + 1) * CH * P) // P - c * CH
                    sp.dma_start(out[c * CH * P:(c * CH + rows) * P, :].rearrange("(t p) f -> p t f", p=P),
                                 XN_c[:, c, 0:rows, :]).then_inc(s_out, 16)
                sp.dma_start(out[(NT - 1) * P:N, :], XN[0:REAL, NT - 1, :]).then_inc(s_out, 16)
                sp.wait_ge(s_out, 16 * (NC + 1))

            @block.scalar
            def _(act):
                for c in range(NC):
                    act.wait_ge(s_eps, c + 1)
                    cols = slice(CH * c, CH * (c + 1))
                    nc.scalar.activation(eps[:, cols], eps[:, cols], ACT.Sqrt).then_inc(s_std, 1)

            @block.vector
            def _(dve):
                chain = [0]

                def link(ins):
                    chain[0] += 1
                    ins.then_inc(s_v, 1)
                    dve.wait_ge(s_v, chain[0])

                V = nc.vector

                def moe(c):
                    for t in range(CH * c, CH * (c + 1)):
                        dve.wait_ge(s_g[t % 4], 32 * (t // 4 + 1))
                        V.scalar_tensor_tensor(out=XN[:, t, :], in0=Y[:, 2 * (t % 4), :], scalar=prob2[:, 0, t:t + 1],
                                               in1=XN[:, t, :], op0=ALU.mult, op1=ALU.add).then_inc(s_first, 1)
                        dve.wait_ge(s_first, t + 1)
                        V.scalar_tensor_tensor(out=XN[:, t, :], in0=Y[:, 2 * (t % 4) + 1, :], scalar=prob2[:, 1, t:t + 1],
                                               in1=XN[:, t, :], op0=ALU.mult, op1=ALU.add).then_inc(s_moe, 1)
                    dve.wait_ge(s_moe, CH * (c + 1))
                    for t in range(CH * c, CH * (c + 1)):
                        last = V.bn_stats(st[:, t, :], XN[:, t, :])
                    link(last)
                    for t in range(CH * c, CH * (c + 1)):
                        last = V.bn_aggr(mv[:, t, :], st[:, t, :])
                    link(last)
                    cols = slice(CH * c, CH * (c + 1))
                    V.tensor_scalar(eps[:, cols], mv[:, cols, 1], EPS, None, ALU.add).then_inc(s_eps, 1)

                def norm(c):
                    cols = slice(CH * c, CH * (c + 1))
                    dve.wait_ge(s_std, c + 1)
                    link(V.reciprocal(rstd[:, cols], eps[:, cols]))
                    for t in range(CH * c, CH * (c + 1)):
                        last = V.tensor_scalar(XN[:, t, :], XN[:, t, :], mv[:, t, 0:1], rstd[:, t:t + 1], ALU.subtract, ALU.mult)
                    link(last)
                    link(V.tensor_tensor(XN_c[:, c], XN_c[:, c], across(vec[:, 0, :]), ALU.mult))
                    link(V.tensor_tensor(XN_c[:, c], XN_c[:, c], across(vec[:, 1, :]), ALU.add))
                    V.tensor_tensor(XN_c[:, c], XN_c[:, c], O_c[:, c], ALU.add).then_inc(s_res, 1)

                dve.wait_ge(s_w, 32)
                moe(0)
                for c in range(NC):
                    if c + 1 < NC:
                        moe(c + 1)
                    norm(c)


def layouts(inputs):
    x = np.asarray(inputs["x"])
    src = np.asarray(inputs["src"]).astype(np.int32)
    dst = np.asarray(inputs["dst"]).astype(np.int32)
    attr = np.asarray(inputs["edge_attr_256"])
    got = {}
    got["x"] = np.concatenate([x, np.zeros((NP - N, D), x.dtype)])
    got["attr"] = np.concatenate([attr, np.zeros((EPAD - E, D), attr.dtype)])
    g = lambda n: np.asarray(inputs["L0_gnn_" + n])
    got["wkvT"] = np.ascontiguousarray(np.concatenate([g("WK"), g("WV")]).T)
    got["wqT"] = np.ascontiguousarray(g("WQ").T)
    got["weT"] = np.ascontiguousarray(g("WE").T)
    got["bo"] = g("bo")
    got["woT"] = np.ascontiguousarray(g("Wo").T)
    for n in ("gamma", "beta", "mean_scale"):
        got[n] = g(n)
    f = lambda n: np.asarray(inputs["L0_ffn_" + n])
    for n in ("gate_w", "gate_b", "w1", "w2", "b2"):
        got[n] = f(n)
    got["b1"] = np.ascontiguousarray(f("b1").reshape(EXP, NF, P).transpose(0, 2, 1))
    got["ffn_gamma"], got["ffn_beta"] = f("gamma"), f("beta")
    srcp = np.concatenate([src, np.zeros(EPAD - E, np.int32)])
    ids = [np.concatenate([dst, np.full(EPAD - E, N, np.int32)])]
    for size in (G * P, P):
        ends = ids[-1].reshape(-1, P)[:, [0, P - 1]].reshape(-1)
        ids.append(np.concatenate([ends, np.full(size - len(ends), N, np.int32)]))
    near, win = [], []
    for v in ids:
        ext = np.concatenate([[-1], v, [-1]]).astype(np.int32)
        near.append(np.stack([ext[1:-1].reshape(-1, P).T, ext[:-2].reshape(-1, P).T, ext[2:].reshape(-1, P).T], 1))
        rows = np.stack([ext[t * P:t * P + P + 2] for t in range(len(v) // P)])
        rows = np.repeat(rows, H, 0)
        win.append(np.concatenate([rows, np.zeros((-len(rows) % P, P + 2), np.int32)]))
    got["near"] = np.ascontiguousarray(np.concatenate(near, 2))
    got["win"] = np.ascontiguousarray(np.concatenate(win))
    got["idx"] = np.ascontiguousarray(srcp.reshape(NG, G, P).transpose(0, 2, 1))
    return got


def kernel(**inputs):
    import concourse.bacc as bacc
    from concourse.bass_utils import run_bass_kernel_spmd
    nc = bacc.Bacc("TRN2", target_bir_lowering=False, num_devices=1)
    arrays = {"in_" + n: v for n, v in layouts(inputs).items()}
    args = {n[3:]: nc.dram_tensor(n, list(v.shape), mybir.dt.from_np(v.dtype), kind="ExternalInput").ap() for n, v in arrays.items()}
    out = nc.dram_tensor("out", [N, D], fp32, kind="ExternalOutput").ap()
    build(nc, args, out)
    r = run_bass_kernel_spmd(nc, [arrays], core_ids=[0])
    return r.results[0]["out"]
```

```python
import numpy as np
import concourse.bass as bass
from concourse import mybir
from contextlib import ExitStack

N = 6250
E = 100000
D = 256
H = 8
HD = D // H
EXP = 16
F = 512
P = 128
ND = D // P
NF = F // P
NT = -(-N // P)
NP = NT * P
G = 16
NG = -(-E // (P * G))
TE = NG * G
EPAD = TE * P
W = D + 2 * H
RW = W + 1
PART2 = NP
PART3 = PART2 + G * P
ROWS = PART3 + P
NOWHERE = 16384
SLOTS = TE + G + 1
assert 2 * TE <= G * P and 2 * G <= P and ROWS < NOWHERE and G * H == P
EPS = 1e-5
LOW = -1.0e30
QD = 4
RD = 8
CH = 7
NC = NT // CH
TS = 256
WD = 4
TX = -(-((2 * NP + EXP * (TS - 1)) // TS) // WD) * WD
assert NC * CH == NT and TX <= P and NF == 2 * ND == WD

fp32 = mybir.dt.float32
bf16 = mybir.dt.bfloat16
i32 = mybir.dt.int32
ALU = mybir.AluOpType
ACT = mybir.ActivationFunctionType
AX = mybir.AxisListType


def wait(eng, sem, value):
    if isinstance(value, int) and value <= 0:
        return
    eng.wait_ge(sem, value)


def wait_apart(eng, waits, passed, count):
    waits = [(s, v if isinstance(v, int) else eng.to_reg(v)) for s, v in waits if not (isinstance(v, int) and v <= 0)]
    eng.wait_ge(passed, count)
    for s, v in waits:
        eng.wait_ge(s, v)


def rounds(eng, body, first, last):
    g = first
    while g <= last and (g < 3 or g % 2 == 0):
        body(g // 2, g % 2)
        g += 1
    n = (last - g + 1) // 2
    if n > 0:
        k0 = (g - 1) // 2
        with eng.Fori(k0, k0 + n) as k:
            body(k, 1)
            body(k, 2)
        g += 2 * n
    while g <= last:
        body(g // 2, g % 2)
        g += 1


def build(nc, a, out):
    ctx0 = ExitStack()
    with ctx0:
        taken = []

        def sem(name):
            taken.append(nc.alloc_semaphore(name))
            return taken[-1]

        def free():
            nc.all_engine_barrier()
            nc.clear_and_free_semaphores(taken)
            nc.all_engine_barrier()
            taken.clear()

        def keep(name, shape, dt):
            return ctx0.enter_context(nc.sbuf_tensor(name, shape, dt))

        kv_tab = nc.dram_tensor("kv_tab", [NP, 2 * D], fp32, kind="Internal").ap()
        q_seg = nc.dram_tensor("q_seg", [NP + P, D], fp32, kind="Internal").ap()
        xbo_d = nc.dram_tensor("xbo_d", [NP, D], fp32, kind="Internal").ap()
        tab = nc.dram_tensor("tab", [ROWS, W], fp32, kind="Internal").ap()
        xs = nc.dram_tensor("slot_in", [TX * TS, D], fp32, kind="Internal").ap()
        ys = nc.dram_tensor("slot_out", [TX * TS, D], fp32, kind="Internal").ap()

        ident = keep("ident", [P, P], fp32)
        ones = keep("ones", [P, P], fp32)
        iota_row = keep("iota_row", [P, P], fp32)
        rank = keep("rank", [P, SLOTS], fp32)
        lastf = keep("lastf", [P, SLOTS], fp32)
        target = keep("target", [P, SLOTS], fp32)

        base = keep("base", [1, TE], i32)
        nodes_stage(nc, sem, a, kv_tab, q_seg, xbo_d, tab, ident, ones, iota_row, rank, lastf, target, base)
        free()
        edges_stage(nc, sem, a, kv_tab, q_seg, tab, ident, iota_row, rank, lastf, target, base)
        free()
        merge_stage(nc, sem, a, tab, ident, iota_row, rank, lastf, target)
        O = keep("O", [P, NT, D], fp32)
        XN = keep("XN", [P, NT, D], fp32)
        st = keep("row_stats", [P, NT, 6], fp32)
        mv = keep("row_meanvar", [P, NT, 2], fp32)
        rstd = keep("row_rstd", [P, NT], fp32)
        prob2 = keep("prob2", [P, 2, NT], fp32)
        L = keep("logits", [P, NT, EXP], fp32)
        slots = keep("slots", [P, 2 * NT], i32)
        experts = keep("experts", [P, TX], i32)
        update_stage(nc, sem, a, tab, xbo_d, xs, ident, ones, O, XN, st, mv, rstd, L)
        route_stage(nc, sem, L, prob2, slots, experts)
        free()
        experts_stage(nc, sem, a, xs, ys, ident, XN, slots, experts)
        result_stage(nc, sem, a, ys, out, O, XN, prob2, slots, st, mv)


def nodes_stage(nc, sem, a, kv_tab, q_seg, xbo_d, tab, ident, ones, iota_row, rank, lastf, target, base):
    with ExitStack() as ctx:
        def sb(name, shape, dt):
            return ctx.enter_context(nc.sbuf_tensor(name, shape, dt))

        def ps(name):
            return ctx.enter_context(nc.psum_tensor(name, [P, 512], fp32))

        wkv = sb("wkv", [P, ND, 2 * D], fp32)
        wq = sb("wq", [P, ND, D], fp32)
        bo = sb("bo", [P, D], fp32)
        neutral = sb("neutral", [P, W], fp32)
        neutral2 = sb("neutral2", [P, W], fp32)
        near = sb("near", [P, 3, SLOTS], i32)
        cur = sb("cur", [P, SLOTS], fp32)
        start = sb("start", [P, SLOTS], bf16)
        slot = sb("slot", [P, SLOTS], fp32)
        sloti = sb("sloti", [P, SLOTS], i32)
        tmp = sb("tmp", [P, SLOTS], fp32)
        iotai = sb("iotai", [P, P], i32)
        iota16 = sb("iota16", [P, P], bf16)
        tri = sb("tri", [P, P], bf16)
        below = sb("below", [P, P], bf16)
        all1 = sb("all1", [P, P], bf16)
        onerow = sb("onerow", [P, TE], fp32)
        at127 = sb("at127", [P, 1], fp32)
        digi = sb("digit_i", [P, 2, TE], i32)
        digit = sb("digit", [P, 2, TE], bf16)
        ohlo = sb("onehot_lo", [P, 2, G, P], bf16)
        ohhi = sb("onehot_hi", [P, 2, G, NT], bf16)
        has = sb("has_edges", [P, NT], fp32)
        has16 = sb("has_edges16", [P, NT], bf16)
        ordf = sb("ordinal_f", [P, NT], fp32)
        ordx = sb("ordinal_x", [P, NT], fp32)
        ordt = sb("ordinal_total", [P, NT], fp32)
        ordi = sb("ordinal", [P, NT], i32)
        X = sb("x_all", [P, NT, D], fp32)
        st = sb("st", [P, NT, 6], fp32)
        mv = sb("mv", [P, NT, 2], fp32)
        eps = sb("eps", [P, NT], fp32)
        rstd = sb("rstd", [P, NT], fp32)
        shift = sb("x_shift", [P, NT], fp32)
        xn = sb("xn", [P, 2, D], fp32)
        xbo = sb("xbo", [P, 2, D], fp32)
        xnT = sb("xnT", [P, 2, ND, P], fp32)
        kv = sb("kv_o", [P, 2, 2 * D], fp32)
        Q = sb("q_all", [P, NT, D], fp32)
        psT = [ps("psT0"), ps("psT1")]
        psKV = [ps("psKV0"), ps("psKV1")]
        psQ = [ps("psQ0"), ps("psQ1")]
        psC = ps("psC")
        psR = ps("psR")

        s_w = sem("weights_loaded")
        s_near = sem("near_loaded")
        s_const = sem("constants_made")
        s_pool = sem("pool_chain")
        s_neutral = sem("neutral_made")
        s_fill = sem("table_filled")
        s_start = sem("starts_ready")
        s_rank = sem("ranks_summed")
        s_rankc = sem("ranks_copied")
        s_prep = sem("prep_chain")
        s_dig = sem("digits_ready")
        s_x = [sem(f"x_loaded{c}") for c in range(NC)]
        s_eps = sem("variance_ready")
        s_std = sem("deviation_ready")
        s_shift = sem("shift_ready")
        s_xn = sem("xn_done")
        s_xbo = sem("xbo_done")
        s_xT = sem("xT_done")
        s_xTc = sem("xT_copied")
        s_kv = sem("kv_done")
        s_kvc = sem("kv_copied")
        s_q = sem("q_done")
        s_qc = sem("q_copied")
        s_lo = sem("onehot_lo_done")
        s_hi = sem("onehot_hi_done")
        s_cnt = sem("edges_counted")
        s_has = sem("has_edges_ready")
        s_ord = sem("ordinals_ready")
        s_oin = sem("ordinal_within_summed")
        s_oinc = sem("ordinal_within_copied")
        s_otot = sem("ordinal_totals_summed")
        s_qs = sem("q_scattered")
        s_out = [sem("node_rows_stored0"), sem("node_rows_stored1")]

        x_c = a["x"].rearrange("(c t p) f -> c p t f", p=P, t=CH)
        kv_t = kv_tab.rearrange("(t p) f -> t p f", p=P)
        xbo_t = xbo_d.rearrange("(t p) f -> t p f", p=P)
        q_t = q_seg.rearrange("(t p) f -> t p f", p=P)
        tab_t = tab[0:NP, :].rearrange("(t p) f -> t p f", p=P)
        Q2 = Q[:, :, :].rearrange("p t f -> p (t f)")
        X2 = X[:, :, :].rearrange("p t f -> p (t f)")

        with nc.Block() as block:

            @block.sync
            def _(sp):
                sp.dma_start(near[:, :, :], a["near"]).then_inc(s_near, 16)
                for c in range(NC):
                    sp.dma_start(X[:, c * CH:(c + 1) * CH, :], x_c[c]).then_inc(s_x[c], 16)
                sp.dma_start(wkv[:, :, :], a["wkvT"].rearrange("(c p) n -> p c n", p=P)).then_inc(s_w, 16)
                sp.dma_start(wq[:, :, :], a["wqT"].rearrange("(c p) n -> p c n", p=P)).then_inc(s_w, 16)
                sp.dma_start(bo[:, :], a["bo"].partition_broadcast(P)).then_inc(s_w, 16)
                sp.wait_ge(s_neutral, 2)
                sp.dma_start(q_seg[NP:NP + P, :], neutral[:, 0:D]).then_inc(s_fill, 16)
                dest = tab[NP:ROWS, :].rearrange("(t p) f -> p t f", p=P)
                sp.dma_start(dest, neutral2[:, :].unsqueeze(1).to_broadcast([P, dest.shape[1], W])).then_inc(s_fill, 16)

                def store(k, c):
                    i, b = 2 * k + c, c % 2
                    wait(sp, s_kvc, i + 1)
                    sp.dma_start(kv_t[i], kv[:, b, :]).then_inc(s_out[b], 16)
                    wait(sp, s_xbo, i + 1)
                    sp.dma_start(xbo_t[i], xbo[:, b, :]).then_inc(s_out[b], 16)
                    sp.dma_start(q_t[i], neutral[:, 0:D]).then_inc(s_fill, 16)
                    sp.dma_start(tab_t[i], neutral[:, :]).then_inc(s_fill, 16)

                rounds(sp, store, 0, NT - 1)
                sp.wait_ge(s_fill, 32 * (NT + 1))
                sp.wait_ge(s_out[0], 32 * ((NT + 1) // 2))
                sp.wait_ge(s_out[1], 32 * (NT // 2))

            @block.gpsimd
            def _(pool):
                pool.memset(neutral[:, :], 0.0).then_inc(s_neutral, 1)
                pool.memset(neutral2[:, 0:D + H], 0.0).then_inc(s_pool, 1)
                pool.memset(neutral2[:, D + H:W], LOW).then_inc(s_neutral, 1)
                pool.memset(ident[:, :], 0.0).then_inc(s_pool, 1)
                pool.memset(ones[:, :], 1.0).then_inc(s_pool, 1)
                pool.iota(iotai[:, :], [[1, P]], base=0, channel_multiplier=0).then_inc(s_pool, 1)
                pool.memset(tri[:, :], 1.0).then_inc(s_pool, 1)
                pool.memset(below[:, :], 1.0).then_inc(s_pool, 1)
                pool.memset(all1[:, :], 1.0).then_inc(s_pool, 1)
                pool.memset(onerow[:, :], 1.0).then_inc(s_pool, 1)
                pool.memset(at127[:, :], 0.0).then_inc(s_pool, 1)
                pool.iota(sloti[:, 0:TE], [[2, TE]], base=PART2, channel_multiplier=0).then_inc(s_pool, 1)
                pool.iota(sloti[:, TE:SLOTS], [[2, G + 1]], base=PART3, channel_multiplier=0).then_inc(s_pool, 1)
                pool.wait_ge(s_pool, 11)
                pool.affine_select(out=ident[:, :], in_=ident[:, :], compare_op=ALU.not_equal, fill=1.0,
                                   base=0, pattern=[[-1, P]], channel_multiplier=1).then_inc(s_const, 1)
                pool.affine_select(out=below[:, :], in_=below[:, :], compare_op=ALU.is_gt, fill=0.0,
                                   base=0, pattern=[[1, P]], channel_multiplier=-1).then_inc(s_const, 1)
                pool.affine_select(out=tri[:, :], in_=tri[:, :], compare_op=ALU.is_ge, fill=0.0,
                                   base=0, pattern=[[1, P]], channel_multiplier=-1).then_inc(s_pool, 1)
                pool.wait_ge(s_pool, 12)
                pool.affine_select(out=tri[:, :], in_=tri[:, :], compare_op=ALU.is_gt, fill=0.0,
                                   base=0, pattern=[[0, P]], channel_multiplier=1).then_inc(s_const, 1)
                pool.affine_select(out=at127[:, :], in_=at127[:, :], compare_op=ALU.not_equal, fill=1.0,
                                   base=-(P - 1), pattern=[[0, 1]], channel_multiplier=1).then_inc(s_const, 1)
                pool.wait_ge(s_w, 48)

                def tile(k, c):
                    i, b = 2 * k + c, c % 2
                    wait(pool, s_xn, i + 1)
                    wait(pool, s_out[b], 32 * (k + c // 2))
                    nc.gpsimd.tensor_tensor(xbo[:, b, :], xn[:, b, :], bo[:, :], ALU.add).then_inc(s_xbo, 1)

                rounds(pool, tile, 0, NT - 1)
                pool.wait_ge(s_fill, 32 * (NT + 1))
                pool.wait_ge(s_ord, 1)
                pool.wait_ge(s_qc, NT)
                for t in range(NT):
                    pool.indirect_dma_start(
                        out=q_seg, out_offset=bass.IndirectOffsetOnAxis(ap=ordi[:, t:t + 1], axis=0),
                        in_=Q[:, t, :], in_offset=None, bounds_check=NP + P - 1, oob_is_err=False).then_inc(s_qs, 16)
                pool.wait_ge(s_qs, 16 * NT)

            @block.vector
            def _(dve):
                chain = [0]

                def link(ins):
                    chain[0] += 1
                    ins.then_inc(s_prep, 1)
                    dve.wait_ge(s_prep, chain[0])

                V = nc.vector
                dve.wait_ge(s_const, 4)
                dve.wait_ge(s_near, 16)
                V.tensor_copy(iota_row[:, :], iotai[:, :])
                V.tensor_copy(iota16[:, :], iotai[:, :])
                V.tensor_copy(cur[:, :], near[:, 0, :])
                V.tensor_copy(slot[:, :], sloti[:, :])
                V.tensor_tensor(start[:, :], near[:, 0, :], near[:, 1, :], ALU.not_equal).then_inc(s_start, 1)
                V.tensor_scalar(digi[:, 0, :], near[:, 0, 0:TE], P - 1, None, ALU.bitwise_and)
                V.tensor_scalar(digi[:, 1, :], near[:, 0, 0:TE], P.bit_length() - 1, None, ALU.arith_shift_right)
                link(V.tensor_tensor(lastf[:, :], near[:, 0, :], near[:, 2, :], ALU.not_equal))
                V.tensor_copy(digit[:, :, :], digi[:, :, :]).then_inc(s_dig, 1)
                link(V.tensor_scalar(lastf[:, :], lastf[:, :], at127[:, 0:1], None, ALU.max))
                for h in range(2):
                    lo, hi = h * 512, min(SLOTS, (h + 1) * 512)
                    dve.wait_ge(s_rank, h + 1)
                    last = V.tensor_copy(rank[:, lo:hi], psR[:, 0:hi - lo])
                    last.then_inc(s_rankc, 1)
                for h in range(2):
                    lo, hi = h * 512, min(TE, (h + 1) * 512)
                    dve.wait_ge(s_rank, h + 3)
                    last = V.tensor_copy(tmp[:, lo:hi], psR[:, 0:hi - lo])
                    last.then_inc(s_rankc, 1)
                for c in range(NC):
                    dve.wait_ge(s_x[c], 16)
                    for t in range(CH * c, CH * (c + 1)):
                        last = V.bn_stats(st[:, t, :], X[:, t, :])
                    link(last)
                    for t in range(CH * c, CH * (c + 1)):
                        last = V.bn_aggr(mv[:, t, :], st[:, t, :])
                    link(last)
                V.tensor_scalar(eps[:, :], mv[:, :, 1], EPS, None, ALU.add).then_inc(s_eps, 1)
                dve.wait_ge(s_std, 1)
                link(V.reciprocal(rstd[:, :], eps[:, :]))

                def tile(k, c):
                    i, b = 2 * k + c, c % 2
                    wait(dve, s_cnt, i - 1)
                    V.tensor_tensor(ohlo[:, b, :, :], digit[:, 0, span(i, G)].unsqueeze(2).to_broadcast([P, G, P]),
                                    iota16[:, :].unsqueeze(1).to_broadcast([P, G, P]), ALU.is_equal).then_inc(s_lo, 1)
                    V.tensor_tensor(ohhi[:, b, :, :], digit[:, 1, span(i, G)].unsqueeze(2).to_broadcast([P, G, NT]),
                                    iota16[:, 0:NT].unsqueeze(1).to_broadcast([P, G, NT]), ALU.is_equal).then_inc(s_hi, 1)

                link(V.tensor_tensor(shift[:, :], mv[:, :, 0], rstd[:, :], ALU.mult))
                V.tensor_scalar(shift[:, :], shift[:, :], -1.0, None, ALU.mult).then_inc(s_shift, 1)
                rounds(dve, tile, 0, NT - 1)
                dve.wait_ge(s_cnt, NT)
                link(V.tensor_scalar(has[:, :], psC[:, 0:NT], 0.0, None, ALU.is_gt))
                V.tensor_copy(has16[:, :], has[:, :]).then_inc(s_has, 1)
                dve.wait_ge(s_oin, 1)
                V.tensor_copy(ordf[:, :], psR[:, 0:NT]).then_inc(s_oinc, 1)
                dve.wait_ge(s_otot, 1)
                link(V.tensor_copy(ordt[:, :], psR[:, 0:NT]))
                link(V.tensor_tensor_scan(ordx[:, :], ones[:, 0:NT], ordt[:, :], 0.0, ALU.mult, ALU.add))
                link(V.tensor_tensor(ordx[:, :], ordx[:, :], ordt[:, :], ALU.subtract))
                link(V.tensor_tensor(ordf[:, :], ordf[:, :], ordx[:, :], ALU.add))
                link(V.tensor_scalar(has[:, :], has[:, :], float(-NOWHERE), float(NOWHERE), ALU.mult, ALU.add))
                link(V.tensor_tensor(ordf[:, :], ordf[:, :], has[:, :], ALU.add))
                V.tensor_copy(ordi[:, :], ordf[:, :]).then_inc(s_ord, 1)
                dve.wait_ge(s_rankc, 4)
                link(V.tensor_tensor_scan(onerow[:, :], onerow[:, :], tmp[:, 0:TE], 0.0, ALU.mult, ALU.add))
                link(V.tensor_tensor(tmp[:, 0:TE], onerow[:, :], tmp[:, 0:TE], ALU.subtract))
                link(V.tensor_tensor(tmp[:, 0:TE], tmp[:, 0:TE], start[:, 0:TE], ALU.add))
                link(V.tensor_scalar(base[0:1, :], tmp[0:1, 0:TE], -1.0, None, ALU.add))
                PT = slice(0, TE + G)
                link(V.tensor_tensor(tmp[:, PT], slot[:, PT], cur[:, PT], ALU.subtract))
                link(V.tensor_scalar(tmp[:, PT], tmp[:, PT], 1.0, at127[:, 0:1], ALU.add, ALU.mult))
                link(V.tensor_tensor(target[:, PT], cur[:, PT], tmp[:, PT], ALU.add))
                link(V.tensor_tensor(slot[:, PT], slot[:, PT], target[:, PT], ALU.subtract))
                link(V.tensor_scalar(tmp[:, PT], rank[:, PT], 0.0, None, ALU.is_equal))
                link(V.tensor_tensor(tmp[:, PT], tmp[:, PT], slot[:, PT], ALU.mult))
                link(V.tensor_tensor(target[:, PT], target[:, PT], tmp[:, PT], ALU.add))
                link(V.tensor_copy(target[:, TE + G:SLOTS], cur[:, TE + G:SLOTS]))
                link(V.tensor_scalar(target[:, :], target[:, :], float(-NOWHERE), None, ALU.add))
                link(V.tensor_tensor(target[:, :], target[:, :], lastf[:, :], ALU.mult))

            @block.tensor
            def _(pe):
                pe.wait_ge(s_const, 4)
                pe.wait_ge(s_start, 1)
                for h in range(4):
                    m, hi = (tri, SLOTS) if h < 2 else (all1, TE)
                    lo = h % 2 * 512
                    hi = min(hi, lo + 512)
                    wait(pe, s_rankc, h)
                    nc.tensor.matmul(psR[:, 0:hi - lo], m[:, :], start[:, lo:hi], start=True, stop=True).then_inc(s_rank, 1)
                pe.wait_ge(s_w, 48)

                def tile(k, c):
                    i, b = 2 * k + c, c % 2
                    wait(pe, s_xn, i + 1)
                    wait(pe, s_xTc, i - 1)
                    for f in range(ND):
                        mm = nc.tensor.transpose(psT[b][:, f * P:(f + 1) * P], xn[:, b, f * P:(f + 1) * P], ident[:, :])
                    mm.then_inc(s_xT, 1)

                def count(k, c):
                    i, b = 2 * k + c, c % 2
                    wait(pe, s_lo, i + 1)
                    wait(pe, s_hi, i + 1)
                    first, last = isinstance(i, int) and i == 0, isinstance(i, int) and i == NT - 1
                    for t in range(G):
                        mm = nc.tensor.matmul(psC[:, 0:NT], ohlo[:, b, t, :], ohhi[:, b, t, :],
                                              start=first and t == 0, stop=last and t == G - 1)
                    mm.then_inc(s_cnt, 1)

                def products(k, c):
                    i, b = 2 * k + c, c % 2
                    wait(pe, s_xTc, i + 1)
                    wait(pe, s_kvc, i - 1)
                    for f in range(ND):
                        mm = nc.tensor.matmul(psKV[b][:, :], xnT[:, b, f, :], wkv[:, f, :], start=f == 0, stop=f == ND - 1)
                    mm.then_inc(s_kv, 1)
                    wait(pe, s_qc, i - 1)
                    for f in range(ND):
                        mm = nc.tensor.matmul(psQ[b][:, 0:D], xnT[:, b, f, :], wq[:, f, :], start=f == 0, stop=f == ND - 1)
                    mm.then_inc(s_q, 1)

                def period(k, c, last=False):
                    if not last:
                        tile(k, c + 1)
                    count(k, c)
                    products(k, c)

                tile(0, 0)
                rounds(pe, period, 0, NT - 2)
                period(NT // 2, 0, last=True)
                pe.wait_ge(s_has, 1)
                nc.tensor.matmul(psR[:, 0:NT], below[:, :], has16[:, :], start=True, stop=True).then_inc(s_oin, 1)
                pe.wait_ge(s_oinc, 1)
                nc.tensor.matmul(psR[:, 0:NT], all1[:, :], has16[:, :], start=True, stop=True).then_inc(s_otot, 1)

            @block.scalar
            def _(act):
                act.wait_ge(s_eps, 1)
                nc.scalar.activation(eps[:, :], eps[:, :], ACT.Sqrt).then_inc(s_std, 1)

                def norm(k, c):
                    i, b = 2 * k + c, c % 2
                    wait(act, s_xT, i - 1)
                    wait(act, s_xbo, i - 1)
                    nc.scalar.activation(xn[:, b, :], X2[:, span(i)], ACT.Identity, scale=rstd[:, span(i, 1)],
                                         bias=shift[:, span(i, 1)]).then_inc(s_xn, 1)

                def columns(k, c):
                    i, b = 2 * k + c, c % 2
                    wait(act, s_xT, i + 1)
                    wait(act, s_q, i - 1)
                    nc.scalar.copy(xnT[:, b, :, :].rearrange("p c n -> p (c n)"), psT[b][:, 0:D]).then_inc(s_xTc, 1)

                def tile(k, c, ahead=2):
                    i, b = 2 * k + c, c % 2
                    if ahead > 0:
                        columns(k, c + 1)
                    if ahead > 1:
                        norm(k + 1, c)
                    wait(act, s_kv, i + 1)
                    wait(act, s_out[b], 32 * (k + c // 2))
                    nc.scalar.copy(kv[:, b, :], psKV[b][:, :]).then_inc(s_kvc, 1)
                    wait(act, s_q, i + 1)
                    nc.scalar.activation(Q2[:, span(i)], psQ[b][:, 0:D], ACT.Copy, scale=float(HD) ** -0.5).then_inc(s_qc, 1)

                act.wait_ge(s_shift, 1)
                norm(0, 0)
                norm(0, 1)
                columns(0, 0)
                rounds(act, tile, 0, NT - 3)
                tile(NT // 2 - 1, 1, ahead=1)
                tile(NT // 2, 0, ahead=0)


def edges_stage(nc, sem, a, kv_tab, q_seg, tab, ident, iota_row, rank, lastf, target, base):
    with ExitStack() as ctx:
        def sb(name, shape, dt):
            return ctx.enter_context(nc.sbuf_tensor(name, shape, dt))

        def ps(name):
            return ctx.enter_context(nc.psum_tensor(name, [P, 512], fp32))

        we = sb("we", [P, ND, D], fp32)
        AT = sb("attr_in", [P, 2, G, ND, P], fp32)
        KV = sb("kv_in", [P, 2, G, 2 * D], fp32)
        Q = sb("q_in", [P, QD, D], fp32)
        prod = sb("prod", [P, 2, D], fp32)
        idx = sb("idx_in", [P, 2, G], i32)
        win = sb("win_in", [P, 2, P + 2], i32)
        ohT = sb("onehotT", [P, 2, P], fp32)
        S = sb("scores", [P, 2, P], fp32)
        mask = sb("mask", [P, P + 1], fp32)
        fwd = sb("max_fwd", [P, P], fp32)
        bwd = sb("max_bwd", [P, P], fp32)
        mT = sb("maxT", [P, P], fp32)
        pT = sb("probT", [P, P], fp32)
        R = sb("rhs", [P, G, RW], fp32)
        OH = sb("onehot", [P, 2, G, P], fp32)
        ROW = sb("rows_out", [P, RD, W], fp32)
        TGT = sb("targets_out", [P, RD, 1], i32)
        psA = [ps("psA0"), ps("psA1")]
        psE = [ps("psE0"), ps("psE1")]
        psO = [ps("psO0"), ps("psO1")]
        psS, psB = ps("psS"), ps("psB")

        s_we = sem("we_loaded")
        s_attr = [sem("attr_loaded0"), sem("attr_loaded1")]
        s_idx = [sem("idx_loaded0"), sem("idx_loaded1")]
        s_win = [sem("win_loaded0"), sem("win_loaded1")]
        s_gat = [[sem(f"gathered{b}_{j}") for j in range(4)] for b in range(2)]
        s_ql = [sem(f"q_loaded{j}") for j in range(QD)]
        s_ohT = sem("onehot_transposed")
        s_ohTc = sem("onehotT_copied")
        s_e = sem("e_done")
        s_kve = sem("kve_done")
        s_prod = sem("prod_done")
        s_score = sem("score_done")
        s_ne = sem("change_found")
        s_mask = sem("mask_done")
        s_sT = sem("scores_transposed")
        s_fwd = sem("fwd_max_done")
        s_bwd = sem("bwd_max_done")
        s_mT = sem("max_done")
        s_dT = sem("diff_done")
        s_pT = sem("probs_done")
        s_back = sem("probs_back")
        s_prob = sem("probs_copied")
        s_lm = sem("max_copied")
        s_tc = sem("targets_copied")
        s_oh = sem("onehot_done")
        s_pve = sem("pve_done")
        s_agg = sem("agg_done")
        s_row = sem("row_copied")
        s_tgt = sem("target_copied")
        s_scat = [sem(f"scattered{j}") for j in range(RD)]

        attr_g = a["attrT"].rearrange("g p (t c e) -> g p t c e", c=ND, e=P)
        win_g = a["win"].rearrange("(g p) w -> g p w", p=P)
        BACKS = {6 + j: (2 * j, 2 * j + 1) for j in range(8)}
        SUMS = {8 + j: (2 * j, 2 * j + 1) for j in range(8)}

        with nc.Block() as block:

            @block.sync
            def _(sp):
                def load_attr(k, c, j):
                    g, b = 2 * k + c, c % 2
                    if j == 0:
                        wait(sp, s_e, G * (g - 1))
                    sp.dma_start(AT[:, b, 2 * j:2 * j + 2, :, :], attr_g[g][:, 2 * j:2 * j + 2, :, :]).then_inc(s_attr[b], 16)

                def load_idx(k, c):
                    b = c % 2
                    for j in range(4):
                        wait(sp, s_gat[b][j], 64 * (k + c // 2))
                    sp.dma_start(idx[:, b, :], a["idx"][2 * k + c]).then_inc(s_idx[b], 16)

                def load_win(k, c):
                    g, b = 2 * k + c, c % 2
                    wait(sp, s_ne, g - 1)
                    sp.dma_start(win[:, b, :], win_g[g]).then_inc(s_win[b], 16)

                def load_q(k, c, t):
                    n = G * (2 * k + c) + t
                    first = sp.value_load(base[0:1, span(n, 1)], min_val=0, max_val=NP)
                    wait(sp, s_e, n - QD + 1)
                    sp.dma_start(Q[:, t % QD, :], q_seg[bass.ds(first, P), :]).then_inc(s_ql[t % QD], 16)

                def period(k, c, more=2):
                    for t in range(QD):
                        load_q(k, c, t)
                    load_win(k, c)
                    for t in range(QD, G):
                        load_q(k, c, t)
                        if more > 0 and t < QD + G // 2:
                            load_attr(k, c + 1, t - QD)
                        if more > 1 and t == G - 3:
                            load_idx(k + 1, c)

                sp.dma_start(we[:, :, :], a["weT"].rearrange("(c p) n -> p c n", p=P)).then_inc(s_we, 16)
                load_idx(0, 0)
                load_idx(0, 1)
                for j in range(G // 2):
                    load_attr(0, 0, j)
                rounds(sp, period, 0, NG - 3)
                period((NG - 2) // 2, (NG - 2) % 2, 1)
                period((NG - 1) // 2, (NG - 1) % 2, 0)

            @block.gpsimd
            def _(pool):
                def gather(k, c, t):
                    b = c % 2
                    ready = [(s_idx[b], 16 * (k + c // 2 + 1))] if t == 0 else []
                    wait_apart(pool, ready + [(s_pve, G * (2 * k + c - 2) + t + 1)], s_idx[b], 16)
                    pool.indirect_dma_start(
                        out=KV[:, b, t, :], out_offset=None, in_=kv_tab,
                        in_offset=bass.IndirectOffsetOnAxis(ap=idx[:, b, t:t + 1], axis=0)).then_inc(s_gat[b][t // 4], 16)

                def scatter(k, c, t):
                    n = G * (2 * k + c) + t
                    wait_apart(pool, [(s_row, n + 1), (s_tgt, n + 1)], s_idx[0], 16)
                    pool.indirect_dma_start(
                        out=tab, out_offset=bass.IndirectOffsetOnAxis(ap=TGT[:, t % RD, :], axis=0),
                        in_=ROW[:, t % RD, :], in_offset=None,
                        bounds_check=ROWS - 1, oob_is_err=False).then_inc(s_scat[t % RD], 16)

                def period(k, c):
                    for t in range(G):
                        gather(k + 1, c, t)
                        if t:
                            scatter(k, c, t - 1)
                    scatter(k, c, G - 1)

                for g in range(2):
                    for t in range(G):
                        gather(0, g, t)
                rounds(pool, period, 0, NG - 3)
                for g in (NG - 2, NG - 1):
                    for t in range(G):
                        scatter(g // 2, g % 2, t)
                for j in range(RD):
                    pool.wait_ge(s_scat[j], 16 * (TE // RD))

            @block.vector
            def _(dve):
                def onehot(k, c, t):
                    n, b = G * (2 * k + c) + t, c % 2
                    wait(dve, s_agg, n - 2 * G + 1)
                    nc.vector.tensor_scalar(OH[:, b, t, :], iota_row[:, :], rank[:, span(n, 1)], None,
                                            ALU.is_equal).then_inc(s_oh, 1)

                def front_sum(k, c, t):
                    n, b = G * (2 * k + c) + t, c % 2
                    if t % 4 == 0:
                        wait(dve, s_gat[b][t // 4], 64 * (k + c // 2 + 1))
                    wait(dve, s_e, n + 1)
                    e2 = psE[t % 2][:, 0:D].unsqueeze(1).to_broadcast([P, 2, D])
                    kv2 = KV[:, b, t, :].rearrange("p (a f) -> p a f", a=2)
                    nc.vector.tensor_tensor(kv2, kv2, e2, ALU.add).then_inc(s_kve, 1)

                def front_product(k, c, t):
                    n, b = G * (2 * k + c) + t, c % 2
                    wait(dve, s_kve, n + 1)
                    nc.vector.tensor_tensor(prod[:, t % 2, :], KV[:, b, t, 0:D], psE[t % 2][:, D:2 * D], ALU.mult).then_inc(s_prod, 1)

                def front_score(k, c, t):
                    n, b = G * (2 * k + c) + t, c % 2
                    wait(dve, s_prod, n + 1)
                    nc.vector.tensor_reduce(S[:, b, t * H:(t + 1) * H], prod[:, t % 2, :].rearrange("p (h d) -> p h d", h=H),
                                            AX.X, ALU.add).then_inc(s_score, 1)

                def masks(k, c):
                    g, b = 2 * k + c, c % 2
                    wait(dve, s_win[b], 16 * (k + c // 2 + 1))
                    wait(dve, s_mT, g)
                    nc.vector.tensor_tensor(mask[:, :], win[:, b, 0:P + 1], win[:, b, 1:P + 2], ALU.not_equal).then_inc(s_ne, 1)
                    wait(dve, s_ne, g + 1)
                    nc.vector.tensor_scalar(mask[:, :], mask[:, :], LOW, None, ALU.mult).then_inc(s_mask, 1)

                def scans(k, c):
                    g = 2 * k + c
                    wait(dve, s_mask, g + 1)
                    wait(dve, s_sT, g + 1)
                    wait(dve, s_pT, g)
                    nc.vector.tensor_tensor_scan(fwd[:, :], mask[:, 0:P], psS[:, 0:P], LOW, ALU.add, ALU.max).then_inc(s_fwd, 1)
                    nc.vector.tensor_tensor_scan(bwd[:, ::-1], mask[:, P:0:-1], psS[:, P - 1::-1], LOW,
                                                 ALU.add, ALU.max).then_inc(s_bwd, 1)

                def maxima(k, c):
                    g = 2 * k + c
                    wait(dve, s_bwd, g + 1)
                    wait(dve, s_fwd, g + 1)
                    wait(dve, s_back, g)
                    nc.vector.tensor_tensor(mT[:, :], fwd[:, :], bwd[:, :], ALU.max).then_inc(s_mT, 1)

                def differences(k, c):
                    g = 2 * k + c
                    wait(dve, s_mT, g + 1)
                    nc.vector.tensor_tensor(fwd[:, :], psS[:, 0:P], mT[:, :], ALU.subtract).then_inc(s_dT, 1)

                def small(k, c):
                    g = 2 * k + c
                    cols = bass.ds(G * g, G)
                    wait(dve, s_back, g + 1)
                    wait(dve, s_agg, G * g)
                    nc.vector.tensor_copy(R[:, :, D:D + H], psB[:, 0:P].rearrange("p (t h) -> p t h", h=H)).then_inc(s_prob, 1)
                    nc.vector.tensor_tensor(R[:, :, D + H:W], psB[:, P:2 * P].rearrange("p (t h) -> p t h", h=H),
                                            lastf[:, cols].unsqueeze(2).to_broadcast([P, G, H]), ALU.mult).then_inc(s_lm, 1)
                    nc.vector.tensor_copy(R[:, :, W:RW], target[:, cols].unsqueeze(2)).then_inc(s_tc, 1)

                def back(k, c, t):
                    n, b = G * (2 * k + c) + t, c % 2
                    if t == 0:
                        wait(dve, s_prob, 2 * k + c + 1)
                    nc.vector.tensor_tensor(
                        R[:, t, 0:D].rearrange("p (h d) -> p h d", h=H),
                        KV[:, b, t, D:2 * D].rearrange("p (h d) -> p h d", h=H),
                        R[:, t, D:D + H].unsqueeze(2).to_broadcast([P, H, HD]), ALU.mult).then_inc(s_pve, 1)

                def period(k, c, do_front=True, do_back=True, last=False):
                    for t in range(G):
                        backs = BACKS.get(t, ()) if do_back else ()
                        if do_back and t == 3:
                            scans(*prev(k, c))
                        if do_back and t == 6:
                            small(*prev(k, c))
                        if do_front:
                            front_sum(k, c, t)
                        if do_front and t + 3 < G:
                            onehot(k, c, t + 3)
                        elif do_front and not last:
                            onehot(k, c + 1, t + 3 - G)
                        if do_back and t == 3:
                            maxima(*prev(k, c))
                        for j in backs[1:]:
                            back(*prev(k, c), j - 1)
                        if do_front:
                            front_product(k, c, t)
                        if do_back and t == 3:
                            differences(*prev(k, c))
                        for j in backs[1:]:
                            back(*prev(k, c), j)
                        if do_front and t == G - 2:
                            masks(k, c)
                        if do_front:
                            front_score(k, c, t)

                onehot(0, 0, 0)
                onehot(0, 0, 1)
                onehot(0, 0, 2)
                period(0, 0, True, False)
                rounds(dve, period, 1, NG - 2)
                period((NG - 1) // 2, (NG - 1) % 2, last=True)
                period(NG // 2, NG % 2, False, True)

            @block.tensor
            def _(pe):
                def front_in(k, c, t):
                    n, b = G * (2 * k + c) + t, c % 2
                    wait(pe, s_ohTc, n - 1)
                    wait(pe, s_oh, n + 1)
                    nc.tensor.transpose(psA[t % 2][:, 0:P], OH[:, b, t, :], ident[:, :]).then_inc(s_ohT, 1)

                def front_out(k, c, t):
                    n, b = G * (2 * k + c) + t, c % 2
                    if t == 0:
                        wait(pe, s_attr[b], 16 * (G // 2) * (k + c // 2 + 1))
                    wait(pe, s_prod, n - 1)
                    for f in range(ND):
                        mm = nc.tensor.matmul(psE[t % 2][:, 0:D], AT[:, b, t, f, :], we[:, f, :], start=f == 0, stop=f == ND - 1)
                    wait(pe, s_ohTc, n + 1)
                    wait(pe, s_ql[t % QD], 16 * (G // QD * (2 * k + c) + t // QD + 1))
                    nc.tensor.matmul(psE[t % 2][:, D:2 * D], ohT[:, t % 2, :], Q[:, t % QD, :], start=True, stop=True).then_inc(s_e, 1)

                def agg(k, c, t):
                    n = G * (2 * k + c) + t
                    b = c % 2
                    if t == 0:
                        wait(pe, s_lm, 2 * k + c + 1)
                        wait(pe, s_tc, 2 * k + c + 1)
                    wait(pe, s_pve, n + 1)
                    wait(pe, s_row, n - 1)
                    wait(pe, s_tgt, n - 1)
                    nc.tensor.matmul(psO[t % 2][:, 0:RW], OH[:, b, t, :], R[:, t, :], start=True, stop=True).then_inc(s_agg, 1)

                def period(k, c, do_front=True, do_back=True, last=False):
                    for t in range(G):
                        if do_front and t + 1 < G:
                            front_in(k, c, t + 1)
                        elif do_front and not last:
                            front_in(k, c + 1, 0)
                        if do_back:
                            kk, cc = prev(k, c)
                            g = 2 * kk + cc
                            if t == 2:
                                wait(pe, s_score, G * (g + 1))
                                wait(pe, s_dT, g)
                                nc.tensor.transpose(psS[:, 0:P], S[:, cc % 2, :], ident[:, :]).then_inc(s_sT, 1)
                            if t == 5:
                                wait(pe, s_pT, g + 1)
                                wait(pe, s_mT, g + 1)
                                wait(pe, s_lm, g)
                                nc.tensor.transpose(psB[:, 0:P], pT[:, :], ident[:, :])
                                nc.tensor.transpose(psB[:, P:2 * P], mT[:, :], ident[:, :]).then_inc(s_back, 1)
                            for j in SUMS.get(t, ()):
                                agg(kk, cc, j)
                        if do_front:
                            front_out(k, c, t)

                pe.wait_ge(s_we, 16)
                front_in(0, 0, 0)
                period(0, 0, True, False)
                rounds(pe, period, 1, NG - 2)
                period((NG - 1) // 2, (NG - 1) % 2, last=True)
                period(NG // 2, NG % 2, False, True)

            @block.scalar
            def _(act):
                def front(k, c, t):
                    n = G * (2 * k + c) + t
                    wait(act, s_ohT, n + 1)
                    wait(act, s_e, n - 1)
                    nc.scalar.copy(ohT[:, t % 2, :], psA[t % 2][:, 0:P]).then_inc(s_ohTc, 1)

                def back(k, c, t):
                    n = G * (2 * k + c) + t
                    wait(act, s_agg, n + 1)
                    wait(act, s_scat[t % RD], 16 * (G // RD * (2 * k + c) + t // RD))
                    nc.scalar.copy(ROW[:, t % RD, :], psO[t % 2][:, 0:W]).then_inc(s_row, 1)
                    nc.scalar.activation(TGT[:, t % RD, :], psO[t % 2][:, W:RW], ACT.Copy, bias=float(NOWHERE)).then_inc(s_tgt, 1)

                def period(k, c, do_front=True, do_back=True, last=False):
                    for t in range(G):
                        if do_front and t + 1 < G:
                            front(k, c, t + 1)
                        elif do_front and not last:
                            front(k, c + 1, 0)
                        if do_back:
                            kk, cc = prev(k, c)
                            g = 2 * kk + cc
                            if t == 4:
                                wait(act, s_dT, g + 1)
                                wait(act, s_back, g)
                                nc.scalar.activation(pT[:, :], fwd[:, :], ACT.Exp).then_inc(s_pT, 1)
                            for j in SUMS.get(t, ()):
                                back(kk, cc, j)

                front(0, 0, 0)
                period(0, 0, True, False)
                rounds(act, period, 1, NG - 2)
                period((NG - 1) // 2, (NG - 1) % 2, last=True)
                period(NG // 2, NG % 2, False, True)


def one(i):
    return slice(i, i + 1) if isinstance(i, int) else bass.ds(i, 1)


def span(i, width=D):
    return slice(i * width, (i + 1) * width) if isinstance(i, int) else bass.ds(i * width, width)


def prev(k, c):
    return (k, c - 1) if c > 0 else (k - 1, 1)


def merge_stage(nc, sem, a, tab, ident, iota_row, rank, lastf, target):
    with ExitStack() as ctx:
        def sb(name, shape, dt):
            return ctx.enter_context(nc.sbuf_tensor(name, shape, dt))

        def ps(name):
            return ctx.enter_context(nc.psum_tensor(name, [P, 512], fp32))

        IN = sb("merge_in", [P, G, W], fp32)
        win = sb("merge_win", [P, P + 2], i32)
        S = sb("merge_scores", [P, P], fp32)
        mask = sb("merge_mask", [P, P + 1], fp32)
        fwd = sb("merge_fwd", [P, P], fp32)
        bwd = sb("merge_bwd", [P, P], fp32)
        mT = sb("merge_maxT", [P, P], fp32)
        pT = sb("merge_probT", [P, P], fp32)
        PR = sb("merge_prob", [P, G, H], fp32)
        R = sb("merge_rhs", [P, G, RW], fp32)
        OH = sb("merge_onehot", [P, G + 1, P], fp32)
        ROW = sb("merge_row", [P, G + 1, W], fp32)
        TGT = sb("merge_target", [P, G + 1, 1], i32)
        psS, psB, psO = ps("mpsS"), ps("mpsB"), [ps("mpsO0"), ps("mpsO1")]

        s_in = sem("merge_loaded")
        s_v = sem("merge_vector")
        s_t = sem("merge_tensor")
        s_a = sem("merge_scalar")
        s_o = sem("merge_scattered")
        LEVELS = (dict(tiles=G, first=PART2, col=TE, v=1, t=0, a=0, o=0),
                  dict(tiles=1, first=PART3, col=TE + G, v=1 + 11 + G, t=3 + G, a=1 + 2 * G, o=G))
        win_g = a["win"].rearrange("(g p) w -> g p w", p=P)

        with nc.Block() as block:

            @block.sync
            def _(sp):
                for n, lv in enumerate(LEVELS):
                    m = lv["tiles"]
                    wait(sp, s_o, 16 * lv["o"])
                    sp.dma_start(IN[:, 0:m, :], tab[lv["first"]:lv["first"] + m * P, :].rearrange("(t p) f -> p t f", p=P)).then_inc(s_in, 16)
                    sp.dma_start(win[:, :], win_g[NG + n]).then_inc(s_in, 16)

            @block.vector
            def _(dve):
                done = [0]

                def link(ins):
                    done[0] += 1
                    ins.then_inc(s_v, 1)
                    dve.wait_ge(s_v, done[0])

                for t in range(G + 1):
                    last = nc.vector.tensor_scalar(OH[:, t, :], iota_row[:, :], rank[:, TE + t:TE + t + 1], None, ALU.is_equal)
                link(last)
                for n, lv in enumerate(LEVELS):
                    m = lv["tiles"]
                    q = m * H
                    cols = slice(lv["col"], lv["col"] + m)
                    assert done[0] == lv["v"]
                    dve.wait_ge(s_in, 32 * (n + 1))
                    link(nc.vector.tensor_copy(S[:, 0:q].rearrange("p (t h) -> p t h", h=H), IN[:, 0:m, D + H:W]))
                    link(nc.vector.tensor_tensor(mask[:, :], win[:, 0:P + 1], win[:, 1:P + 2], ALU.not_equal))
                    link(nc.vector.tensor_scalar(mask[:, :], mask[:, :], LOW, None, ALU.mult))
                    dve.wait_ge(s_t, lv["t"] + 1)
                    link(nc.vector.tensor_tensor_scan(fwd[0:q, :], mask[0:q, 0:P], psS[0:q, 0:P], LOW, ALU.add, ALU.max))
                    link(nc.vector.tensor_tensor_scan(bwd[0:q, ::-1], mask[0:q, P:0:-1], psS[0:q, P - 1::-1], LOW, ALU.add, ALU.max))
                    link(nc.vector.tensor_tensor(mT[0:q, :], fwd[0:q, :], bwd[0:q, :], ALU.max))
                    link(nc.vector.tensor_tensor(fwd[0:q, :], psS[0:q, 0:P], mT[0:q, :], ALU.subtract))
                    dve.wait_ge(s_t, lv["t"] + 3)
                    link(nc.vector.tensor_copy(PR[:, 0:m, :], psB[:, 0:q].rearrange("p (t h) -> p t h", h=H)))
                    link(nc.vector.tensor_tensor(R[:, 0:m, D:D + H], PR[:, 0:m, :], IN[:, 0:m, D:D + H], ALU.mult))
                    link(nc.vector.tensor_tensor(R[:, 0:m, D + H:W], psB[:, P:P + q].rearrange("p (t h) -> p t h", h=H),
                                                 lastf[:, cols].unsqueeze(2).to_broadcast([P, m, H]), ALU.mult))
                    link(nc.vector.tensor_copy(R[:, 0:m, W:RW], target[:, cols].unsqueeze(2)))
                    for t in range(m):
                        done[0] += 1
                        nc.vector.tensor_tensor(
                            R[:, t, 0:D].rearrange("p (h d) -> p h d", h=H), IN[:, t, 0:D].rearrange("p (h d) -> p h d", h=H),
                            PR[:, t, :].unsqueeze(2).to_broadcast([P, H, HD]), ALU.mult).then_inc(s_v, 1)

            @block.tensor
            def _(pe):
                for n, lv in enumerate(LEVELS):
                    m = lv["tiles"]
                    q = m * H
                    pe.wait_ge(s_v, lv["v"] + 3)
                    nc.tensor.transpose(psS[0:q, 0:P], S[:, 0:q], ident[:, :]).then_inc(s_t, 1)
                    pe.wait_ge(s_a, lv["a"] + 1)
                    nc.tensor.transpose(psB[:, 0:q], pT[0:q, :], ident[0:q, 0:q]).then_inc(s_t, 1)
                    nc.tensor.transpose(psB[:, P:P + q], mT[0:q, :], ident[0:q, 0:q]).then_inc(s_t, 1)
                    for t in range(m):
                        pe.wait_ge(s_v, lv["v"] + 11 + t + 1)
                        if t >= 2:
                            pe.wait_ge(s_a, lv["a"] + 1 + 2 * (t - 1))
                        nc.tensor.matmul(psO[t % 2][:, 0:RW], OH[:, lv["o"] + t, :], R[:, t, :], start=True, stop=True).then_inc(s_t, 1)

            @block.scalar
            def _(act):
                for n, lv in enumerate(LEVELS):
                    m = lv["tiles"]
                    q = m * H
                    act.wait_ge(s_v, lv["v"] + 7)
                    nc.scalar.activation(pT[0:q, :], fwd[0:q, :], ACT.Exp).then_inc(s_a, 1)
                    for t in range(m):
                        act.wait_ge(s_t, lv["t"] + 3 + t + 1)
                        nc.scalar.copy(ROW[:, lv["o"] + t, :], psO[t % 2][:, 0:W]).then_inc(s_a, 1)
                        nc.scalar.activation(TGT[:, lv["o"] + t, :], psO[t % 2][:, W:RW], ACT.Copy, bias=float(NOWHERE)).then_inc(s_a, 1)

            @block.gpsimd
            def _(pool):
                for n, lv in enumerate(LEVELS):
                    for t in range(lv["tiles"]):
                        pool.wait_ge(s_a, lv["a"] + 1 + 2 * (t + 1))
                        pool.indirect_dma_start(
                            out=tab, out_offset=bass.IndirectOffsetOnAxis(ap=TGT[:, lv["o"] + t, :], axis=0),
                            in_=ROW[:, lv["o"] + t, :], in_offset=None, bounds_check=ROWS - 1, oob_is_err=False).then_inc(s_o, 16)
                pool.wait_ge(s_o, 16 * (G + 1))


def update_stage(nc, sem, a, tab, xbo_d, xs, ident, ones, O, XN, st, mv, rstd, L):
    with ExitStack() as ctx:
        def sb(name, shape, dt):
            return ctx.enter_context(nc.sbuf_tensor(name, shape, dt))

        def ps(name):
            return ctx.enter_context(nc.psum_tensor(name, [P, 512], fp32))

        wo = sb("wo", [P, ND, D], fp32)
        vec = sb("norm_vectors", [P, 3, D], fp32)
        zeros = sb("zeros", [P, D], fp32)
        row = sb("row_in", [P, 2, CH, W], fp32)
        xbo = sb("xbo_in", [P, 2, CH, D], fp32)
        zr = sb("inv_sum", [P, CH, H], fp32)
        agg = sb("agg", [P, 2, CH, D], fp32)
        aggT = sb("aggT", [P, 2, D], fp32)
        colsum = sb("column_sums", [P, D], fp32)
        shift = sb("shift", [P, D], fp32)
        gain = sb("gain", [P, D], fp32)
        var = sb("col_var", [P, D], fp32)
        sq = sb("squares", [P, 2, CH, D], fp32)
        xc = sb("x_chunk", [P, 2, CH, D], fp32)
        eps = sb("var_eps", [P, NT], fp32)
        psT = [ps("upsT0"), ps("upsT1")]
        psY = [ps("upsY0"), ps("upsY1")]
        wg = sb("gate_w", [P, ND, EXP], fp32)
        bg = sb("gate_b", [P, EXP], fp32)
        psM, psV = ps("psM"), ps("psV")
        psL = [ps("psL0"), ps("psL1")]
        LT = 512 // EXP

        s_w = sem("update_weights")
        s_zero = sem("zeros_made")
        s_slots = sem("slots_cleared")
        s_in = [sem("rows_loaded0"), sem("rows_loaded1")]
        s_xb = [sem("xbo_loaded0"), sem("xbo_loaded1")]
        s_den = sem("sum_guarded")
        s_inv = sem("sum_inverted")
        s_agg = sem("agg_scaled")
        s_aT = sem("agg_transposed")
        s_aTc = sem("aggT_copied")
        s_y = sem("projected")
        s_o = sem("out_rows_done")
        s_acc = sem("tiles_added")
        s_mean = sem("mean_summed")
        s_chain = sem("norm_chain")
        s_cent = sem("centred")
        s_sq = sem("squared")
        s_sum = sem("squares_summed")
        s_var = sem("variance_summed")
        s_veps = sem("variance_done")
        s_std = sem("deviation_done")
        s_gain = sem("gain_done")
        s_x = [sem("x_chunk_loaded0"), sem("x_chunk_loaded1")]
        s_pre = sem("pre_gelu_done")
        s_gelu = sem("gelu_done")
        s_x2 = sem("residual_done")
        s_eps2 = sem("row_variance_done")
        s_std2 = sem("row_deviation_done")
        s_xn = sem("rows_normed")
        s_gT = sem("gate_transposed")
        s_gTc = sem("gate_columns_copied")
        s_l = sem("logits_done")

        tab_c = tab[0:NP, :].rearrange("(c t p) f -> c p t f", p=P, t=CH)
        xbo_c = xbo_d.rearrange("(c t p) f -> c p t f", p=P, t=CH)
        xs_c = xs.rearrange("(c t p) f -> c p t f", p=P, t=TX * TS // P // (NC + 1))
        x_c = a["x"].rearrange("(c t p) f -> c p t f", p=P, t=CH)
        O2 = O[:, :, :].rearrange("p t f -> p (t f)")
        O_c = O[:, :, :].rearrange("p (c t) f -> p c t f", t=CH)
        XN_c = XN[:, :, :].rearrange("p (c t) f -> p c t f", t=CH)
        REAL = N - (NT - 1) * P

        def across(v):
            return v.unsqueeze(1).to_broadcast([P, CH, D])

        with nc.Block() as block:

            @block.sync
            def _(sp):
                sp.dma_start(wo[:, :, :], a["woT"].rearrange("(c p) n -> p c n", p=P)).then_inc(s_w, 16)
                for j, n in enumerate(("gamma", "beta", "mean_scale")):
                    sp.dma_start(vec[:, j, :], a[n].partition_broadcast(P)).then_inc(s_w, 16)
                sp.dma_start(wg[:, :, :], a["gate_w"].rearrange("(c p) n -> p c n", p=P)).then_inc(s_w, 16)
                sp.dma_start(bg[:, :], a["gate_b"].partition_broadcast(P)).then_inc(s_w, 16)

                def load(c):
                    wait(sp, s_agg, CH * (c - 1))
                    sp.dma_start(row[:, c % 2, :, :], tab_c[c]).then_inc(s_in[c % 2], 16)
                    wait(sp, s_o, CH * (c - 1))
                    sp.dma_start(xbo[:, c % 2, :, :], xbo_c[c]).then_inc(s_xb[c % 2], 16)

                for c in range(NC):
                    load(c)
                for c in range(NC):
                    if c >= 2:
                        sp.wait_ge(s_x2, c - 1)
                    sp.dma_start(xc[:, c % 2, :, :], x_c[c]).then_inc(s_x[c % 2], 16)

            @block.vector
            def _(dve):
                def invert(c):
                    dve.wait_ge(s_in[c % 2], 16 * (c // 2 + 1))
                    wait(dve, s_agg, CH * c)
                    nc.vector.tensor_scalar(zr[:, :, :], row[:, c % 2, :, D:D + H], 1e-30, None, ALU.max).then_inc(s_den, 1)
                    dve.wait_ge(s_den, c + 1)
                    nc.vector.reciprocal(zr[:, :, :], zr[:, :, :]).then_inc(s_inv, 1)
                    dve.wait_ge(s_inv, c + 1)
                    wait(dve, s_aT, CH * (c - 1))

                def scale(c, t):
                    nc.vector.tensor_tensor(
                        agg[:, c % 2, t, :].rearrange("p (h d) -> p h d", h=H), row[:, c % 2, t, 0:D].rearrange("p (h d) -> p h d", h=H),
                        zr[:, t, :].unsqueeze(2).to_broadcast([P, H, HD]), ALU.mult).then_inc(s_agg, 1)

                def finish(i):
                    if i % CH == 0:
                        dve.wait_ge(s_xb[i // CH % 2], 16 * (i // CH // 2 + 1))
                    dve.wait_ge(s_y, i + 1)
                    nc.vector.tensor_tensor(O[:, i, :], psY[i % 2][:, 0:D], xbo[:, i // CH % 2, i % CH, :], ALU.add).then_inc(s_o, 1)

                invert(0)
                for t in range(CH):
                    scale(0, t)
                for c in range(NC):
                    if c + 1 < NC:
                        invert(c + 1)
                    for t in range(CH):
                        finish(c * CH + t)
                        if c + 1 < NC:
                            scale(c + 1, t)

                chain = [0]

                def link(ins):
                    chain[0] += 1
                    ins.then_inc(s_chain, 1)
                    dve.wait_ge(s_chain, chain[0])

                dve.wait_ge(s_w, 96)
                dve.wait_ge(s_mean, 1)
                link(nc.vector.tensor_scalar(shift[:, :], psM[:, 0:D], 1.0 / N, None, ALU.mult))
                link(nc.vector.tensor_tensor(shift[:, :], shift[:, :], vec[:, 2, :], ALU.mult))
                for c in range(NC):
                    nc.vector.tensor_tensor(O_c[:, c], O_c[:, c], across(shift[:, :]), ALU.subtract).then_inc(s_cent, 1)
                dve.wait_ge(s_var, 1)
                nc.vector.tensor_scalar(var[:, :], psV[:, 0:D], 1.0 / N, EPS, ALU.mult, ALU.add).then_inc(s_veps, 1)
                dve.wait_ge(s_std, 1)
                link(nc.vector.reciprocal(gain[:, :], var[:, :]))
                link(nc.vector.tensor_tensor(gain[:, :], gain[:, :], vec[:, 0, :], ALU.mult))

                def pre_gelu(c):
                    dve.wait_ge(s_cent, NC)
                    link(nc.vector.tensor_tensor(O_c[:, c], O_c[:, c], across(gain[:, :]), ALU.mult))
                    if c >= 2:
                        dve.wait_ge(s_gelu, c - 1)
                    nc.vector.tensor_tensor(sq[:, c % 2, :, :], O_c[:, c], across(vec[:, 1, :]), ALU.add).then_inc(s_pre, 1)

                def stats(c):
                    dve.wait_ge(s_x2, c + 1)
                    for t in range(CH * c, CH * (c + 1)):
                        last = nc.vector.bn_stats(st[:, t, :], O[:, t, :])
                    link(last)
                    for t in range(CH * c, CH * (c + 1)):
                        last = nc.vector.bn_aggr(mv[:, t, :], st[:, t, :])
                    link(last)
                    cols = slice(CH * c, CH * (c + 1))
                    nc.vector.tensor_scalar(eps[:, cols], mv[:, cols, 1], EPS, None, ALU.add).then_inc(s_eps2, 1)

                def norm(c):
                    cols = slice(CH * c, CH * (c + 1))
                    dve.wait_ge(s_std2, c + 1)
                    link(nc.vector.reciprocal(rstd[:, cols], eps[:, cols]))
                    for t in range(CH * c, CH * (c + 1)):
                        nc.vector.tensor_scalar(XN[:, t, :], O[:, t, :], mv[:, t, 0:1], rstd[:, t:t + 1],
                                                ALU.subtract, ALU.mult).then_inc(s_xn, 1)

                pre_gelu(0)
                for c in range(NC + 1):
                    if c + 1 < NC:
                        pre_gelu(c + 1)
                    if c < NC:
                        stats(c)
                    if c > 0:
                        norm(c - 1)
                dve.wait_ge(s_l, NT)
                for j in range(2):
                    n = min(LT, NT - j * LT)
                    nc.vector.tensor_tensor(L[:, j * LT:j * LT + n, :], psL[j][:, 0:n * EXP].rearrange("p (t e) -> p t e", e=EXP),
                                            bg[:, :].unsqueeze(1).to_broadcast([P, n, EXP]), ALU.add)

            @block.gpsimd
            def _(pool):
                pool.memset(zeros[:, :], 0.0).then_inc(s_zero, 1)
                pool.memset(colsum[:, :], 0.0).then_inc(s_zero, 1)
                pool.wait_ge(s_zero, 2)
                for i in range(NT):
                    rows = REAL if i == NT - 1 else P
                    pool.wait_ge(s_o, i + 1)
                    wait(pool, s_acc, i)
                    nc.gpsimd.tensor_tensor(colsum[0:rows, :], colsum[0:rows, :], O[0:rows, i, :], ALU.add).then_inc(s_acc, 1)
                pool.wait_ge(s_mean, 1)

                def clear(c):
                    pool.dma_start(xs_c[c], zeros[:, :].unsqueeze(1).to_broadcast([P, xs_c.shape[2], D])).then_inc(s_slots, 16)

                clear(NC)
                for c in range(NC):
                    pool.wait_ge(s_gelu, c + 1)
                    pool.wait_ge(s_x[c % 2], 16 * (c // 2 + 1))
                    nc.gpsimd.tensor_tensor(O_c[:, c], XN_c[:, c], xc[:, c % 2, :, :], ALU.add).then_inc(s_x2, 1)
                    clear(c)
                pool.wait_ge(s_slots, 16 * (NC + 1))

            @block.tensor
            def _(pe):
                pe.wait_ge(s_w, 96)

                def transposes(i):
                    pe.wait_ge(s_agg, i + 1)
                    wait(pe, s_aTc, i - 1)
                    for f in range(ND):
                        mm = nc.tensor.transpose(psT[i % 2][:, f * P:(f + 1) * P], agg[:, i // CH % 2, i % CH, f * P:(f + 1) * P], ident[:, :])
                    mm.then_inc(s_aT, 1)

                def product(i):
                    pe.wait_ge(s_aTc, i + 1)
                    wait(pe, s_o, i - 1)
                    for f in range(ND):
                        mm = nc.tensor.matmul(psY[i % 2][:, 0:D], aggT[:, i % 2, f * P:(f + 1) * P], wo[:, f, :], start=f == 0, stop=f == ND - 1)
                    mm.then_inc(s_y, 1)

                transposes(0)
                for i in range(NT):
                    if i + 1 < NT:
                        transposes(i + 1)
                    product(i)
                pe.wait_ge(s_acc, NT)
                nc.tensor.matmul(psM[:, 0:D], ones[:, :], colsum[:, :], start=True, stop=True).then_inc(s_mean, 1)
                for c in range(NC):
                    pe.wait_ge(s_sq, c + 1)
                    for t in range(CH):
                        rows = REAL if c * CH + t == NT - 1 else P
                        mm = nc.tensor.matmul(psV[:, 0:D], ones[0:rows, :], sq[0:rows, c % 2, t, :],
                                              start=c + t == 0, stop=rows == REAL)
                    mm.then_inc(s_sum, 1)
                pe.wait_ge(s_sum, NC)
                pe.nop().then_inc(s_var, 1)

                def gate_transposes(i):
                    pe.wait_ge(s_xn, i + 1)
                    wait(pe, s_gTc, i - 1)
                    for f in range(ND):
                        mm = nc.tensor.transpose(psT[i % 2][:, f * P:(f + 1) * P], XN[:, i, f * P:(f + 1) * P], ident[:, :])
                    mm.then_inc(s_gT, 1)

                def logits(i):
                    pe.wait_ge(s_gTc, i + 1)
                    for f in range(ND):
                        mm = nc.tensor.matmul(psL[i // LT][:, i % LT * EXP:(i % LT + 1) * EXP], aggT[:, i % 2, f * P:(f + 1) * P], wg[:, f, :],
                                              start=f == 0, stop=f == ND - 1)
                    mm.then_inc(s_l, 1)

                gate_transposes(0)
                for i in range(NT):
                    if i + 1 < NT:
                        gate_transposes(i + 1)
                    logits(i)

            @block.scalar
            def _(act):
                for i in range(NT):
                    act.wait_ge(s_aT, i + 1)
                    wait(act, s_y, i - 1)
                    nc.scalar.copy(aggT[:, i % 2, :], psT[i % 2][:, 0:D]).then_inc(s_aTc, 1)
                for c in range(NC):
                    act.wait_ge(s_cent, c + 1)
                    if c >= 2:
                        act.wait_ge(s_sum, c - 1)
                    nc.scalar.activation(sq[:, c % 2, :, :], O_c[:, c], ACT.Square).then_inc(s_sq, 1)
                act.wait_ge(s_veps, 1)
                nc.scalar.activation(var[:, :], var[:, :], ACT.Sqrt).then_inc(s_std, 1)
                act.wait_ge(s_y, NT)
                for c in range(NC + 2):
                    if c < NC:
                        act.wait_ge(s_pre, c + 1)
                        nc.scalar.activation(XN_c[:, c], sq[:, c % 2, :, :], ACT.Gelu).then_inc(s_gelu, 1)
                    if 1 <= c <= NC:
                        cols = slice(CH * (c - 1), CH * c)
                        act.wait_ge(s_eps2, c)
                        nc.scalar.activation(eps[:, cols], eps[:, cols], ACT.Sqrt).then_inc(s_std2, 1)
                    if c >= 2:
                        for i in range(CH * (c - 2), CH * (c - 1)):
                            act.wait_ge(s_gT, i + 1)
                            wait(act, s_l, i - 1)
                            nc.scalar.copy(aggT[:, i % 2, :], psT[i % 2][:, 0:D]).then_inc(s_gTc, 1)


def route_stage(nc, sem, L, prob2, slots, experts):
    J = 2 * NT
    MT = -(-NP // TS)
    with ExitStack() as ctx:
        def sb(name, shape, dt):
            return ctx.enter_context(nc.sbuf_tensor(name, shape, dt))

        def ps(name):
            return ctx.enter_context(nc.psum_tensor(name, [P, 512], fp32))

        top = sb("top", [P, 2, NT], fp32)
        pick = sb("pick", [P, NT], fp32)
        eq = sb("equal", [P, NT, EXP], fp32)
        numi = sb("numbers_i", [P, P], i32)
        num = sb("numbers", [P, P], fp32)
        below = sb("expert_below", [P, EXP], fp32)
        pairs = sb("pairs", [P, EXP, J], fp32)
        pairs16 = sb("pairs16", [P, EXP, J], bf16)
        tri = sb("strict_tri", [P, P], bf16)
        all1 = sb("all_ones", [P, P], bf16)
        keepst = sb("keep_state", [P, EXP, J], fp32)
        total = sb("total", [P, EXP, J], fp32)
        upto = sb("upto", [P, EXP, J], fp32)
        place = sb("place", [P, EXP, J], fp32)
        ntile = sb("expert_tiles", [P, EXP], fp32)
        endt = sb("expert_end", [P, EXP], fp32)
        one16 = sb("one16", [P, EXP], fp32)
        mult = sb("multiples", [P, MT], fp32)
        over = sb("count_over", [P, EXP, MT], fp32)
        ended = sb("expert_ended", [P, TX, EXP], fp32)
        slotf = sb("slot_f", [P, J], fp32)
        eidf = sb("expert_f", [P, TX], fp32)
        psW = [ps(f"psW{j}") for j in range(4)]
        QB = EXP // 4

        s_c = sem("route_constants")
        s_cc = sem("route_const_chain")
        s_v = sem("route_chain")
        s_d = sem("top_difference")
        s_e = sem("second_exp")
        s_p = sem("pairs_ready")
        s_in = sem("within_summed")
        s_inc = sem("within_copied")
        s_tot = sem("totals_summed")

        with nc.Block() as block:

            @block.gpsimd
            def _(pool):
                pool.iota(numi[:, :], [[1, P]], base=0, channel_multiplier=0).then_inc(s_cc, 1)
                pool.memset(tri[:, :], 1.0).then_inc(s_cc, 1)
                pool.memset(all1[:, :], 1.0).then_inc(s_cc, 1)
                pool.memset(keepst[:, :, :], 1.0).then_inc(s_cc, 1)
                pool.memset(one16[:, :], 1.0).then_inc(s_cc, 1)
                pool.wait_ge(s_cc, 5)
                pool.affine_select(out=tri[:, :], in_=tri[:, :], compare_op=ALU.is_gt, fill=0.0,
                                   base=0, pattern=[[1, P]], channel_multiplier=-1).then_inc(s_c, 1)
                pool.memset(keepst[:, :, 0:1], 0.0).then_inc(s_c, 1)

            @block.tensor
            def _(pe):
                pe.wait_ge(s_c, 2)
                pe.wait_ge(s_p, 1)
                for j in range(4):
                    mm = nc.tensor.matmul(psW[j][:, 0:QB * J], tri[:, :], pairs16[:, QB * j:QB * (j + 1), :].rearrange("p e j -> p (e j)"), start=True, stop=True)
                mm.then_inc(s_in, 1)
                pe.wait_ge(s_inc, 1)
                for j in range(4):
                    mm = nc.tensor.matmul(psW[j][:, 0:QB * J], all1[:, :], pairs16[:, QB * j:QB * (j + 1), :].rearrange("p e j -> p (e j)"), start=True, stop=True)
                mm.then_inc(s_tot, 1)

            @block.scalar
            def _(act):
                act.wait_ge(s_d, 1)
                nc.scalar.activation(prob2[:, 1, :], top[:, 1, :], ACT.Exp).then_inc(s_e, 1)

            @block.vector
            def _(dve):
                chain = [0]

                def link(ins):
                    chain[0] += 1
                    ins.then_inc(s_v, 1)
                    dve.wait_ge(s_v, chain[0])

                V = nc.vector
                dve.wait_ge(s_c, 2)
                link(V.tensor_copy(num[:, :], numi[:, :]))
                link(V.tensor_scalar(below[:, :], num[:, 0:EXP], float(-EXP), None, ALU.add))
                by_expert = [P, NT, EXP]
                for k in range(2):
                    oh = pairs[:, :, k * NT:(k + 1) * NT].rearrange("p e t -> p t e")
                    link(V.tensor_reduce(top[:, k, :], L[:, :, :], AX.X, ALU.max))
                    link(V.tensor_tensor(eq[:, :, :], L[:, :, :], top[:, k, :].unsqueeze(2).to_broadcast(by_expert), ALU.is_equal))
                    link(V.tensor_tensor(eq[:, :, :], eq[:, :, :], below[:, :].unsqueeze(1).to_broadcast(by_expert), ALU.mult))
                    link(V.tensor_reduce(pick[:, :], eq[:, :, :], AX.X, ALU.min))
                    link(V.tensor_tensor(oh, below[:, :].unsqueeze(1).to_broadcast(by_expert), pick[:, :].unsqueeze(2).to_broadcast(by_expert), ALU.is_equal))
                    if k == 0:
                        link(V.tensor_scalar(eq[:, :, :], oh, LOW, None, ALU.mult))
                        link(V.tensor_tensor(L[:, :, :], L[:, :, :], eq[:, :, :], ALU.add))
                V.tensor_copy(pairs16[:, :, :], pairs[:, :, :]).then_inc(s_p, 1)
                V.tensor_tensor(top[:, 1, :], top[:, 1, :], top[:, 0, :], ALU.subtract).then_inc(s_d, 1)
                dve.wait_ge(s_e, 1)
                link(V.tensor_scalar(pick[:, :], prob2[:, 1, :], 1.0, None, ALU.add))
                link(V.reciprocal(prob2[:, 0, :], pick[:, :]))
                link(V.tensor_tensor(prob2[:, 1, :], prob2[:, 1, :], prob2[:, 0, :], ALU.mult))
                dve.wait_ge(s_in, 1)
                for j in range(4):
                    last = V.tensor_copy(place[:, QB * j:QB * (j + 1), :].rearrange("p e j -> p (e j)"), psW[j][:, 0:QB * J])
                last.then_inc(s_inc, 1)
                dve.wait_ge(s_tot, 1)
                for j in range(4):
                    last = V.tensor_copy(total[:, QB * j:QB * (j + 1), :].rearrange("p e j -> p (e j)"), psW[j][:, 0:QB * J])
                link(last)
                flat = lambda v: v[:, :, :].rearrange("p e j -> p (e j)")
                link(V.tensor_tensor_scan(flat(upto), flat(keepst), flat(total), 0.0, ALU.mult, ALU.add))
                link(V.tensor_tensor(place[:, :, :], place[:, :, :], upto[:, :, :], ALU.add))
                link(V.tensor_tensor(place[:, :, :], place[:, :, :], total[:, :, :], ALU.subtract))
                link(V.tensor_scalar(mult[:, :], num[:, 0:MT], float(TS), None, ALU.mult))
                link(V.tensor_tensor(over[:, :, :], upto[:, :, J - 1:J].to_broadcast([P, EXP, MT]),
                                     mult[:, :].unsqueeze(1).to_broadcast([P, EXP, MT]), ALU.is_gt))
                link(V.tensor_reduce(ntile[:, :], over[:, :, :], AX.X, ALU.add))
                link(V.tensor_tensor_scan(endt[:, :], one16[:, :], ntile[:, :], 0.0, ALU.mult, ALU.add))
                link(V.tensor_tensor(ntile[:, :], endt[:, :], ntile[:, :], ALU.subtract))
                link(V.tensor_scalar(ntile[:, :], ntile[:, :], float(TS), None, ALU.mult))
                link(V.tensor_tensor(place[:, :, :], place[:, :, :], ntile[:, :].unsqueeze(2).to_broadcast([P, EXP, J]), ALU.add))
                link(V.tensor_tensor(place[:, :, :], place[:, :, :], pairs[:, :, :], ALU.mult))
                link(V.tensor_reduce(slotf[:, :], place[:, :, :].rearrange("p e j -> p j e"), AX.X, ALU.add))
                link(V.tensor_copy(slots[:, :], slotf[:, :]))
                link(V.tensor_tensor(ended[:, :, :], num[:, 0:TX].unsqueeze(2).to_broadcast([P, TX, EXP]),
                                     endt[:, :].unsqueeze(1).to_broadcast([P, TX, EXP]), ALU.is_ge))
                link(V.tensor_reduce(eidf[:, :], ended[:, :, :], AX.X, ALU.add))
                link(V.tensor_scalar(experts[:, :], eidf[:, :], float(EXP - 1), None, ALU.min))


def experts_stage(nc, sem, a, xs, ys, ident, XN, slots, experts):
    SH = TS // P
    with ExitStack() as ctx:
        def sb(name, shape, dt):
            return ctx.enter_context(nc.sbuf_tensor(name, shape, dt))

        def ps(name):
            return ctx.enter_context(nc.psum_tensor(name, [P, 512], fp32))

        w1 = sb("w1", [P, WD, ND, F], fp32)
        w2 = sb("w2", [P, WD, NF, D], fp32)
        b1 = sb("b1", [P, WD, NF], fp32)
        b2 = sb("b2", [P, WD, D], fp32)
        xin = sb("slot_x", [P, WD, SH, D], fp32)
        xT = sb("slot_xT", [P, 2, ND * TS], fp32)
        hT = sb("hidden", [P, 2, NF, TS], fp32)
        y = sb("slot_y", [P, 2, SH, D], fp32)
        psT = [ps("epsT0"), ps("epsT1")]
        psH = [[ps(f"epsH{b}{g}") for g in range(2)] for b in range(2)]
        psY = [ps("epsY0"), ps("epsY1")]

        s_sc = sem("slots_written")
        s_lx = [sem(f"slot_x_loaded{j}") for j in range(WD)]
        s_l1 = [sem(f"w1_loaded{j}") for j in range(WD)]
        s_l2 = [sem(f"w2_loaded{j}") for j in range(WD)]
        s_lb = [sem(f"biases_loaded{j}") for j in range(WD)]
        s_xT = sem("slot_transposed")
        s_xTc = sem("slot_xT_copied")
        s_h = [sem("hidden_summed0"), sem("hidden_summed1")]
        s_ha = sem("hidden_done_act")
        s_hv = sem("hidden_done_vector")
        s_y = sem("slot_y_summed")
        s_yc = sem("slot_y_done")
        s_st = [sem("slot_y_stored0"), sem("slot_y_stored1")]

        xs_t = xs.rearrange("(t h p) f -> t p h f", p=P, h=SH)
        ys_t = ys.rearrange("(t h p) f -> t p h f", p=P, h=SH)
        w1_e = a["w1"].rearrange("e (c p) n -> e p c n", p=P)
        w2_e = a["w2"].rearrange("e (c p) n -> e p c n", p=P)

        def before(k, c):
            return (k, c - 1) if c > 0 else (k - 1, WD - 1)

        def after(k, c):
            return (k, c + 1) if c < WD - 1 else (k + 1, 0)

        def tiles(eng, period):
            for c in range(WD):
                period(0, c)
            with eng.Fori(1, TX // WD - 1) as k:
                for c in range(WD):
                    period(k, c)
            for c in range(WD):
                period(TX // WD - 1, c)

        with nc.Block() as block:

            @block.gpsimd
            def _(pool):
                for j in range(2 * NT):
                    pool.indirect_dma_start(
                        out=xs, out_offset=bass.IndirectOffsetOnAxis(ap=slots[:, j:j + 1], axis=0),
                        in_=XN[:, j % NT, :], in_offset=None, bounds_check=TX * TS - 1, oob_is_err=False).then_inc(s_sc, 16)

            @block.sync
            def _(sp):
                def load_weights(k, c):
                    i = WD * k + c
                    e = sp.value_load(experts[0:1, one(i)], min_val=0, max_val=EXP - 1)
                    wait(sp, s_h[1], i - WD + 1)
                    sp.dma_start(w1[:, c, :, :], w1_e[e]).then_inc(s_l1[c], 16)
                    wait(sp, s_ha, i - WD + 1)
                    wait(sp, s_hv, i - WD + 1)
                    sp.dma_start(b1[:, c, :], a["b1"][e]).then_inc(s_lb[c], 16)
                    wait(sp, s_y, i - WD + 1)
                    sp.dma_start(w2[:, c, :, :], w2_e[e]).then_inc(s_l2[c], 16)
                    wait(sp, s_yc, i - WD + 1)
                    sp.dma_start(b2[:, c, :], a["b2"][e].partition_broadcast(P)).then_inc(s_lb[c], 16)

                def load_x(k, c):
                    i = WD * k + c
                    wait(sp, s_xT, i - WD + 1)
                    sp.dma_start(xin[:, c, :, :], xs_t[i]).then_inc(s_lx[c], 16)

                for c in range(WD):
                    load_weights(0, c)
                sp.wait_ge(s_sc, 16 * 2 * NT)
                for c in range(WD):
                    load_x(0, c)
                with sp.Fori(1, TX // WD) as k:
                    for c in range(WD):
                        load_x(k, c)
                        load_weights(k, c)

            @block.tensor
            def _(pe):
                def transposes(k, c):
                    i, b = WD * k + c, c % 2
                    wait(pe, s_lx[c], 16 * (k + 1))
                    wait(pe, s_xTc, i - 1)
                    for d in range(ND):
                        for h in range(SH):
                            at = d * TS + h * P
                            mm = nc.tensor.transpose(psT[b][:, at:at + P], xin[:, c, h, d * P:(d + 1) * P], ident[:, :])
                    mm.then_inc(s_xT, 1)

                def hidden(k, c):
                    i, b = WD * k + c, c % 2
                    wait(pe, s_xTc, i + 1)
                    wait(pe, s_l1[c], 16 * (k + 1))
                    for g in range(2):
                        wait(pe, (s_ha, s_hv)[g], i - 1)
                        for f in (2 * g, 2 * g + 1):
                            for d in range(ND):
                                mm = nc.tensor.matmul(psH[b][g][:, (f % 2) * TS:(f % 2 + 1) * TS], w1[:, c, d, f * P:(f + 1) * P],
                                                      xT[:, b, d * TS:(d + 1) * TS], start=d == 0, stop=d == ND - 1)
                        mm.then_inc(s_h[g], 1)

                def second(k, c):
                    i, b = WD * k + c, c % 2
                    wait(pe, s_ha, i + 1)
                    wait(pe, s_hv, i + 1)
                    wait(pe, s_l2[c], 16 * (k + 1))
                    wait(pe, s_yc, i - 1)
                    for h in range(SH):
                        for f in range(NF):
                            mm = nc.tensor.matmul(psY[b][:, h * D:(h + 1) * D], hT[:, b, f, h * P:(h + 1) * P], w2[:, c, f, :],
                                                  start=f == 0, stop=f == NF - 1)
                    mm.then_inc(s_y, 1)

                def period(k, c):
                    first, last = isinstance(k, int) and k + c == 0, isinstance(k, int) and WD * k + c == TX - 1
                    if not last:
                        transposes(*after(k, c))
                    hidden(k, c)
                    if not first:
                        second(*before(k, c))
                    if last:
                        second(k, c)

                transposes(0, 0)
                tiles(pe, period)

            @block.scalar
            def _(act):
                def copy(k, c):
                    i, b = WD * k + c, c % 2
                    wait(act, s_xT, i + 1)
                    wait(act, s_h[1], i - 1)
                    nc.scalar.copy(xT[:, b, :], psT[b][:, :]).then_inc(s_xTc, 1)

                def relu(k, c):
                    i, b = WD * k + c, c % 2
                    wait(act, s_lb[c], 32 * (k + 1))
                    wait(act, s_h[0], i + 1)
                    wait(act, s_y, i - 1)
                    for f in range(2):
                        last = nc.scalar.activation(hT[:, b, f, :], psH[b][0][:, f * TS:(f + 1) * TS], ACT.Relu, bias=b1[:, c, f:f + 1])
                    last.then_inc(s_ha, 1)

                def store(k, c):
                    i, b = WD * k + c, c % 2
                    wait(act, s_yc, i + 1)
                    act.dma_start(ys_t[i], y[:, b, :, :]).then_inc(s_st[b], 16)

                def period(k, c):
                    first, last = isinstance(k, int) and k + c == 0, isinstance(k, int) and WD * k + c == TX - 1
                    if not last:
                        copy(*after(k, c))
                    relu(k, c)
                    if not first:
                        store(*before(k, c))
                    if last:
                        store(k, c)

                copy(0, 0)
                tiles(act, period)
                for b in range(2):
                    act.wait_ge(s_st[b], 16 * (TX // 2))

            @block.vector
            def _(dve):
                def relu(k, c):
                    i, b = WD * k + c, c % 2
                    wait(dve, s_lb[c], 32 * (k + 1))
                    wait(dve, s_h[1], i + 1)
                    wait(dve, s_y, i - 1)
                    for f in range(2, NF):
                        last = nc.vector.tensor_scalar(hT[:, b, f, :], psH[b][1][:, (f - 2) * TS:(f - 1) * TS], b1[:, c, f:f + 1], 0.0, ALU.add, ALU.max)
                    last.then_inc(s_hv, 1)

                def out_rows(k, c):
                    i, b = WD * k + c, c % 2
                    wait(dve, s_y, i + 1)
                    wait(dve, s_st[b], 16 * (WD // 2 * k + c // 2))
                    nc.vector.tensor_tensor(y[:, b, :, :], psY[b][:, :].rearrange("p (h f) -> p h f", h=SH),
                                            b2[:, c, :].unsqueeze(1).to_broadcast([P, SH, D]), ALU.add).then_inc(s_yc, 1)

                def period(k, c):
                    first, last = isinstance(k, int) and k + c == 0, isinstance(k, int) and WD * k + c == TX - 1
                    relu(k, c)
                    if not first:
                        out_rows(*before(k, c))
                    if last:
                        out_rows(k, c)

                tiles(dve, period)


def result_stage(nc, sem, a, ys, out, O, XN, prob2, slots, st, mv):
    YD = 12
    with ExitStack() as ctx:
        def sb(name, shape, dt):
            return ctx.enter_context(nc.sbuf_tensor(name, shape, dt))

        vec = sb("ffn_vectors", [P, 2, D], fp32)
        Y = sb("expert_rows", [P, 2 * YD, D], fp32)
        eps = sb("out_eps", [P, NT], fp32)
        rstd = sb("out_rstd", [P, NT], fp32)
        shift = sb("out_shift", [P, NT], fp32)

        s_w = sem("ffn_vectors_loaded")
        s_g = [sem(f"rows_gathered{j}") for j in range(YD)]
        s_first = sem("first_added")
        s_moe = sem("second_added")
        s_v = sem("result_chain")
        s_eps = sem("result_variance")
        s_std = sem("result_deviation")
        s_inv = sem("result_inverted")
        s_nrm = sem("result_normed")
        s_res = sem("result_ready")
        s_out = sem("result_stored")
        REAL = N - (NT - 1) * P

        def across(v):
            return v.unsqueeze(1).to_broadcast([P, CH, D])

        O_c = O[:, :, :].rearrange("p (c t) f -> p c t f", t=CH)
        XN_c = XN[:, :, :].rearrange("p (c t) f -> p c t f", t=CH)

        with nc.Block() as block:

            @block.gpsimd
            def _(pool):
                for t in range(NT):
                    if t >= YD:
                        pool.wait_ge(s_moe, t - YD + 1)
                    for k in range(2):
                        pool.indirect_dma_start(
                            out=Y[:, 2 * (t % YD) + k, :], out_offset=None, in_=ys,
                            in_offset=bass.IndirectOffsetOnAxis(ap=slots[:, k * NT + t:k * NT + t + 1], axis=0)).then_inc(s_g[t % YD], 16)

            @block.sync
            def _(sp):
                for j, n in enumerate(("ffn_gamma", "ffn_beta")):
                    sp.dma_start(vec[:, j, :], a[n].partition_broadcast(P)).then_inc(s_w, 16)
                for c in range(NC):
                    sp.wait_ge(s_res, c + 1)
                    rows = min(N, (c + 1) * CH * P) // P - c * CH
                    sp.dma_start(out[c * CH * P:(c * CH + rows) * P, :].rearrange("(t p) f -> p t f", p=P),
                                 XN_c[:, c, 0:rows, :]).then_inc(s_out, 16)
                sp.dma_start(out[(NT - 1) * P:N, :], XN[0:REAL, NT - 1, :]).then_inc(s_out, 16)
                sp.wait_ge(s_out, 16 * (NC + 1))

            @block.scalar
            def _(act):
                for c in range(NC):
                    act.wait_ge(s_eps, c + 1)
                    cols = slice(CH * c, CH * (c + 1))
                    nc.scalar.activation(eps[:, cols], eps[:, cols], ACT.Sqrt).then_inc(s_std, 1)
                    act.wait_ge(s_inv, c + 1)
                    for t in range(CH * c, CH * (c + 1)):
                        last = nc.scalar.activation(XN[:, t, :], XN[:, t, :], ACT.Identity, scale=rstd[:, t:t + 1], bias=shift[:, t:t + 1])
                    last.then_inc(s_nrm, 1)

            @block.vector
            def _(dve):
                chain = [0]

                def link(ins):
                    chain[0] += 1
                    ins.then_inc(s_v, 1)
                    dve.wait_ge(s_v, chain[0])

                V = nc.vector

                def moe(c, part):
                    for t in range(CH * c, CH * (c + 1))[part]:
                        dve.wait_ge(s_g[t % YD], 32 * (t // YD + 1))
                        V.scalar_tensor_tensor(out=XN[:, t, :], in0=Y[:, 2 * (t % YD), :], scalar=prob2[:, 0, t:t + 1],
                                               in1=XN[:, t, :], op0=ALU.mult, op1=ALU.add).then_inc(s_first, 1)
                        dve.wait_ge(s_first, t + 1)
                        V.scalar_tensor_tensor(out=XN[:, t, :], in0=Y[:, 2 * (t % YD) + 1, :], scalar=prob2[:, 1, t:t + 1],
                                               in1=XN[:, t, :], op0=ALU.mult, op1=ALU.add).then_inc(s_moe, 1)

                def stats(c):
                    dve.wait_ge(s_moe, CH * (c + 1))
                    for t in range(CH * c, CH * (c + 1)):
                        last = V.bn_stats(st[:, t, :], XN[:, t, :])
                    link(last)
                    for t in range(CH * c, CH * (c + 1)):
                        last = V.bn_aggr(mv[:, t, :], st[:, t, :])
                    link(last)
                    cols = slice(CH * c, CH * (c + 1))
                    V.tensor_scalar(eps[:, cols], mv[:, cols, 1], EPS, None, ALU.add).then_inc(s_eps, 1)

                def invert(c):
                    cols = slice(CH * c, CH * (c + 1))
                    dve.wait_ge(s_std, c + 1)
                    link(V.reciprocal(rstd[:, cols], eps[:, cols]))
                    link(V.tensor_tensor(shift[:, cols], mv[:, cols, 0], rstd[:, cols], ALU.mult))
                    V.tensor_scalar(shift[:, cols], shift[:, cols], -1.0, None, ALU.mult).then_inc(s_inv, 1)

                def norm(c):
                    dve.wait_ge(s_nrm, c + 1)
                    link(V.tensor_tensor(XN_c[:, c], XN_c[:, c], across(vec[:, 0, :]), ALU.mult))
                    link(V.tensor_tensor(XN_c[:, c], XN_c[:, c], across(vec[:, 1, :]), ALU.add))
                    V.tensor_tensor(XN_c[:, c], XN_c[:, c], O_c[:, c], ALU.add).then_inc(s_res, 1)

                dve.wait_ge(s_w, 32)
                HALF = CH // 2
                moe(0, slice(None))
                stats(0)
                invert(0)
                for c in range(NC):
                    if c + 1 < NC:
                        moe(c + 1, slice(0, HALF))
                    norm(c)
                    if c + 1 < NC:
                        moe(c + 1, slice(HALF, CH))
                        stats(c + 1)
                        invert(c + 1)


def layouts(inputs):
    x = np.asarray(inputs["x"])
    src = np.asarray(inputs["src"]).astype(np.int32)
    dst = np.asarray(inputs["dst"]).astype(np.int32)
    attr = np.asarray(inputs["edge_attr_256"])
    got = {}
    got["x"] = np.concatenate([x, np.zeros((NP - N, D), x.dtype)])
    attr = np.concatenate([attr, np.zeros((EPAD - E, D), attr.dtype)])
    got["attrT"] = np.ascontiguousarray(attr.reshape(NG, G, P, ND, P).transpose(0, 4, 1, 3, 2).reshape(NG, P, G * D))
    g = lambda n: np.asarray(inputs["L0_gnn_" + n])
    got["wkvT"] = np.ascontiguousarray(np.concatenate([g("WK"), g("WV")]).T)
    got["wqT"] = np.ascontiguousarray(g("WQ").T)
    got["weT"] = np.ascontiguousarray(g("WE").T)
    got["bo"] = g("bo")
    got["woT"] = np.ascontiguousarray(g("Wo").T)
    for n in ("gamma", "beta", "mean_scale"):
        got[n] = g(n)
    f = lambda n: np.asarray(inputs["L0_ffn_" + n])
    for n in ("gate_w", "gate_b", "w1", "w2", "b2"):
        got[n] = f(n)
    got["b1"] = np.ascontiguousarray(f("b1").reshape(EXP, NF, P).transpose(0, 2, 1))
    got["ffn_gamma"], got["ffn_beta"] = f("gamma"), f("beta")
    srcp = np.concatenate([src, np.zeros(EPAD - E, np.int32)])
    ids = [np.concatenate([dst, np.full(EPAD - E, N, np.int32)])]
    for size in (G * P, P):
        ends = ids[-1].reshape(-1, P)[:, [0, P - 1]].reshape(-1)
        ids.append(np.concatenate([ends, np.full(size - len(ends), N, np.int32)]))
    near, win = [], []
    for v in ids:
        ext = np.concatenate([[-1], v, [-1]]).astype(np.int32)
        near.append(np.stack([ext[1:-1].reshape(-1, P).T, ext[:-2].reshape(-1, P).T, ext[2:].reshape(-1, P).T], 1))
        rows = np.stack([ext[t * P:t * P + P + 2] for t in range(len(v) // P)])
        rows = np.repeat(rows, H, 0)
        win.append(np.concatenate([rows, np.zeros((-len(rows) % P, P + 2), np.int32)]))
    got["near"] = np.ascontiguousarray(np.concatenate(near, 2))
    got["win"] = np.ascontiguousarray(np.concatenate(win))
    got["idx"] = np.ascontiguousarray(srcp.reshape(NG, G, P).transpose(0, 2, 1))
    return got


def kernel(**inputs):
    import concourse.bacc as bacc
    from concourse.bass_utils import run_bass_kernel_spmd
    nc = bacc.Bacc("TRN2", target_bir_lowering=False, num_devices=1)
    arrays = {"in_" + n: v for n, v in layouts(inputs).items()}
    args = {n[3:]: nc.dram_tensor(n, list(v.shape), mybir.dt.from_np(v.dtype), kind="ExternalInput").ap() for n, v in arrays.items()}
    out = nc.dram_tensor("out", [N, D], fp32, kind="ExternalOutput").ap()
    build(nc, args, out)
    r = run_bass_kernel_spmd(nc, [arrays], core_ids=[0])
    return r.results[0]["out"]
```
